# Optimizing a Trainium2 kernel written in Bass

```python
import numpy as np
import jax
import jax.numpy as jnp

def _softmax(x, axis=-1):
    return jax.nn.softmax(x, axis=axis)

def _gelu(x):
    return jax.nn.gelu(x, approximate=True)

def _silu(x):
    return jax.nn.silu(x)

def _sigmoid(x):
    return jax.nn.sigmoid(x)

def _layernorm(x, axis=-1, eps=1e-05):
    m = jnp.mean(x, axis=axis, keepdims=True)
    v = jnp.var(x, axis=axis, keepdims=True)
    return (x - m) / jnp.sqrt(v + eps)

def _scatter_add(tgt, idx, src, axis=0):
    return tgt.at[idx].add(src)

def _segment_sum(src, seg, n):
    return jax.ops.segment_sum(src, seg, n)
kernel_name = 'mk_perceiver_d1_seqx_r8_d3f6a2'

def setup_inputs(seed: int=0):
    np.random.seed(seed)
    _w = jnp.asarray

    def _rec_inputs():
        import jax
        import jax.numpy as jnp
        _rk = jax.random.key(seed)
        x = -0.0003929 + 0.9999 * jax.random.normal(jax.random.fold_in(_rk, 1), (1, 128, 512), jnp.float32)
        _lenS = 128 - jax.random.randint(jax.random.fold_in(_rk, 7), (1,), 0, max(1, 128 // 4) + 1, jnp.int32)
        _lenS2 = 2048 - jax.random.randint(jax.random.fold_in(_rk, 8), (1,), 0, max(1, 2048 // 4) + 1, jnp.int32)
        _ctx_4096P = jax.random.normal(jax.random.fold_in(_rk, 11), (1, 16, 512), jnp.float32)
        _ctx_4096c = jax.random.dirichlet(jax.random.fold_in(_rk, 511), 0.3 * jnp.ones((16,), jnp.float32), (1, 2048))
        _ctx_4096t = jnp.einsum('bsk,bkd->bsd', _ctx_4096c, _ctx_4096P)
        _ctx_4096t = _ctx_4096t * jax.lax.rsqrt(jnp.mean(jnp.square(_ctx_4096t)) + 1e-12) * 0.953939
        ctx_4096 = 2.81802e-05 + 1.00001 * (_ctx_4096t + 0.3 * jax.random.normal(jax.random.fold_in(_rk, 611), (1, 2048, 512), jnp.float32))
        _validS = jnp.arange(128)[None, :] < _lenS[:, None]
        _validS2 = jnp.arange(2048)[None, :] < _lenS2[:, None]
        _causal = jnp.tril(jnp.ones((128, 128), dtype=bool))
        mask_BxSxS2_ff0 = jnp.where(jnp.ones((1, 128, 2048), dtype=bool), 0.0, -1000000000.0).astype(jnp.float32)
        return (x, ctx_4096, mask_BxSxS2_ff0)
    x, ctx_4096, mask_BxSxS2_ff0 = _rec_inputs()

    def _L0_xattn_setup():
        import jax, jax.numpy as jnp
        import numpy as np
        B, S, D = (4, 128, 512)
        HQ, HKV, DK, DV = (32, 8, 128, 128)

        def apply_rope(x, positions):
            d = x.shape[-1]
            inv_freq = 1.0 / 10000.0 ** (jnp.arange(0, d, 2, dtype=jnp.float32) / d)
            ang = positions.astype(jnp.float32)[:, None] * inv_freq[None, :]
            cos = jnp.cos(ang)[None, None]
            sin = jnp.sin(ang)[None, None]
            x1, x2 = (x[..., :d // 2], x[..., d // 2:])
            return jnp.concatenate([x1 * cos - x2 * sin, x2 * cos + x1 * sin], axis=-1)
        key = jax.random.key(seed)
        ks = jax.random.split(key, 8)
        return {'query': jax.random.normal(ks[0], (B, S, D), jnp.float32), 'key': jax.random.normal(ks[1], (B, S, D), jnp.float32), 'value': jax.random.normal(ks[2], (B, S, D), jnp.float32), 'mask': jnp.zeros((B, S, S), jnp.float32), 'wq': jax.random.normal(ks[3], (D, HQ * DK), jnp.float32) * 0.02, 'wk': jax.random.normal(ks[4], (D, HKV * DK), jnp.float32) * 0.02, 'wv': jax.random.normal(ks[5], (D, HKV * DV), jnp.float32) * 0.02, 'wo': jax.random.normal(ks[6], (HQ * DV, D), jnp.float32) * 0.02, 'curr_seq_pos': 0}
    _L0_xattn_all = _L0_xattn_setup()
    _L0_xattn_in = {k: v for k, v in _L0_xattn_all.items() if k in ('wq', 'wk', 'wv', 'wo')}
    del _L0_xattn_all

    def _L0_attn_setup():
        import jax, jax.numpy as jnp
        import numpy as np
        HID = 512
        H = 128
        P = 64
        N = 128
        G = 8
        K = 4
        CH = 128
        INTER = H * P
        CONV_DIM = INTER + 2 * G * N
        PROJ = INTER + CONV_DIM + H
        EPS = 1e-05

        def segsum(x):
            T = x.shape[-1]
            xe = jnp.repeat(x[..., None], T, axis=-1)
            strict = jnp.tril(jnp.ones((T, T), bool), -1)
            s = jnp.cumsum(jnp.where(strict, xe, 0.0), axis=-2)
            keep = jnp.tril(jnp.ones((T, T), bool), 0)
            return jnp.where(keep, s, -jnp.inf)

        def _mamba2(hidden_states, in_proj_w, conv_w, conv_b, dt_bias, A_log, D, norm_weight, out_proj_w):
            b, L, _ = hidden_states.shape
            nchunk = L // CH
            proj = hidden_states @ in_proj_w.T
            gate, hBC, dt = jnp.split(proj, [INTER, INTER + CONV_DIM], axis=-1)
            xp = jnp.pad(hBC.transpose(0, 2, 1), ((0, 0), (0, 0), (K - 1, 0)))
            xc = jax.lax.conv_general_dilated(xp, conv_w, (1,), 'VALID', feature_group_count=CONV_DIM, dimension_numbers=('NCW', 'OIW', 'NCW'))
            hBC = jax.nn.silu((xc + conv_b[None, :, None]).transpose(0, 2, 1))
            hs, Bx, Cx = jnp.split(hBC, [INTER, INTER + G * N], axis=-1)
            A = -jnp.exp(A_log)
            dt = jax.nn.softplus(dt + dt_bias)
            hs = hs.reshape(b, L, H, P)
            rep = H // G
            Bm = jnp.tile(Bx.reshape(b, L, G, N), (1, 1, rep, 1))
            Cm = jnp.tile(Cx.reshape(b, L, G, N), (1, 1, rep, 1))
            D_res = D[None, None, :, None] * hs
            X = (hs * dt[..., None]).reshape(b, nchunk, CH, H, P)
            A_dt = (A[None, None, :] * dt).reshape(b, nchunk, CH, H).transpose(0, 3, 1, 2)
            Bc = Bm.reshape(b, nchunk, CH, H, N)
            Cc = Cm.reshape(b, nchunk, CH, H, N)
            A_cs = jnp.cumsum(A_dt, axis=-1)
            Lmat = jnp.exp(segsum(A_dt))
            Gm = jnp.einsum('bclhn,bcshn->bclsh', Cc, Bc)
            M = Gm * Lmat.transpose(0, 2, 3, 4, 1)
            Y_diag = jnp.einsum('bclsh,bcshp->bclhp', M, X)
            decay_states = jnp.exp(A_cs[..., -1:] - A_cs)
            B_decay = Bc * decay_states.transpose(0, 2, 3, 1)[..., None]
            states = jnp.einsum('bclhn,bclhp->bchpn', B_decay, X)
            states = jnp.concatenate([jnp.zeros_like(states[:, :1]), states], axis=1)
            A_last = jnp.pad(A_cs[..., -1], ((0, 0), (0, 0), (1, 0)))
            decay_chunk = jnp.exp(segsum(A_last)).transpose(0, 3, 2, 1)
            new_states = jnp.einsum('bzjh,bzhpn->bjhpn', decay_chunk, states)
            prev_states = new_states[:, :-1]
            sdo = jnp.exp(A_cs).transpose(0, 2, 3, 1)
            Y_off = jnp.einsum('bclhn,bchpn->bclhp', Cc, prev_states) * sdo[..., None]
            y = (Y_diag + Y_off).reshape(b, L, H, P) + D_res
            scan_out = y.reshape(b, L, INTER)
            xg = scan_out * jax.nn.silu(gate)
            xr = xg.reshape(b, L, G, INTER // G)
            xr = xr * jax.lax.rsqrt(jnp.mean(xr * xr, axis=-1, keepdims=True) + EPS)
            normed = xr.reshape(b, L, INTER) * norm_weight
            return normed @ out_proj_w.T
        key = jax.random.key(seed)
        ks = jax.random.split(key, 6)
        b, L = (2, 256)
        hidden_states = jax.random.normal(ks[0], (b, L, HID), jnp.float32)
        in_proj_w = jax.random.normal(ks[1], (PROJ, HID), jnp.float32) * HID ** (-0.5)
        conv_w = jax.random.normal(ks[2], (CONV_DIM, 1, K), jnp.float32) * 0.2
        conv_b = jax.random.normal(ks[3], (CONV_DIM,), jnp.float32) * 0.02
        dt_bias = jnp.ones((H,), jnp.float32)
        A_log = jnp.log(jnp.arange(1, H + 1, dtype=jnp.float32))
        D = jnp.ones((H,), jnp.float32)
        norm_weight = jnp.ones((INTER,), jnp.float32)
        out_proj_w = jax.random.normal(ks[4], (HID, INTER), jnp.float32) * INTER ** (-0.5)
        return dict(hidden_states=hidden_states, in_proj_w=in_proj_w, conv_w=conv_w, conv_b=conv_b, dt_bias=dt_bias, A_log=A_log, D=D, norm_weight=norm_weight, out_proj_w=out_proj_w)
    _L0_attn_all = _L0_attn_setup()
    _L0_attn_in = {k: v for k, v in _L0_attn_all.items() if k in ('in_proj_w', 'conv_w', 'conv_b', 'dt_bias', 'A_log', 'D', 'norm_weight', 'out_proj_w')}
    del _L0_attn_all

    def _L0_ffn_setup():
        import jax, jax.numpy as jnp
        import numpy as np
        key = jax.random.key(seed)
        k1, k2, k3, k4, k5 = jax.random.split(key, 5)
        O, I, G = (512, 512, 32)
        x = jax.random.normal(k1, (8, 256, I), dtype=jnp.float32)
        weight_quantized = jax.random.randint(k2, ((O * I + 1) // 2,), 0, 32, dtype=jnp.int32)
        weight_scales = jax.random.uniform(k3, (O, G), dtype=jnp.float32) * 0.01
        weight_zero_points = jax.random.randint(k4, (O, G), 0, 16, dtype=jnp.int32)
        bias = jax.random.normal(k5, (O,), dtype=jnp.float32)
        return {'x': x, 'weight_quantized': weight_quantized, 'weight_scales': weight_scales, 'weight_zero_points': weight_zero_points, 'bias': bias}
    _L0_ffn_all = _L0_ffn_setup()
    _L0_ffn_in = {k: v for k, v in _L0_ffn_all.items() if k in ('weight_quantized', 'weight_scales', 'weight_zero_points', 'bias')}
    del _L0_ffn_all
    return {'x': x, 'ctx_4096': ctx_4096, 'mask_BxSxS2_ff0': mask_BxSxS2_ff0, 'L0_xattn_wq': _L0_xattn_in['wq'], 'L0_xattn_wk': _L0_xattn_in['wk'], 'L0_xattn_wv': _L0_xattn_in['wv'], 'L0_xattn_wo': _L0_xattn_in['wo'], 'L0_attn_in_proj_w': _L0_attn_in['in_proj_w'], 'L0_attn_conv_w': _L0_attn_in['conv_w'], 'L0_attn_conv_b': _L0_attn_in['conv_b'], 'L0_attn_dt_bias': _L0_attn_in['dt_bias'], 'L0_attn_A_log': _L0_attn_in['A_log'], 'L0_attn_D': _L0_attn_in['D'], 'L0_attn_norm_weight': _L0_attn_in['norm_weight'], 'L0_attn_out_proj_w': _L0_attn_in['out_proj_w'], 'L0_ffn_weight_quantized': _L0_ffn_in['weight_quantized'], 'L0_ffn_weight_scales': _L0_ffn_in['weight_scales'], 'L0_ffn_weight_zero_points': _L0_ffn_in['weight_zero_points'], 'L0_ffn_bias': _L0_ffn_in['bias']}

def reference(x, ctx_4096, mask_BxSxS2_ff0, L0_xattn_wq, L0_xattn_wk, L0_xattn_wv, L0_xattn_wo, L0_attn_in_proj_w, L0_attn_conv_w, L0_attn_conv_b, L0_attn_dt_bias, L0_attn_A_log, L0_attn_D, L0_attn_norm_weight, L0_attn_out_proj_w, L0_ffn_weight_quantized, L0_ffn_weight_scales, L0_ffn_weight_zero_points, L0_ffn_bias):
    import jax
    import jax.numpy as jnp

    def _L0_xattn_ref(query, key, value, mask, wq, wk, wv, wo, curr_seq_pos):
        import jax, jax.numpy as jnp
        import numpy as np
        B, S, D = (4, 128, 512)
        HQ, HKV, DK, DV = (32, 8, 128, 128)

        def apply_rope(x, positions):
            d = x.shape[-1]
            inv_freq = 1.0 / 10000.0 ** (jnp.arange(0, d, 2, dtype=jnp.float32) / d)
            ang = positions.astype(jnp.float32)[:, None] * inv_freq[None, :]
            cos = jnp.cos(ang)[None, None]
            sin = jnp.sin(ang)[None, None]
            x1, x2 = (x[..., :d // 2], x[..., d // 2:])
            return jnp.concatenate([x1 * cos - x2 * sin, x2 * cos + x1 * sin], axis=-1)
        bs, sq, _ = query.shape
        sk = key.shape[1]
        n_groups = HQ // HKV
        q = (query @ wq).reshape(bs, sq, HQ, DK).transpose(0, 2, 1, 3)
        k = (key @ wk).reshape(bs, sk, HKV, DK)
        v = (value @ wv).reshape(bs, sk, HKV, DV)
        k = jnp.repeat(k, n_groups, axis=2).transpose(0, 2, 1, 3)
        v = jnp.repeat(v, n_groups, axis=2).transpose(0, 2, 1, 3)
        scale = jnp.sqrt(jnp.float32(DK))
        pos = curr_seq_pos + jnp.arange(sq)
        q = apply_rope(q, pos)
        k = apply_rope(k, curr_seq_pos + jnp.arange(sk))
        scores = jnp.einsum('bhqd,bhkd->bhqk', q, k) / scale
        m = jax.lax.dynamic_slice(mask, (0, curr_seq_pos, 0), (bs, sq, sk))
        attn = jax.nn.softmax(scores + m[:, None, :, :], axis=-1)
        out = jnp.einsum('bhqk,bhkd->bhqd', attn, v)
        out = out.transpose(0, 2, 1, 3).reshape(bs, sq, HQ * DV)
        return out @ wo

    def _L0_attn_ref(hidden_states, in_proj_w, conv_w, conv_b, dt_bias, A_log, D, norm_weight, out_proj_w):
        import jax, jax.numpy as jnp
        import numpy as np
        HID = 512
        H = 128
        P = 64
        N = 128
        G = 8
        K = 4
        CH = 128
        INTER = H * P
        CONV_DIM = INTER + 2 * G * N
        PROJ = INTER + CONV_DIM + H
        EPS = 1e-05

        def segsum(x):
            T = x.shape[-1]
            xe = jnp.repeat(x[..., None], T, axis=-1)
            strict = jnp.tril(jnp.ones((T, T), bool), -1)
            s = jnp.cumsum(jnp.where(strict, xe, 0.0), axis=-2)
            keep = jnp.tril(jnp.ones((T, T), bool), 0)
            return jnp.where(keep, s, -jnp.inf)

        def _mamba2(hidden_states, in_proj_w, conv_w, conv_b, dt_bias, A_log, D, norm_weight, out_proj_w):
            b, L, _ = hidden_states.shape
            nchunk = L // CH
            proj = hidden_states @ in_proj_w.T
            gate, hBC, dt = jnp.split(proj, [INTER, INTER + CONV_DIM], axis=-1)
            xp = jnp.pad(hBC.transpose(0, 2, 1), ((0, 0), (0, 0), (K - 1, 0)))
            xc = jax.lax.conv_general_dilated(xp, conv_w, (1,), 'VALID', feature_group_count=CONV_DIM, dimension_numbers=('NCW', 'OIW', 'NCW'))
            hBC = jax.nn.silu((xc + conv_b[None, :, None]).transpose(0, 2, 1))
            hs, Bx, Cx = jnp.split(hBC, [INTER, INTER + G * N], axis=-1)
            A = -jnp.exp(A_log)
            dt = jax.nn.softplus(dt + dt_bias)
            hs = hs.reshape(b, L, H, P)
            rep = H // G
            Bm = jnp.tile(Bx.reshape(b, L, G, N), (1, 1, rep, 1))
            Cm = jnp.tile(Cx.reshape(b, L, G, N), (1, 1, rep, 1))
            D_res = D[None, None, :, None] * hs
            X = (hs * dt[..., None]).reshape(b, nchunk, CH, H, P)
            A_dt = (A[None, None, :] * dt).reshape(b, nchunk, CH, H).transpose(0, 3, 1, 2)
            Bc = Bm.reshape(b, nchunk, CH, H, N)
            Cc = Cm.reshape(b, nchunk, CH, H, N)
            A_cs = jnp.cumsum(A_dt, axis=-1)
            Lmat = jnp.exp(segsum(A_dt))
            Gm = jnp.einsum('bclhn,bcshn->bclsh', Cc, Bc)
            M = Gm * Lmat.transpose(0, 2, 3, 4, 1)
            Y_diag = jnp.einsum('bclsh,bcshp->bclhp', M, X)
            decay_states = jnp.exp(A_cs[..., -1:] - A_cs)
            B_decay = Bc * decay_states.transpose(0, 2, 3, 1)[..., None]
            states = jnp.einsum('bclhn,bclhp->bchpn', B_decay, X)
            states = jnp.concatenate([jnp.zeros_like(states[:, :1]), states], axis=1)
            A_last = jnp.pad(A_cs[..., -1], ((0, 0), (0, 0), (1, 0)))
            decay_chunk = jnp.exp(segsum(A_last)).transpose(0, 3, 2, 1)
            new_states = jnp.einsum('bzjh,bzhpn->bjhpn', decay_chunk, states)
            prev_states = new_states[:, :-1]
            sdo = jnp.exp(A_cs).transpose(0, 2, 3, 1)
            Y_off = jnp.einsum('bclhn,bchpn->bclhp', Cc, prev_states) * sdo[..., None]
            y = (Y_diag + Y_off).reshape(b, L, H, P) + D_res
            scan_out = y.reshape(b, L, INTER)
            xg = scan_out * jax.nn.silu(gate)
            xr = xg.reshape(b, L, G, INTER // G)
            xr = xr * jax.lax.rsqrt(jnp.mean(xr * xr, axis=-1, keepdims=True) + EPS)
            normed = xr.reshape(b, L, INTER) * norm_weight
            return normed @ out_proj_w.T
        return _mamba2(hidden_states, in_proj_w, conv_w, conv_b, dt_bias, A_log, D, norm_weight, out_proj_w)

    def _L0_ffn_ref(x, weight_quantized, weight_scales, weight_zero_points, bias):
        import jax, jax.numpy as jnp
        import numpy as np
        O, G = weight_scales.shape
        I = x.shape[-1]
        gs = I // G
        low = weight_quantized % 16
        high = weight_quantized // 16
        q = jnp.stack([low, high], axis=1).reshape(-1)[:O * I].astype(jnp.float32)
        q = q.reshape(O, G, gs)
        w = weight_scales[:, :, None] * (q - weight_zero_points[:, :, None].astype(jnp.float32))
        w = w.reshape(O, I)
        return jnp.einsum('bsi,oi->bso', x, w) + bias
    x = x + _L0_xattn_ref(_layernorm(x, axis=-1), ctx_4096, ctx_4096, mask_BxSxS2_ff0, L0_xattn_wq, L0_xattn_wk, L0_xattn_wv, L0_xattn_wo, 0)
    x = x + _L0_attn_ref(_layernorm(x, axis=-1), L0_attn_in_proj_w, L0_attn_conv_w, L0_attn_conv_b, L0_attn_dt_bias, L0_attn_A_log, L0_attn_D, L0_attn_norm_weight, L0_attn_out_proj_w)
    x = x + _L0_ffn_ref(_layernorm(x, axis=-1), L0_ffn_weight_quantized, L0_ffn_weight_scales, L0_ffn_weight_zero_points, L0_ffn_bias)
    return x

_drawn_inputs = setup_inputs


def setup_inputs(seed=0):
    import zlib

    import numpy as np

    out = dict(_drawn_inputs(seed))
    spreads = {'L0_attn_dt_bias': (1.0, 0.578),
     'L0_attn_D': (1.0, 0.2),
     'L0_attn_norm_weight': (1.0, 0.2)}
    factors = {'L0_xattn_wq': 4.447, 'L0_xattn_wk': 4.523, 'L0_attn_A_log': 2.909}
    for name, (base, spread) in spreads.items():
        noise = np.random.default_rng([zlib.crc32(name.encode()), seed]).standard_normal(out[name].shape)
        drawn = base * np.exp(spread * noise) if base else spread * noise
        out[name] = jnp.asarray(drawn.astype(out[name].dtype))
    for name, factor in factors.items():
        out[name] = (out[name] * factor).astype(out[name].dtype)
    return out
```

```python
from contextlib import ExitStack

import numpy as np

import concourse.bass as bass
from concourse import mybir

F32 = mybir.dt.float32
F32R = mybir.dt.float32r
I32 = mybir.dt.int32
ALU = mybir.AluOpType
ACT = mybir.ActivationFunctionType
X_AXIS = mybir.AxisListType.X

P = 128
DM = 512
KC = DM // P
SK = 2048
KB = SK // 512
KT = SK // P
G = 8
HG = 4
DH = 128
INTER = 8192
CH = INTER // 512
HC = 8
PH = 64
NS = 128
MH = 128
TAPS = 4
BCC = 4
XT_TILES = INTER // P + 4 * BCC
NG = 8
QG = 32
EPS = 1e-5
LOWEST = -3.4028234663852886e38


def at_least(eng, sem, count):
    if not isinstance(count, int) or count > 0:
        eng.wait_ge(sem, count)


def keep_wait_apart(eng):
    eng.nop(nofuse=True)


def build(nc, x, mask, ctx_t, rope_k_cos, rope_k_sin, rope_q_cos, rope_q_sin, wk, wv, wq, wo, w_dt, w_bc,
          w_hs, w_gate, w_out, conv_w, conv_b, dt_bias, a_log, d_skip, norm_w, q_packed, q_scale, q_zero,
          q_bias, out):
    with ExitStack() as whole:
        def sb(name, shape, dt=F32, scope=whole):
            return scope.enter_context(nc.sbuf_tensor(name, shape, dt))

        xres = sb("xres", [P, DM])
        xn = sb("xn", [P, DM])
        xnT = sb("xnT", [P, KC, P])
        ident = sb("ident", [P, P])
        ones = sb("ones", [P, P])
        upper = sb("upper", [P, P])
        below = sb("below", [P, P])
        stats = sb("stats", [P, 6])
        mean_var = sb("mean_var", [P, 2])
        var_eps = sb("var_eps", [P, 1])
        rstd = sb("rstd", [P, 1])
        half_neg = sb("half_neg", [P, 1])
        bias_bc = sb("bias_bc", [P, DM])

        attn = ExitStack()
        ctx_hi = sb("ctx_hi", [P, KC, SK], F32R, attn)
        ctx_lo = sb("ctx_lo", [P, KC, SK], F32R, attn)
        k_hi = sb("k_hi", [P, SK], F32R, attn)
        k_lo = sb("k_lo", [P, SK], F32R, attn)
        v_hi = sb("v_hi", [P, KT, DH], F32R, attn)
        v_lo = sb("v_lo", [P, KT, DH], F32R, attn)
        cos_k = sb("cos_k", [P, SK], F32, attn)
        sin_k = sb("sin_k", [P, SK], F32, attn)
        mask_sb = sb("mask_sb", [P, SK], F32, attn)
        pt_hi = sb("pt_hi", [P, 2, 512], F32R, attn)
        pt_lo = sb("pt_lo", [P, 2, 512], F32R, attn)
        rope_a = sb("rope_a", [P, 2, 512], F32, attn)
        rope_b = sb("rope_b", [P, 2, 512], F32, attn)
        wq_sb = sb("wq_sb", [P, KC, 512], F32, attn)
        wo_sb = sb("wo_sb", [P, HG, 512], F32, attn)
        wk_hi = sb("wk_hi", [P, KC, DH], F32R, attn)
        wv_hi = sb("wv_hi", [P, KC, DH], F32R, attn)
        arriving = ExitStack()
        wk_raw = sb("wk_raw", [P, KC, DH], F32, arriving)
        wv_raw = sb("wv_raw", [P, KC, DH], F32, arriving)
        arriving.close()
        wk_lo = sb("wk_lo", [P, KC, DH], F32R, attn)
        wv_lo = sb("wv_lo", [P, KC, DH], F32R, attn)
        qT_hi = sb("qT_hi", [P, HG, P], F32R, attn)
        qT_lo = sb("qT_lo", [P, HG, P], F32R, attn)
        cos_q = sb("cos_q", [P, DH // 2], F32, attn)
        sin_q = sb("sin_q", [P, DH // 2], F32, attn)
        block_max = sb("block_max", [P, HG, KB], F32, attn)
        neg_max = sb("neg_max", [P, HG], F32, attn)
        row_sum = sb("row_sum", [P, HG], F32, attn)
        inv_sum = sb("inv_sum", [P, HG], F32, attn)
        stage = ExitStack()
        ctx_raw = sb("ctx_raw", [P, 2, KC, 512], F32, stage)
        stage.close()
        probs = sb("probs", [P, HG, SK], F32, attn)
        attn.close()

        mam = ExitStack()
        w_gate_sb = sb("w_gate_sb", [P, 2, KC, 512], F32, mam)
        w_out_sb = sb("w_out_sb", [P, 2, KC, 512], F32, mam)
        w_hs_sb = sb("w_hs_sb", [P, 2, KC, 512], F32, mam)
        w_dt_sb = sb("w_dt_sb", [P, KC, MH], F32, mam)
        cw = sb("cw", [P, XT_TILES, TAPS], F32, mam)
        cb = sb("cb", [P, XT_TILES], F32, mam)
        nw = sb("nw", [P, INTER // P], F32, mam)
        d_bc = sb("d_bc", [P, MH], F32, mam)
        dtb_bc = sb("dtb_bc", [P, MH], F32, mam)
        alog_bc = sb("alog_bc", [P, MH], F32, mam)
        scale_sb = sb("scale_sb", [P, KC, QG], F32, mam)
        zero_sb = sb("zero_sb", [P, KC, QG], I32, mam)
        packed = sb("packed", [P, KC, DM // 2], I32, mam)
        decay = sb("decay", [P, MH, P], F32, mam)
        bc_acc = sb("bc_acc", [P, 4 * BCC, P], F32, mam)
        bc_act = sb("bc_act", [P, 4 * BCC, P], F32, mam)
        gm = sb("gm", [P, G, P], F32, mam)
        dt_x = sb("dt_x", [P, MH], F32, mam)
        dt_t = sb("dt_t", [P, 4, MH], F32, mam)
        dt = sb("dt", [P, MH], F32, mam)
        a_dt = sb("a_dt", [P, MH], F32, mam)
        pre = ExitStack()
        digits = sb("digits", [P, KC, DM // 2, 2], I32, pre)
        weights = sb("weights", [P, KC, DM], F32, pre)
        pre.close()
        x_dt = sb("x_dt", [P, 2, HC, PH], F32, mam)
        x_skip = sb("x_skip", [P, 2, 512], F32, mam)
        gate = sb("gate", [P, 2, 512], F32, mam)
        y = sb("y", [P, 2, 512], F32, mam)
        conv = sb("conv", [P, 2, 4, P], F32, mam)
        hsT = sb("hsT", [P, 2, 4, P], F32, mam)
        pre = ExitStack()
        steps = sb("steps", [P, 2, HC, P], F32, pre)
        pre.close()
        m_t = sb("m_t", [P, 2, HC, P], F32, mam)
        y_gT = sb("y_gT", [P, 2, 4, P], F32, mam)
        squares = sb("squares", [P, 512], F32, mam)
        square_sum = sb("square_sum", [P, 2], F32, mam)
        ms = sb("ms", [P, 1], F32, mam)
        ms_eps = sb("ms_eps", [P, 1], F32, mam)
        group_scale = sb("group_scale", [P, 1], F32, mam)
        wT = sb("wT", [P, KC, DM], F32, mam)
        mam.close()

        bank = [whole.enter_context(nc.psum_tensor(f"bank{i}", [P, 512], F32)) for i in range(8)]
        ring_a = bank[0:4]
        ring_b = bank[4:6]
        pv_bank, oq_bank = bank[6], bank[7]

        names = """consts_ready x_in mask_in tables_in rope_k_in wk_in wv_in wq_in wo_in out_stored
            norm_stats norm_agg norm_eps norm_rstd xn_ready xnT_mm xnT_ready
            ctx_hi_ready ctx_lo_ready wk_hi_ready wk_lo_ready wv_hi_ready wv_lo_ready
            kproj_ready krope_mul krope_add k_hi_ready k_lo_ready
            qproj_ready qrope_mul qrope_add qT_mm qT_hi_ready qT_lo_ready
            vproj_ready v_copied vT_mm v_hi_ready v_lo_ready
            scores_ready scores_masked neg_max_ready probs_ready pT_mm pt_hi_ready pt_lo_ready pv_ready
            inv_sum_ready diag_ready bcast_mm bcast_ready attn_out_ready oproj_ready res_added
            small_in dequant_in dt_in gate_in0 gate_in1 hs_in0 hs_in1 wout_in0 wout_in1
            dt_mm dt_step dt_act neg_a a_dt_ready bc_mm bc_tap bc_conv bc_act_ready steps_ready segsum_mm decay_ready
            g_mm gm_ready digits_ready digits_off weights_ready wT_mm wT_ready
            hs_mm hs_tap hs_conv hs_act hsT_mm x_ready m_ready gate_mm gate_act y_mm y_sum y_gated square_ready
            ygT_mm ygT_ready out_mm ms_sum ms_eps_ready scale_ready out_added
            ffn_mm ffn_bias""".split()
        s = {n: whole.enter_context(nc.semaphore(n)) for n in names}
        ctx_in = [whole.enter_context(nc.semaphore(f"ctx_in{b}")) for b in range(KB)]
        gate_in, hs_in, wout_in = ([s[f"{n}{i}"] for i in range(2)] for n in ("gate_in", "hs_in", "wout_in"))
        tap_chain = whole.enter_context(nc.semaphore("tap_chain"))
        block = whole.enter_context(nc.Block())

        N1 = 1

        @block.sync
        def _(sp):
            sp.dma_start(xres[:, :], x).then_inc(s["x_in"], 16)
            for b in range(KB):
                if b >= 2:
                    sp.wait_ge(s["ctx_lo_ready"], b - 1)
                sp.dma_start(ctx_raw[:, b % 2, :, :], ctx_t[:, :, b * 512:(b + 1) * 512]).then_inc(ctx_in[b], 16)
                if b == 0:
                    sp.dma_start(wk_raw[:, :, :], wk[0]).then_inc(s["wk_in"], 16)
                    sp.dma_start(cos_k[:, :], rope_k_cos).then_inc(s["rope_k_in"], 16)
                    sp.dma_start(sin_k[:, :], rope_k_sin).then_inc(s["rope_k_in"], 16)
                if b == 1:
                    sp.dma_start(wq_sb[:, :, :], wq[0]).then_inc(s["wq_in"], 16)
                    sp.dma_start(cos_q[:, :], rope_q_cos).then_inc(s["tables_in"], 16)
                    sp.dma_start(sin_q[:, :], rope_q_sin).then_inc(s["tables_in"], 16)
                    sp.dma_start(wv_raw[:, :, :], wv[0]).then_inc(s["wv_in"], 16)
            sp.dma_start(mask_sb[:, :], mask).then_inc(s["mask_in"], 16)
            sp.dma_start(bias_bc[:, :], q_bias.partition_broadcast(P)).then_inc(s["tables_in"], 16)
            sp.dma_start(wo_sb[:, :, :], wo[0]).then_inc(s["wo_in"], 16)
            with sp.Fori(1, G) as g:
                sp.wait_ge(s["kproj_ready"], KB * g)
                sp.dma_start(wk_raw[:, :, :], wk[g]).then_inc(s["wk_in"], 16)
                sp.wait_ge(s["qproj_ready"], g)
                sp.dma_start(wq_sb[:, :, :], wq[g]).then_inc(s["wq_in"], 16)
                sp.wait_ge(s["vproj_ready"], KB * g)
                sp.dma_start(wv_raw[:, :, :], wv[g]).then_inc(s["wv_in"], 16)
                sp.wait_ge(s["oproj_ready"], g)
                sp.dma_start(wo_sb[:, :, :], wo[g]).then_inc(s["wo_in"], 16)

            sp.wait_ge(s["vproj_ready"], KB * G)
            for i in range(BCC):
                ring, sem = (w_gate_sb, gate_in) if i < 2 else (w_out_sb, wout_in)
                sp.dma_start(ring[:, i % 2, :, :], w_bc[i]).then_inc(sem[i % 2], 16)
            sp.wait_ge(s["res_added"], G)
            sp.dma_start(w_dt_sb[:, :, :], w_dt).then_inc(s["dt_in"], 16)
            for dst, src in ((dtb_bc, dt_bias), (alog_bc, a_log), (d_bc, d_skip)):
                sp.dma_start(dst[:, :], src.partition_broadcast(P)).then_inc(s["small_in"], 16)
            sp.dma_start(cw[:, :, :], conv_w).then_inc(s["small_in"], 16)
            sp.dma_start(cb[:, :], conv_b).then_inc(s["small_in"], 16)
            sp.dma_start(nw[:, :], norm_w).then_inc(s["small_in"], 16)
            sp.dma_start(w_hs_sb[:, 0, :, :], w_hs[0]).then_inc(hs_in[0], 16)
            sp.dma_start(w_hs_sb[:, 1, :, :], w_hs[1]).then_inc(hs_in[1], 16)
            sp.dma_start(packed[:, :, :], q_packed).then_inc(s["dequant_in"], 16)
            sp.dma_start(scale_sb[:, :, :], q_scale).then_inc(s["dequant_in"], 16)
            sp.dma_start(zero_sb[:, :, :], q_zero).then_inc(s["dequant_in"], 16)
            for i in range(2):
                sp.wait_ge(s["bc_mm"], i + 1)
                sp.dma_start(w_gate_sb[:, i, :, :], w_gate[i]).then_inc(gate_in[i], 16)
            for i in range(2):
                sp.wait_ge(s["bc_mm"], i + 3)
                sp.dma_start(w_out_sb[:, i, :, :], w_out[i]).then_inc(wout_in[i], 16)

            def refill(n, i, hs, gate, out_w):
                c = 2 * n + i
                if hs:
                    sp.wait_ge(s["hs_mm"], c + 2)
                    sp.dma_start(w_hs_sb[:, 1 - i, :, :], w_hs[c + 3]).then_inc(hs_in[1 - i], 16)
                if gate:
                    sp.wait_ge(s["gate_mm"], c + 1)
                    sp.dma_start(w_gate_sb[:, i, :, :], w_gate[c + 2]).then_inc(gate_in[i], 16)
                if out_w:
                    sp.wait_ge(s["out_mm"], c)
                    sp.dma_start(w_out_sb[:, 1 - i, :, :], w_out[c + 1]).then_inc(wout_in[1 - i], 16)

            sp.wait_ge(s["hs_mm"], 1)
            sp.dma_start(w_hs_sb[:, 0, :, :], w_hs[2]).then_inc(hs_in[0], 16)
            refill(0, 0, True, True, False)
            refill(0, 1, True, True, True)
            with sp.Fori(1, CH // 2 - 2) as n:
                refill(n, 0, True, True, True)
                refill(n, 1, True, True, True)
            refill(CH // 2 - 2, 0, True, True, True)
            refill(CH // 2 - 2, 1, False, True, True)
            refill(CH // 2 - 1, 0, False, False, True)

            sp.wait_ge(s["ffn_bias"], 2)
            sp.dma_start(out, xres[:, :]).then_inc(s["out_stored"], 16)
            sp.wait_ge(s["out_stored"], 16)

        @block.tensor
        def _(pe):
            def pairs(dst, left_hi, left_lo, right_hi, right_lo, first, last):
                pe.matmul(dst, left_hi, right_hi, start=first, stop=False)
                pe.matmul(dst, left_hi, right_lo, start=False, stop=False)
                return pe.matmul(dst, left_lo, right_hi, start=False, stop=last)

            def transpose_norm(n):
                pe.wait_ge(s["xn_ready"], n)
                for c in range(KC):
                    last = pe.transpose(oq_bank[:, c * P:(c + 1) * P], xn[:, c * P:(c + 1) * P], ident[:, :])
                last.then_inc(s["xnT_mm"], 1)

            def project_k(g):
                pe.wait_ge(s["wk_lo_ready"], g + 1)
                for b in range(KB):
                    if isinstance(g, int) and g == 0:
                        pe.wait_ge(s["ctx_lo_ready"], b + 1)
                    else:
                        pe.wait_ge(s["scores_masked"], HG * KB * g - KB + b + 1)
                    for c in range(KC):
                        last = pairs(ring_a[b][:, :], wk_hi[:, c, :], wk_lo[:, c, :],
                                     ctx_hi[:, c, b * 512:(b + 1) * 512], ctx_lo[:, c, b * 512:(b + 1) * 512],
                                     c == 0, c == KC - 1)
                    last.then_inc(s["kproj_ready"], 1)

            def project_q(g):
                pe.wait_ge(s["wq_in"], 16 * (g + 1))
                if isinstance(g, int) and g == 0:
                    pe.wait_ge(s["xnT_ready"], 1)
                for c in range(KC):
                    last = pe.matmul(oq_bank[:, :], xnT[:, c, :], wq_sb[:, c, :], start=c == 0, stop=c == KC - 1)
                last.then_inc(s["qproj_ready"], 1)

            def transpose_q(g):
                pe.wait_ge(s["qrope_add"], g + 1)
                if not (isinstance(g, int) and g == 0):
                    pe.wait_ge(s["pt_lo_ready"], KT * g)
                for h in range(HG):
                    last = pe.transpose(ring_b[1][:, h * P:(h + 1) * P], rope_a[:, 0, h * P:(h + 1) * P], ident[:, :])
                last.then_inc(s["qT_mm"], 1)

            def project_v_block(g, b):
                if b == 0:
                    pe.wait_ge(s["wv_lo_ready"], g + 1)
                pe.wait_ge(s["krope_mul"], KB * g + b + 1)
                for c in range(KC):
                    last = pairs(ring_a[b][:, :], wv_hi[:, c, :], wv_lo[:, c, :],
                                 ctx_hi[:, c, b * 512:(b + 1) * 512], ctx_lo[:, c, b * 512:(b + 1) * 512],
                                 c == 0, c == KC - 1)
                last.then_inc(s["vproj_ready"], 1)

            def transpose_v_block(g, b):
                pe.wait_ge(s["v_copied"], KB * g + b + 1)
                if b == 0 and not (isinstance(g, int) and g == 0):
                    pe.wait_ge(s["bcast_ready"], g)
                if b == 1:
                    pe.wait_ge(s["qT_lo_ready"], g + 1)
                if b >= 2:
                    pe.wait_ge(s["v_lo_ready"], KB * g + b - 1)
                for t in range(4):
                    last = pe.transpose(ring_b[b % 2][:, t * P:(t + 1) * P], rope_b[:, b % 2, t * P:(t + 1) * P],
                                        ident[:, :])
                last.then_inc(s["vT_mm"], 1)

            def scores(g):
                pe.wait_ge(s["qT_lo_ready"], g + 1)
                for h in range(HG):
                    for b in range(KB):
                        j = KB * h + b
                        if h == 0:
                            pe.wait_ge(s["k_lo_ready"], KB * g + b + 1)
                            pe.wait_ge(s["v_copied"], KB * g + b + 1)
                        else:
                            pe.wait_ge(s["scores_masked"], HG * KB * g + j - KB + 1)
                        pairs(ring_a[b][:, :], qT_hi[:, h, :], qT_lo[:, h, :], k_hi[:, b * 512:(b + 1) * 512],
                              k_lo[:, b * 512:(b + 1) * 512], True, True).then_inc(s["scores_ready"], 1)

            def transpose_probs(g, t):
                if t == 0:
                    pe.wait_ge(s["probs_ready"], HG * (g + 1))
                    pe.wait_ge(s["v_lo_ready"], KB * g + 3)
                elif t == 1:
                    pe.wait_ge(s["v_lo_ready"], KB * g + 4)
                else:
                    pe.wait_ge(s["pt_lo_ready"], KT * g + t - 1)
                for h in range(HG):
                    last = pe.transpose(ring_b[t % 2][:, h * P:(h + 1) * P], probs[:, h, t * P:(t + 1) * P],
                                        ident[:, :])
                last.then_inc(s["pT_mm"], 1)

            def attend(g):
                for t in range(KT + 1):
                    if t < KT:
                        transpose_probs(g, t)
                    if t >= 1:
                        j = t - 1
                        pe.wait_ge(s["pt_lo_ready"], KT * g + j + 1)
                        last = pairs(pv_bank[:, :], v_hi[:, j, :], v_lo[:, j, :], pt_hi[:, j % 2, :],
                                     pt_lo[:, j % 2, :], j == 0, j == KT - 1)
                last.then_inc(s["pv_ready"], 1)
                pe.wait_ge(s["diag_ready"], g + 1)
                pe.matmul(ring_b[0][:, :], ones[:, :], probs[:, 0, 0:512], start=True, stop=True)\
                    .then_inc(s["bcast_mm"], 1)

            def project_out(g):
                pe.wait_ge(s["wo_in"], 16 * (g + 1))
                pe.wait_ge(s["attn_out_ready"], g + 1)
                for h in range(HG):
                    last = pe.matmul(oq_bank[:, :], probs[:, 1, h * P:(h + 1) * P], wo_sb[:, h, :],
                                     start=h == 0, stop=h == HG - 1)
                last.then_inc(s["oproj_ready"], 1)

            def project_v(g, before_last=None):
                for b in range(KB + 2):
                    if b < KB:
                        project_v_block(g, b)
                    if b == KB + 1 and before_last:
                        before_last()
                    if b >= 2:
                        transpose_v_block(g, b - 2)

            pe.wait_ge(s["consts_ready"], 4)
            transpose_norm(1)
            project_k(0)
            project_q(0)
            transpose_q(0)
            project_v(0)
            with pe.Fori(0, G - 1) as g:
                scores(g)
                project_k(g + 1)
                project_q(g + 1)
                attend(g)
                transpose_q(g + 1)
                project_v(g + 1, lambda: project_out(g))
            scores(G - 1)
            attend(G - 1)
            project_out(G - 1)

            transpose_norm(2)
            pe.wait_ge(s["xnT_ready"], 2)
            pe.wait_ge(s["dt_in"], 16)
            for c in range(KC):
                last = pe.matmul(bank[0][:, 0:MH], xnT[:, c, :], w_dt_sb[:, c, :], start=c == 0, stop=c == KC - 1)
            last.then_inc(s["dt_mm"], 1)

            def project_transposed(dst, w, done):
                for t in range(4):
                    for c in range(KC):
                        last = pe.matmul(dst[:, t * P:(t + 1) * P], w[:, c, t * P:(t + 1) * P], xnT[:, c, :],
                                         start=c == 0, stop=c == KC - 1)
                last.then_inc(done, 1)

            for i in range(BCC):
                ring, sem = (w_gate_sb, gate_in) if i < 2 else (w_out_sb, wout_in)
                pe.wait_ge(sem[i % 2], 16)
                project_transposed(bank[1 + i], ring[:, i % 2, :, :], s["bc_mm"])

            def segment_sums(n):
                for i in range(2):
                    pe.wait_ge(s["steps_ready"], 2 * n + i + 1)
                    if i == 1:
                        pe.wait_ge(s["dt_step"], 1)
                    at_least(pe, s["decay_ready"], 2 * n + i - 1)
                    for j in range(2):
                        dst = bank[(5 + 2 * i + j) % 8]
                        last = pe.matmul(dst[:, :], below[:, :],
                                         steps[:, i, 4 * j:4 * j + 4, :].rearrange("p h l -> p (h l)"),
                                         start=True, stop=True)
                    last.then_inc(s["segsum_mm"], 1)

            segment_sums(0)
            with pe.Fori(1, CH // 2) as n:
                segment_sums(n)

            for c in range(KC):
                if c == 0:
                    pe.wait_ge(s["weights_ready"], 1)
                    pe.wait_ge(s["bc_tap"], 16)
                    pe.wait_ge(s["bc_conv"], 16)
                for o in range(KC):
                    last = pe.transpose(bank[1 + c][:, o * P:(o + 1) * P], weights[:, o, c * P:(c + 1) * P],
                                        ident[:, :])
                last.then_inc(s["wT_mm"], 1)

            pe.wait_ge(s["bc_act_ready"], BCC)
            pe.wait_ge(s["decay_ready"], CH)
            for g in range(G):
                last = pe.matmul(bank[5 + g // 4][:, (g % 4) * P:(g % 4 + 1) * P], bc_act[:, g, :], bc_act[:, 8 + g, :],
                                 start=True, stop=True)
            last.then_inc(s["g_mm"], 1)

            def project_hs(c, i):
                pe.wait_ge(hs_in[i], 16 * (c // 2 + 1) if isinstance(c, int) else c)
                project_transposed(bank[i], w_hs_sb[:, i, :, :], s["hs_mm"])

            def hs_step(n, i):
                pe.wait_ge(hs_in[i], 16 * n + 16)
                if not (isinstance(n, int) and n == 0):
                    pe.wait_ge(s["hs_conv"], 12 * (2 * n + i - 1))
                project_transposed(bank[i], w_hs_sb[:, i, :, :], s["hs_mm"])

            def out_step(n, i):
                pe.wait_ge(wout_in[i], 16 * n + 32)
                pe.wait_ge(s["ygT_ready"], 4 * (2 * n + i + 1))
                if i == 0:
                    at_least(pe, s["out_added"], n)
                for t in range(4):
                    last = pe.matmul(bank[6][:, :], y_gT[:, i, t, :], w_out_sb[:, i, t, :],
                                     start=i == 0 and t == 0, stop=i == 1 and t == 3)
                last.then_inc(s["out_mm"], 1)

            def chunk_step(n, i, first, last_chunk):
                c = 2 * n + i
                if not last_chunk:
                    hs_step(n + i, 1 - i)
                pe.wait_ge(s["hs_act"], c + 1)
                at_least(pe, s["x_ready"], c)
                for t in range(4):
                    last = pe.transpose(bank[3][:, t * P:(t + 1) * P], hsT[:, i, t, :], ident[:, :])
                last.then_inc(s["hsT_mm"], 1)
                pe.wait_ge(gate_in[i], 16 * n + 32)
                at_least(pe, s["gate_act"], c)
                for k in range(KC):
                    last = pe.matmul(bank[2][:, :], xnT[:, k, :], w_gate_sb[:, i, k, :], start=k == 0, stop=k == KC - 1)
                last.then_inc(s["gate_mm"], 1)
                pe.wait_ge(s["x_ready"], c + 1)
                pe.wait_ge(s["m_ready"], c + 1)
                at_least(pe, s["y_sum"], c)
                for h in range(HC):
                    last = pe.matmul(bank[4][:, h * PH:(h + 1) * PH], m_t[:, i, h, :], x_dt[:, i, h, :],
                                     start=True, stop=True)
                last.then_inc(s["y_mm"], 1)
                if not first:
                    out_step(n + i - 1, 1 - i)
                pe.wait_ge(s["y_gated"], c + 1)
                if not (isinstance(n, int) and n == 0 and i == 0):
                    pe.wait_ge(s["ygT_ready"], 4 * c)
                for t in range(4):
                    last = pe.transpose(bank[5][:, t * P:(t + 1) * P], y[:, i, t * P:(t + 1) * P], ident[:, :])
                last.then_inc(s["ygT_mm"], 1)

            pe.wait_ge(s["wT_ready"], KC)
            hs_step(0, 0)
            pe.wait_ge(s["gm_ready"], 2)
            chunk_step(0, 0, True, False)
            chunk_step(0, 1, False, False)
            with pe.Fori(1, CH // 2 - 1) as n:
                chunk_step(n, 0, False, False)
                chunk_step(n, 1, False, False)
            chunk_step(CH // 2 - 1, 0, False, False)
            chunk_step(CH // 2 - 1, 1, False, True)
            out_step(CH // 2 - 1, 1)

            transpose_norm(3)
            pe.wait_ge(s["xnT_ready"], 3)
            for c in range(KC):
                last = pe.matmul(bank[0][:, :], xnT[:, c, :], wT[:, c, :], start=c == 0, stop=c == KC - 1)
            last.then_inc(s["ffn_mm"], 1)

        @block.scalar
        def _(act):
            act.wait_ge(s["xnT_mm"], 1)
            act.activation(xnT[:, :, :].rearrange("p c t -> p (c t)"), oq_bank[:, :], ACT.Copy).then_inc(s["xnT_ready"], 1)

            def k_high(g):
                for b in range(KB):
                    act.wait_ge(s["krope_add"], KB * g + b + 1)
                    act.activation(k_hi[:, b * 512:(b + 1) * 512], rope_a[:, b % 2, :], ACT.Copy)\
                        .then_inc(s["k_hi_ready"], 1)

            def q_high(g):
                act.wait_ge(s["qT_mm"], g + 1)
                act.activation(qT_hi[:, :, :].rearrange("p h t -> p (h t)"), ring_b[1][:, :], ACT.Copy)\
                    .then_inc(s["qT_hi_ready"], 1)

            def v_copies(g):
                for b in range(KB + 2):
                    if b < KB:
                        act.wait_ge(s["vproj_ready"], KB * g + b + 1)
                        act.wait_ge(s["krope_add"], KB * g + KB)
                        act.wait_ge(s["qrope_add"], g + 1)
                        if b >= 2:
                            act.wait_ge(s["vT_mm"], KB * g + b - 1)
                        act.activation(rope_b[:, b % 2, :], ring_a[b][:, :], ACT.Copy).then_inc(s["v_copied"], 1)
                    if b >= 2:
                        j = b - 2
                        act.wait_ge(s["vT_mm"], KB * g + j + 1)
                        act.activation(v_hi[:, 4 * j:4 * j + 4, :].rearrange("p t d -> p (t d)"), ring_b[j % 2][:, :],
                                       ACT.Copy).then_inc(s["v_hi_ready"], 1)

            def exps(g):
                for h in range(HG):
                    act.wait_ge(s["neg_max_ready"], HG * g + h + 1)
                    act.activation(probs[:, h, :], probs[:, h, :], ACT.Exp, bias=neg_max[:, h:h + 1],
                                   accum_out=row_sum[:, h:h + 1]).then_inc(s["probs_ready"], 1)

            def pt_high(g):
                for t in range(KT):
                    act.wait_ge(s["pT_mm"], KT * g + t + 1)
                    act.activation(pt_hi[:, t % 2, :], ring_b[t % 2][:, :], ACT.Copy).then_inc(s["pt_hi_ready"], 1)
                act.wait_ge(s["bcast_mm"], g + 1)
                act.activation(probs[:, 2, 0:512], ring_b[0][:, :], ACT.Copy).then_inc(s["bcast_ready"], 1)

            for b in range(KB):
                act.wait_ge(ctx_in[b], 16)
                act.activation(ctx_hi[:, :, b * 512:(b + 1) * 512], ctx_raw[:, b % 2, :, :], ACT.Copy)\
                    .then_inc(s["ctx_hi_ready"], 1)
            k_high(0)
            q_high(0)
            v_copies(0)
            with act.Fori(0, G - 1) as g:
                exps(g)
                k_high(g + 1)
                pt_high(g)
                q_high(g + 1)
                v_copies(g + 1)
            exps(G - 1)
            pt_high(G - 1)

            act.wait_ge(s["xnT_mm"], 2)
            act.activation(xnT[:, :, :].rearrange("p c t -> p (c t)"), oq_bank[:, :], ACT.Copy).then_inc(s["xnT_ready"], 1)
            act.wait_ge(s["small_in"], 96)
            act.activation(alog_bc[:, :], alog_bc[:, :], ACT.Exp).then_inc(s["neg_a"], 1)
            act.wait_ge(s["dt_step"], 2)
            act.activation(dt_t[:, 1, :], dt_t[:, 0, :], ACT.Exp).then_inc(s["dt_act"], 1)
            act.wait_ge(s["dt_act"], 1)
            act.activation(dt_t[:, 2, :], dt_t[:, 1, :], ACT.Ln, bias=1.0).then_inc(s["dt_act"], 1)
            for i in range(BCC):
                act.wait_ge(s["bc_mm"], i + 1)
                for t in range(4):
                    tile = 4 * i + t
                    act.activation(bc_acc[:, tile, :], bank[1 + i][:, t * P:(t + 1) * P], ACT.Identity,
                                   bias=cb[:, INTER // P + tile:INTER // P + tile + 1],
                                   scale=cw[:, INTER // P + tile, 3:4]).then_inc(s["bc_tap"], 1)
            with act.Fori(0, CH // 2) as n:
                for i in range(2):
                    act.wait_ge(s["segsum_mm"], 2 * n + i + 1)
                    for j in range(2):
                        src = bank[(5 + 2 * i + j) % 8]
                        last = act.activation(
                            decay[:, bass.ds(16 * n + 8 * i + 4 * j, 4), :].rearrange("p h l -> p (h l)"),
                            src[:, :], ACT.Exp)
                    last.then_inc(s["decay_ready"], 1)
            for i in range(BCC):
                act.wait_ge(s["bc_conv"], 4 * (i + 1))
                act.activation(bc_act[:, 4 * i:4 * i + 4, :].rearrange("p t l -> p (t l)"),
                               bc_acc[:, 4 * i:4 * i + 4, :].rearrange("p t l -> p (t l)"), ACT.Silu)\
                    .then_inc(s["bc_act_ready"], 1)
            for c in range(KC):
                act.wait_ge(s["wT_mm"], c + 1)
                act.activation(wT[:, c, :], bank[1 + c][:, :], ACT.Copy).then_inc(s["wT_ready"], 1)

            def tap_step(n, i):
                c = 2 * n + i
                act.wait_ge(s["hs_mm"], c + 1)
                if not (isinstance(n, int) and n == 0):
                    act.wait_ge(s["hs_act"], c - 1)
                for t in range(4):
                    act.activation(conv[:, i, t, :], bank[i][:, t * P:(t + 1) * P], ACT.Identity,
                                   bias=cb[:, bass.ds(4 * c + t, 1)],
                                   scale=cw[:, bass.ds(4 * c + t, 1), 3:4].rearrange("p a b -> p (a b)"))\
                        .then_inc(s["hs_tap"], 1)

            def silu_step(n, i):
                c = 2 * n + i
                act.wait_ge(s["hs_conv"], 12 * (c + 1))
                if not (isinstance(n, int) and n == 0):
                    act.wait_ge(s["hsT_mm"], c - 1)
                act.activation(hsT[:, i, :, :].rearrange("p t l -> p (t l)"),
                               conv[:, i, :, :].rearrange("p t l -> p (t l)"), ACT.Silu).then_inc(s["hs_act"], 1)

            def chunk_act(n, i, last_chunk):
                c = 2 * n + i
                if not last_chunk:
                    tap_step(n + i, 1 - i)
                act.wait_ge(s["gate_mm"], c + 1)
                if not (isinstance(n, int) and n == 0):
                    act.wait_ge(s["y_gated"], c - 1)
                act.activation(gate[:, i, :], bank[2][:, :], ACT.Silu).then_inc(s["gate_act"], 1)
                if not last_chunk:
                    silu_step(n + i, 1 - i)
                act.wait_ge(s["y_gated"], c + 1)
                if i == 0:
                    at_least(act, s["ms_sum"], n)
                if not (isinstance(n, int) and n == 0 and i == 0):
                    act.wait_ge(s["square_ready"], c)
                act.activation(squares[:, :], y[:, i, :], ACT.Square, accum_out=square_sum[:, i:i + 1])\
                    .then_inc(s["square_ready"], 1)
                act.wait_ge(s["ygT_mm"], c + 1)
                if not (isinstance(n, int) and n == 0):
                    act.wait_ge(s["out_mm"], c - 1)
                for t in range(4):
                    act.activation(y_gT[:, i, t, :], bank[5][:, t * P:(t + 1) * P], ACT.Identity,
                                   scale=nw[:, bass.ds(4 * c + t, 1)]).then_inc(s["ygT_ready"], 1)

            tap_step(0, 0)
            silu_step(0, 0)
            chunk_act(0, 0, False)
            chunk_act(0, 1, False)
            with act.Fori(1, CH // 2 - 1) as n:
                chunk_act(n, 0, False)
                chunk_act(n, 1, False)
            chunk_act(CH // 2 - 1, 0, False)
            chunk_act(CH // 2 - 1, 1, True)

            act.wait_ge(s["xnT_mm"], 3)
            act.activation(xnT[:, :, :].rearrange("p c t -> p (c t)"), oq_bank[:, :], ACT.Copy).then_inc(s["xnT_ready"], 1)

        @block.vector
        def _(dve):
            def layer_norm(n):
                dve.bn_stats(stats[:, :], xres[:, :]).then_inc(s["norm_stats"], 1)
                dve.wait_ge(s["norm_stats"], n)
                dve.bn_aggr(mean_var[:, :], stats[:, :]).then_inc(s["norm_agg"], 1)
                dve.wait_ge(s["norm_rstd"], n)
                dve.tensor_scalar(xn[:, :], xres[:, :], mean_var[:, 0:1], rstd[:, 0:1], ALU.subtract, ALU.mult)\
                    .then_inc(s["xn_ready"], 1)

            def k_rotate(g):
                for b in range(KB):
                    blk = slice(b * 512, (b + 1) * 512)
                    dve.wait_ge(s["kproj_ready"], KB * g + b + 1)
                    if b >= 2:
                        dve.wait_ge(s["k_lo_ready"], KB * g + b - 1)
                    elif not (isinstance(g, int) and g == 0):
                        dve.wait_ge(s["k_lo_ready"], KB * g)
                        dve.wait_ge(s["qT_mm"], g)
                        dve.wait_ge(s["vT_mm"], KB * g)
                    dve.tensor_tensor(rope_a[:, b % 2, :], ring_a[b][:, :], cos_k[:, blk], ALU.mult)
                    dve.tensor_tensor(rope_b[0:64, b % 2, :], ring_a[b][64:128, :], sin_k[64:128, blk], ALU.mult)
                    dve.tensor_tensor(rope_b[64:128, b % 2, :], ring_a[b][0:64, :], sin_k[0:64, blk], ALU.mult)\
                        .then_inc(s["krope_mul"], 1)

            def q_rotate(g):
                dve.wait_ge(s["qproj_ready"], g + 1)
                dve.wait_ge(s["k_lo_ready"], KB * g + 3)
                q = oq_bank[:, :].rearrange("p (h two d) -> p h two d", h=HG, two=2)
                qa = rope_a[:, 0, :].rearrange("p (h two d) -> p h two d", h=HG, two=2)
                qb = rope_b[:, 0, :].rearrange("p (h two d) -> p h two d", h=HG, two=2)
                cos = cos_q[:, :].unsqueeze(1).broadcast_to([P, 2 * HG, DH // 2])
                sin = sin_q[:, :].unsqueeze(1).broadcast_to([P, HG, DH // 2])
                dve.tensor_tensor(rope_a[:, 0, :].rearrange("p (h d) -> p h d", d=DH // 2),
                                  oq_bank[:, :].rearrange("p (h d) -> p h d", d=DH // 2), cos, ALU.mult)
                dve.scalar_tensor_tensor(qb[:, :, 0, :], q[:, :, 1, :], -1.0, sin, ALU.mult, ALU.mult)
                dve.tensor_tensor(qb[:, :, 1, :], q[:, :, 0, :], sin, ALU.mult).then_inc(s["qrope_mul"], 1)

            def q_low(g):
                dve.wait_ge(s["qT_hi_ready"], g + 1)
                dve.tensor_tensor(qT_lo[:, :, :].rearrange("p h t -> p (h t)"), ring_b[1][:, :],
                                  qT_hi[:, :, :].rearrange("p h t -> p (h t)").bitcast(F32), ALU.subtract)\
                    .then_inc(s["qT_lo_ready"], 1)

            def v_low(g):
                for b in range(KB):
                    dve.wait_ge(s["v_hi_ready"], KB * g + b + 1)
                    dve.tensor_tensor(v_lo[:, 4 * b:4 * b + 4, :].rearrange("p t d -> p (t d)"), ring_b[b % 2][:, :],
                                      v_hi[:, 4 * b:4 * b + 4, :].rearrange("p t d -> p (t d)").bitcast(F32),
                                      ALU.subtract).then_inc(s["v_lo_ready"], 1)

            def mask_scores(g):
                for h in range(HG):
                    for b in range(KB):
                        dve.wait_ge(s["mask_in"], 16)
                        dve.wait_ge(s["scores_ready"], HG * KB * g + KB * h + b + 1)
                        keep_wait_apart(dve)
                        dve.tensor_tensor_reduce(
                            out=probs[:, h, b * 512:(b + 1) * 512], in0=ring_a[b][:, :],
                            in1=mask_sb[:, b * 512:(b + 1) * 512], scale=1.0, scalar=LOWEST, op0=ALU.add, op1=ALU.max,
                            accum_out=block_max[:, h, b:b + 1]).then_inc(s["scores_masked"], 1)
                    dve.wait_ge(s["scores_masked"], HG * KB * g + KB * (h + 1))
                    dve.tensor_reduce(neg_max[:, h:h + 1], block_max[:, h, :], X_AXIS, ALU.max, negate=True)\
                        .then_inc(s["neg_max_ready"], 1)

            def pt_low(g):
                for t in range(KT):
                    dve.wait_ge(s["pt_hi_ready"], KT * g + t + 1)
                    dve.tensor_tensor(pt_lo[:, t % 2, :], ring_b[t % 2][:, :], pt_hi[:, t % 2, :].bitcast(F32),
                                      ALU.subtract).then_inc(s["pt_lo_ready"], 1)

            def normalise(g):
                dve.wait_ge(s["probs_ready"], HG * (g + 1))
                dve.reciprocal(inv_sum[:, :], row_sum[:, :]).then_inc(s["inv_sum_ready"], 1)
                dve.wait_ge(s["inv_sum_ready"], g + 1)
                dve.wait_ge(s["pT_mm"], KT * (g + 1))
                dve.tensor_tensor(probs[:, 0, 0:512].rearrange("p (h t) -> p h t", h=HG),
                                  ident[:, :].unsqueeze(1).broadcast_to([P, HG, P]),
                                  inv_sum[:, :].unsqueeze(2).broadcast_to([P, HG, P]), ALU.mult)\
                    .then_inc(s["diag_ready"], 1)

            def scale_out(g):
                dve.wait_ge(s["bcast_ready"], g + 1)
                dve.wait_ge(s["pv_ready"], g + 1)
                dve.tensor_tensor(probs[:, 1, 0:512], pv_bank[:, :], probs[:, 2, 0:512], ALU.mult)\
                    .then_inc(s["attn_out_ready"], 1)

            def add_out(g):
                dve.wait_ge(s["oproj_ready"], g + 1)
                dve.tensor_tensor(xres[:, :], xres[:, :], oq_bank[:, :], ALU.add).then_inc(s["res_added"], 1)
                dve.wait_ge(s["res_added"], g + 1)

            dve.wait_ge(s["x_in"], 16)
            layer_norm(1)
            for b in range(KB):
                dve.wait_ge(s["ctx_hi_ready"], b + 1)
                dve.tensor_tensor(ctx_lo[:, :, b * 512:(b + 1) * 512], ctx_raw[:, b % 2, :, :],
                                  ctx_hi[:, :, b * 512:(b + 1) * 512].bitcast(F32), ALU.subtract)\
                    .then_inc(s["ctx_lo_ready"], 1)
            dve.wait_ge(s["rope_k_in"], 32)
            k_rotate(0)
            dve.wait_ge(s["tables_in"], 48)
            q_rotate(0)
            q_low(0)
            v_low(0)
            with dve.Fori(0, G - 1) as g:
                mask_scores(g)
                k_rotate(g + 1)
                q_rotate(g + 1)
                pt_low(g)
                normalise(g)
                scale_out(g)
                q_low(g + 1)
                v_low(g + 1)
                add_out(g)
            mask_scores(G - 1)
            pt_low(G - 1)
            normalise(G - 1)
            scale_out(G - 1)
            add_out(G - 1)

            layer_norm(2)
            dve.wait_ge(s["small_in"], 96)
            dve.wait_ge(s["dt_mm"], 1)
            dve.tensor_tensor(dt_x[:, :], bank[0][:, 0:MH], dtb_bc[:, :], ALU.add).then_inc(s["dt_step"], 1)
            dve.wait_ge(s["dt_step"], 1)
            dve.scalar_tensor_tensor(dt_t[:, 0, :], dt_x[:, :], -1.0, dt_x[:, :], ALU.mult, ALU.min)\
                .then_inc(s["dt_step"], 1)
            dve.wait_ge(s["dt_act"], 1)
            dve.tensor_scalar(dt[:, :], dt_t[:, 1, :], 1.0, -1.0, ALU.add, ALU.add).then_inc(s["dt_step"], 1)
            dve.wait_ge(s["dt_step"], 3)
            dve.tensor_scalar(dt_t[:, 3, :], dt[:, :], 0.0, None, ALU.is_equal).then_inc(s["dt_step"], 1)
            dve.wait_ge(s["dt_step"], 4)
            dve.tensor_tensor(dt[:, :], dt[:, :], dt_t[:, 3, :], ALU.add).then_inc(s["dt_step"], 1)
            dve.wait_ge(s["dt_step"], 5)
            dve.reciprocal(dt[:, :], dt[:, :]).then_inc(s["dt_step"], 1)
            dve.wait_ge(s["dt_step"], 6)
            dve.wait_ge(s["dt_act"], 2)
            dve.tensor_tensor(dt_t[:, 2, :], dt_t[:, 2, :], dt[:, :], ALU.mult).then_inc(s["dt_step"], 1)
            dve.wait_ge(s["dt_step"], 7)
            dve.tensor_tensor(dt_t[:, 2, :], dt_t[:, 2, :], dt_t[:, 3, :], ALU.add).then_inc(s["dt_step"], 1)
            dve.wait_ge(s["dt_step"], 8)
            dve.tensor_tensor(dt_t[:, 2, :], dt_t[:, 2, :], dt_t[:, 1, :], ALU.mult).then_inc(s["dt_step"], 1)
            dve.wait_ge(s["dt_step"], 9)
            dve.scalar_tensor_tensor(dt[:, :], dt_x[:, :], 0.0, dt_t[:, 2, :], ALU.max, ALU.add)\
                .then_inc(s["dt_step"], 1)
            dve.wait_ge(s["dt_step"], 10)
            dve.wait_ge(s["neg_a"], 1)
            dve.scalar_tensor_tensor(a_dt[:, :], dt[:, :], -1.0, alog_bc[:, :], ALU.mult, ALU.mult)\
                .then_inc(s["a_dt_ready"], 1)
            dve.wait_ge(s["a_dt_ready"], 1)

            def steps_chunk(n, i):
                c = 2 * n + i
                if not (isinstance(n, int) and n == 0):
                    dve.wait_ge(s["segsum_mm"], c - 1)
                dve.tensor_tensor(steps[:, i, :, :], upper[:, :].unsqueeze(1).broadcast_to([P, HC, P]),
                                  a_dt[:, bass.ds(HC * c, HC)].unsqueeze(2).broadcast_to([P, HC, P]), ALU.mult)\
                    .then_inc(s["steps_ready"], 1)

            steps_chunk(0, 0)
            steps_chunk(0, 1)
            with dve.Fori(1, CH // 2) as n:
                steps_chunk(n, 0)
                steps_chunk(n, 1)

            def taps(acc, src, tile, t, done, count):
                for k in range(1, TAPS):
                    dve.wait_ge(done, count) if k > 1 else None
                    dve.scalar_tensor_tensor(acc[:, k:], src[:, t * P:t * P + P - k],
                                             cw[:, tile, TAPS - 1 - k:TAPS - k], acc[:, k:], ALU.mult, ALU.add)

            for i in range(BCC):
                dve.wait_ge(s["bc_tap"], 4 * (i + 1))
                for k in range(1, TAPS):
                    if k > 1:
                        dve.wait_ge(tap_chain, 4 * (2 * i + k - 1))
                    for t in range(4):
                        tile = 4 * i + t
                        dve.scalar_tensor_tensor(
                            bc_acc[:, tile, k:], bank[1 + i][:, t * P:t * P + P - k],
                            cw[:, INTER // P + tile, TAPS - 1 - k:TAPS - k], bc_acc[:, tile, k:], ALU.mult, ALU.add)\
                            .then_inc(tap_chain if k < TAPS - 1 else s["bc_conv"], 1)

            dve.wait_ge(s["dequant_in"], 48)
            dve.tensor_scalar(digits[:, :, :, 0], packed[:, :, :], 15, None, ALU.bitwise_and).then_inc(s["digits_ready"], 1)
            dve.tensor_scalar(digits[:, :, :, 1], packed[:, :, :], 4, None, ALU.arith_shift_right)\
                .then_inc(s["digits_ready"], 1)
            dve.wait_ge(s["digits_ready"], 2)
            for o in range(KC):
                dve.tensor_tensor(weights[:, o, :].rearrange("p (g k) -> p g k", g=QG),
                                  digits[:, o, :, :].rearrange("p (g k) two -> p g (k two)", g=QG),
                                  zero_sb[:, o, :].unsqueeze(2).broadcast_to([P, QG, DM // QG]), ALU.subtract)\
                    .then_inc(s["digits_off"], 1)
            dve.wait_ge(s["digits_off"], KC)
            for o in range(KC):
                last = dve.tensor_tensor(weights[:, o, :].rearrange("p (g k) -> p g k", g=QG),
                                         weights[:, o, :].rearrange("p (g k) -> p g k", g=QG),
                                         scale_sb[:, o, :].unsqueeze(2).broadcast_to([P, QG, DM // QG]), ALU.mult)
            last.then_inc(s["weights_ready"], 1)

            dve.wait_ge(s["g_mm"], 1)
            for j in range(2):
                dve.tensor_tensor(gm[:, 4 * j:4 * j + 4, :],
                                  bank[5 + j][:, :].rearrange("p (g l) -> p g l", g=4),
                                  upper[:, :].unsqueeze(1).broadcast_to([P, 4, P]), ALU.mult).then_inc(s["gm_ready"], 1)

            def conv_step(n, i):
                c = 2 * n + i
                dve.wait_ge(s["hs_tap"], 4 * (c + 1))
                for k in range(1, TAPS):
                    if k > 1:
                        dve.wait_ge(s["hs_conv"], 12 * c + 4 * (k - 1))
                    for t in range(4):
                        w = cw[:, bass.ds(4 * c + t, 1), TAPS - 1 - k:TAPS - k].rearrange("p a b -> p (a b)")
                        dve.scalar_tensor_tensor(conv[:, i, t, k:], bank[i][:, t * P:t * P + P - k], w,
                                                 conv[:, i, t, k:], ALU.mult, ALU.add).then_inc(s["hs_conv"], 1)

            def add_group(n):
                dve.wait_ge(s["out_mm"], 2 * (n + 1))
                dve.wait_ge(s["scale_ready"], n + 1)
                dve.scalar_tensor_tensor(xres[:, :], bank[6][:, :], group_scale[:, 0:1], xres[:, :], ALU.mult, ALU.add)\
                    .then_inc(s["out_added"], 1)
                dve.wait_ge(s["out_added"], n + 1)

            def chunk_dve(n, i, first_group, last_chunk):
                c = 2 * n + i
                dve.wait_ge(s["hsT_mm"], c + 1)
                if not first_group:
                    dve.wait_ge(s["y_mm"], c - 1)
                hs = bank[3][:, :].rearrange("p (h d) -> p h d", h=HC)
                dve.tensor_tensor(x_dt[:, i, :, :], hs, dt[:, bass.ds(HC * c, HC)].unsqueeze(2)
                                  .broadcast_to([P, HC, PH]), ALU.mult)
                dve.tensor_tensor(x_skip[:, i, :].rearrange("p (h d) -> p h d", h=HC), hs,
                                  d_bc[:, bass.ds(HC * c, HC)].unsqueeze(2).broadcast_to([P, HC, PH]), ALU.mult)\
                    .then_inc(s["x_ready"], 1)
                if not last_chunk:
                    conv_step(n + i, 1 - i)
                dve.wait_ge(s["y_mm"], c + 1)
                dve.wait_ge(s["x_ready"], c + 1)
                if not first_group:
                    dve.wait_ge(s["ygT_mm"], c - 1)
                    dve.wait_ge(s["square_ready"], c - 1)
                dve.tensor_tensor(y[:, i, :], bank[4][:, :], x_skip[:, i, :], ALU.add).then_inc(s["y_sum"], 1)
                dve.wait_ge(s["y_sum"], c + 1)
                dve.wait_ge(s["gate_act"], c + 1)
                dve.tensor_tensor(y[:, i, :], y[:, i, :], gate[:, i, :], ALU.mult).then_inc(s["y_gated"], 1)
                if i == 0 and not first_group:
                    add_group(n - 1)

            conv_step(0, 0)
            chunk_dve(0, 0, True, False)
            chunk_dve(0, 1, True, False)
            with dve.Fori(1, CH // 2 - 1) as n:
                chunk_dve(n, 0, False, False)
                chunk_dve(n, 1, False, False)
            chunk_dve(CH // 2 - 1, 0, False, False)
            chunk_dve(CH // 2 - 1, 1, False, True)
            add_group(CH // 2 - 1)

            layer_norm(3)
            dve.wait_ge(s["xn_ready"], 3)
            dve.tensor_tensor(xres[:, :], xres[:, :], bias_bc[:, :], ALU.add).then_inc(s["ffn_bias"], 1)
            dve.wait_ge(s["ffn_bias"], 1)
            dve.wait_ge(s["ffn_mm"], 1)
            dve.tensor_tensor(xres[:, :], xres[:, :], bank[0][:, :], ALU.add).then_inc(s["ffn_bias"], 1)

        @block.gpsimd
        def _(pool):
            def norm_scale(n):
                pool.wait_ge(s["norm_agg"], n)
                pool.tensor_scalar(var_eps[:, :], mean_var[:, 1:2], EPS, None, ALU.add).then_inc(s["norm_eps"], 1)
                pool.wait_ge(s["norm_eps"], n)
                pool.tensor_tensor(rstd[:, :], var_eps[:, :], half_neg[:, :], ALU.pow).then_inc(s["norm_rstd"], 1)

            def split_weight(raw, hi, lo, arrived, hi_done, lo_done, g):
                pool.wait_ge(arrived, 16 * (g + 1))
                keep_wait_apart(pool)
                pool.tensor_copy(hi[:, :, :], raw[:, :, :]).then_inc(hi_done, 1)
                pool.wait_ge(hi_done, g + 1)
                pool.tensor_tensor(lo[:, :, :], raw[:, :, :], hi[:, :, :].bitcast(F32), ALU.subtract)\
                    .then_inc(lo_done, 1)

            def k_finish(g):
                for b in range(KB + 1):
                    if b < KB:
                        pool.wait_ge(s["krope_mul"], KB * g + b + 1)
                        pool.tensor_tensor(rope_a[:, b % 2, :], rope_a[:, b % 2, :], rope_b[:, b % 2, :], ALU.add)\
                            .then_inc(s["krope_add"], 1)
                    if b >= 1:
                        j = b - 1
                        blk = slice(j * 512, (j + 1) * 512)
                        pool.wait_ge(s["k_hi_ready"], KB * g + j + 1)
                        pool.tensor_tensor(k_lo[:, blk], rope_a[:, j % 2, :], k_hi[:, blk].bitcast(F32), ALU.subtract)\
                            .then_inc(s["k_lo_ready"], 1)
                pool.wait_ge(s["qrope_mul"], g + 1)
                pool.tensor_tensor(rope_a[:, 0, :], rope_a[:, 0, :], rope_b[:, 0, :], ALU.add).then_inc(s["qrope_add"], 1)

            def split_weights(g):
                split_weight(wk_raw, wk_hi, wk_lo, s["wk_in"], s["wk_hi_ready"], s["wk_lo_ready"], g)
                split_weight(wv_raw, wv_hi, wv_lo, s["wv_in"], s["wv_hi_ready"], s["wv_lo_ready"], g)

            pool.memset(half_neg[:, :], -0.5).then_inc(s["consts_ready"], 1)
            pool.memset(ones[:, :], 1.0).then_inc(s["consts_ready"], 1)
            pool.wait_ge(s["consts_ready"], 2)
            pool.affine_select(out=ident[:, :], in_=ones[:, :], compare_op=ALU.is_equal, fill=0.0, base=0,
                               pattern=[[-1, P]], channel_multiplier=1).then_inc(s["consts_ready"], 1)
            pool.affine_select(out=upper[:, :], in_=ones[:, :], compare_op=ALU.is_ge, fill=0.0, base=0,
                               pattern=[[1, P]], channel_multiplier=-1).then_inc(s["consts_ready"], 1)
            pool.affine_select(out=below[:, :], in_=ones[:, :], compare_op=ALU.is_gt, fill=0.0, base=0,
                               pattern=[[-1, P]], channel_multiplier=1).then_inc(s["consts_ready"], 1)
            norm_scale(1)
            split_weights(0)
            k_finish(0)
            with pool.Fori(1, G) as g:
                split_weights(g)
                k_finish(g)

            norm_scale(2)

            def decay_products(n, i):
                c = 2 * n + i
                if isinstance(n, int) and n == 0:
                    pool.wait_ge(s["gm_ready"], 2)
                    pool.wait_ge(s["decay_ready"], CH)
                else:
                    pool.wait_ge(s["y_mm"], c - 1)
                pool.tensor_tensor(m_t[:, i, :, :], decay[:, bass.ds(HC * c, HC), :], gm[:, :, :], ALU.mult)\
                    .then_inc(s["m_ready"], 1)

            def group_norm(n):
                pool.wait_ge(s["square_ready"], 2 * (n + 1))
                pool.tensor_tensor(ms[:, :], square_sum[:, 0:1], square_sum[:, 1:2], ALU.add).then_inc(s["ms_sum"], 1)
                pool.wait_ge(s["ms_sum"], n + 1)
                keep_wait_apart(pool)
                pool.tensor_scalar(ms_eps[:, :], ms[:, :], NG / INTER, EPS, ALU.mult, ALU.add)\
                    .then_inc(s["ms_eps_ready"], 1)
                pool.wait_ge(s["ms_eps_ready"], n + 1)
                at_least(pool, s["out_added"], n)
                pool.tensor_tensor(group_scale[:, :], ms_eps[:, :], half_neg[:, :], ALU.pow).then_inc(s["scale_ready"], 1)

            decay_products(0, 0)
            decay_products(0, 1)

            def pool_step(n):
                decay_products(n, 0)
                group_norm(n - 1)
                decay_products(n, 1)

            pool_step(1)
            with pool.Fori(2, CH // 2) as n:
                pool_step(n)
            group_norm(CH // 2 - 1)
            norm_scale(3)


_F = np.float32


def _rope_tables():
    freq = _F(1.0) / _F(10000.0) ** (np.arange(0, DH, 2, dtype=_F) / _F(DH))
    angle = np.arange(SK, dtype=_F)[:, None] * freq[None, :].astype(_F)
    cos, sin = np.cos(angle.astype(np.float64)), np.sin(angle.astype(np.float64))
    k_cos = np.concatenate([cos.T, cos.T]).astype(_F)
    k_sin = np.concatenate([sin.T, -sin.T]).astype(_F)
    q_scale = 1.0 / np.sqrt(float(DH))
    return k_cos, k_sin, (cos[:P] * q_scale).astype(_F), (sin[:P] * q_scale).astype(_F)


def kernel(**inputs):
    import concourse.bacc as bacc
    from concourse.bass_utils import run_bass_kernel_spmd

    a = {name: np.asarray(v) for name, v in inputs.items()}

    def by_input(w, columns):
        return w.reshape(KC, P, -1, columns).transpose(2, 1, 0, 3)

    w_in = a["L0_attn_in_proj_w"].T
    gate_end, hs_end, bc_end = INTER, 2 * INTER, 2 * INTER + 2 * G * NS
    k_cos, k_sin, q_cos, q_sin = _rope_tables()
    laid = {
        "x": a["x"][0],
        "mask": a["mask_BxSxS2_ff0"][0],
        "ctx_t": a["ctx_4096"][0].T.reshape(KC, P, SK).transpose(1, 0, 2),
        "rope_k_cos": k_cos, "rope_k_sin": k_sin, "rope_q_cos": q_cos, "rope_q_sin": q_sin,
        "wk": by_input(a["L0_xattn_wk"], DH),
        "wv": by_input(a["L0_xattn_wv"], DH),
        "wq": by_input(a["L0_xattn_wq"], HG * DH),
        "wo": a["L0_xattn_wo"].reshape(G, HG, DH, DM).transpose(0, 2, 1, 3),
        "w_dt": by_input(w_in[:, bc_end:], MH)[0],
        "w_bc": by_input(w_in[:, hs_end:bc_end], 512),
        "w_hs": by_input(w_in[:, gate_end:hs_end], 512),
        "w_gate": by_input(w_in[:, :gate_end], 512),
        "w_out": a["L0_attn_out_proj_w"].T.reshape(CH, 4, P, DM).transpose(0, 2, 1, 3),
        "conv_w": a["L0_attn_conv_w"].reshape(XT_TILES, P, TAPS).transpose(1, 0, 2),
        "conv_b": a["L0_attn_conv_b"].reshape(XT_TILES, P).T,
        "dt_bias": a["L0_attn_dt_bias"],
        "a_log": a["L0_attn_A_log"],
        "d_skip": a["L0_attn_D"],
        "norm_w": a["L0_attn_norm_weight"].reshape(INTER // P, P).T,
        "q_packed": a["L0_ffn_weight_quantized"].reshape(KC, P, DM // 2).transpose(1, 0, 2),
        "q_scale": a["L0_ffn_weight_scales"].reshape(KC, P, QG).transpose(1, 0, 2),
        "q_zero": a["L0_ffn_weight_zero_points"].reshape(KC, P, QG).transpose(1, 0, 2),
        "q_bias": a["L0_ffn_bias"],
    }
    nc = bacc.Bacc("TRN2", target_bir_lowering=False, num_devices=1)
    arrays, args = {}, []
    for name, v in laid.items():
        arrays[f"in_{name}"] = v = np.ascontiguousarray(v)
        args.append(nc.dram_tensor(f"in_{name}", v.shape, mybir.dt.from_np(v.dtype), kind="ExternalInput").ap())
    args.append(nc.dram_tensor("out_x", (P, DM), F32, kind="ExternalOutput").ap())
    build(nc, *args)
    r = run_bass_kernel_spmd(nc, [arrays], core_ids=[0])
    return r.results[0]["out_x"].reshape(1, P, DM)
```

```python
from contextlib import ExitStack

import numpy as np

import concourse.bass as bass
from concourse import mybir

F32 = mybir.dt.float32
F32R = mybir.dt.float32r
I32 = mybir.dt.int32
ALU = mybir.AluOpType
ACT = mybir.ActivationFunctionType
X_AXIS = mybir.AxisListType.X

P = 128
DM = 512
KC = DM // P
SK = 2048
KB = SK // 512
KT = SK // P
G = 8
HG = 4
DH = 128
INTER = 8192
CH = INTER // 512
HC = 8
PH = 64
NS = 128
MH = 128
TAPS = 4
BCC = 4
XT_TILES = INTER // P + 4 * BCC
NG = 8
QG = 32
EPS = 1e-5
LOWEST = -3.4028234663852886e38


def at_least(eng, sem, count):
    if not isinstance(count, int) or count > 0:
        eng.wait_ge(sem, count)


def keep_wait_apart(eng):
    eng.nop(nofuse=True)


def build(nc, x, mask, ctx_t, rope_k_cos, rope_k_sin, rope_q_cos, rope_q_sin, wk, wv, wq, wo, w_dt, w_bc,
          w_hs, w_gate, w_out, conv_w, conv_b, dt_bias, a_log, d_skip, norm_w, q_packed, q_scale, q_zero,
          q_bias, out):
    with ExitStack() as whole:
        def sb(name, shape, dt=F32, scope=whole):
            return scope.enter_context(nc.sbuf_tensor(name, shape, dt))

        xres = sb("xres", [P, DM])
        for_q = ExitStack()
        qx_lo = sb("qx_lo", [P, KC, P], F32R, for_q)
        qx_hi = sb("qx_hi", [P, KC, P], F32R, for_q)
        for_q.close()
        xn = sb("xn", [P, DM])
        bias_bc = sb("bias_bc", [P, DM])
        xnT = sb("xnT", [P, KC, P])
        ident = sb("ident", [P, P])
        ones = sb("ones", [P, P])
        upper = sb("upper", [P, P])
        below = sb("below", [P, P])
        stats = sb("stats", [P, 6])
        mean_var = sb("mean_var", [P, 2])
        var_eps = sb("var_eps", [P, 1])
        rstd = sb("rstd", [P, 1])
        half_neg = sb("half_neg", [P, 1])

        attn = ExitStack()
        ctx_hi = sb("ctx_hi", [P, KC, SK], F32R, attn)
        ctx_lo = sb("ctx_lo", [P, KC, SK], F32R, attn)
        k_hi = sb("k_hi", [P, SK], F32R, attn)
        k_lo = sb("k_lo", [P, SK], F32R, attn)
        v_hi = sb("v_hi", [P, KT, DH], F32R, attn)
        v_lo = sb("v_lo", [P, KT, DH], F32R, attn)
        cos_k = sb("cos_k", [P, SK], F32, attn)
        sin_k = sb("sin_k", [P, SK], F32, attn)
        mask_sb = sb("mask_sb", [P, SK], F32, attn)
        pt_hi_01 = sb("pt_hi_01", [P, 2, 512], F32R, attn)
        pt_lo_01 = sb("pt_lo_01", [P, 2, 512], F32R, attn)
        third = ExitStack()
        sb("rope_a_first", [P, 512], F32, third)
        pt_hi_2 = sb("pt_hi_2", [P, 512], F32R, third)
        sb("rope_b_first", [P, 512], F32, third)
        pt_lo_2 = sb("pt_lo_2", [P, 512], F32R, third)
        third.close()
        rope_a = sb("rope_a", [P, 2, 512], F32, attn)
        rope_b = sb("rope_b", [P, 2, 512], F32, attn)
        pt_hi = [pt_hi_01[:, 0, :], pt_hi_01[:, 1, :], pt_hi_2[:, :]]
        pt_lo = [pt_lo_01[:, 0, :], pt_lo_01[:, 1, :], pt_lo_2[:, :]]
        wqo_hi = sb("wqo_hi", [P, KC, 512], F32R, attn)
        wk_hi = sb("wk_hi", [P, KC, DH], F32R, attn)
        wv_hi = sb("wv_hi", [P, KC, DH], F32R, attn)
        arriving = ExitStack()
        wk_raw = sb("wk_raw", [P, KC, DH], F32, arriving)
        wv_raw = sb("wv_raw", [P, KC, DH], F32, arriving)
        wqo_raw = sb("wqo_raw", [P, KC, 512], F32, arriving)
        arriving.close()
        wk_lo = sb("wk_lo", [P, KC, DH], F32R, attn)
        wv_lo = sb("wv_lo", [P, KC, DH], F32R, attn)
        wqo_lo = sb("wqo_lo", [P, KC, 512], F32R, attn)
        qT_hi = sb("qT_hi", [P, HG, P], F32R, attn)
        qT_lo = sb("qT_lo", [P, HG, P], F32R, attn)
        cos_q = sb("cos_q", [P, DH // 2], F32, attn)
        sin_q = sb("sin_q", [P, DH // 2], F32, attn)
        block_max = sb("block_max", [P, HG, KB], F32, attn)
        neg_max = sb("neg_max", [P, HG], F32, attn)
        row_sum = sb("row_sum", [P, HG], F32, attn)
        inv_sum = sb("inv_sum", [P, HG], F32, attn)
        stage = ExitStack()
        ctx_raw = sb("ctx_raw", [P, KB, KC, 512], F32, stage)
        stage.close()
        output = ExitStack()
        sb("probs_of_three", [P, HG - 1, SK], F32, output)
        attn_hi = sb("attn_hi", [P, HG, P], F32R, output)
        attn_lo = sb("attn_lo", [P, HG, P], F32R, output)
        output.close()
        probs = sb("probs", [P, HG, SK], F32, attn)
        attn.close()

        mam = ExitStack()
        arriving = ExitStack()
        w_gate_sb = sb("w_gate_sb", [P, 2, KC, 512], F32, arriving)
        w_out_sb = sb("w_out_sb", [P, 2, KC, 512], F32, arriving)
        arriving.close()
        w_gate_lo = sb("w_gate_lo", [P, 2, KC, 512], F32R, mam)
        w_out_lo = sb("w_out_lo", [P, 2, KC, 512], F32R, mam)
        w_hs_sb = sb("w_hs_sb", [P, 2, KC, 512], F32, mam)
        w_dt_sb = sb("w_dt_sb", [P, KC, MH], F32, mam)
        cw = sb("cw", [P, XT_TILES, TAPS], F32, mam)
        cb = sb("cb", [P, XT_TILES], F32, mam)
        nw = sb("nw", [P, INTER // P], F32, mam)
        d_bc = sb("d_bc", [P, MH], F32, mam)
        dtb_bc = sb("dtb_bc", [P, MH], F32, mam)
        alog_bc = sb("alog_bc", [P, MH], F32, mam)
        scale_sb = sb("scale_sb", [P, KC, QG], F32, mam)
        zero_sb = sb("zero_sb", [P, KC, QG], I32, mam)
        packed = sb("packed", [P, KC, DM // 2], I32, mam)
        after_decay = ExitStack()
        digits = sb("digits", [P, KC, DM // 2, 2], I32, after_decay)
        weights = sb("weights", [P, KC, DM], F32, after_decay)
        wT = sb("wT", [P, KC, DM], F32, after_decay)
        after_decay.close()
        decay = sb("decay", [P, MH, P], F32, mam)
        pre = ExitStack()
        bc_acc = sb("bc_acc", [P, 4 * BCC, P], F32, pre)
        bc_act = sb("bc_act", [P, 4 * BCC, P], F32, pre)
        pre.close()
        w_gate_hi = sb("w_gate_hi", [P, KC, 512], F32R, mam)
        w_out_hi = sb("w_out_hi", [P, 2, KC, 512], F32R, mam)
        xnT_hi = sb("xnT_hi", [P, KC, P], F32R, mam)
        xnT_lo = sb("xnT_lo", [P, KC, P], F32R, mam)
        gm = sb("gm", [P, G, P], F32, mam)
        dt_x = sb("dt_x", [P, MH], F32, mam)
        dt_t = sb("dt_t", [P, 4, MH], F32, mam)
        dt = sb("dt", [P, MH], F32, mam)
        a_dt = sb("a_dt", [P, MH], F32, mam)
        x_dt = sb("x_dt", [P, 2, HC, PH], F32, mam)
        x_skip = sb("x_skip", [P, 2, 512], F32, mam)
        gate = sb("gate", [P, 2, 512], F32, mam)
        y = sb("y", [P, 2, 512], F32, mam)
        conv = sb("conv", [P, 2, 4, P], F32, mam)
        hsT = sb("hsT", [P, 2, 4, P], F32, mam)
        pre = ExitStack()
        steps = sb("steps", [P, 2, HC, P], F32, pre)
        pre.close()
        m_t = sb("m_t", [P, 2, HC, P], F32, mam)
        y_gT_hi = sb("y_gT_hi", [P, 4, P], F32R, mam)
        y_gT_lo = sb("y_gT_lo", [P, 4, P], F32R, mam)
        square_sum = sb("square_sum", [P, 2], F32, mam)
        ms = sb("ms", [P, 1], F32, mam)
        ms_eps = sb("ms_eps", [P, 1], F32, mam)
        group_scale = sb("group_scale", [P, 1], F32, mam)
        mam.close()

        bank = [whole.enter_context(nc.psum_tensor(f"bank{i}", [P, 512], F32)) for i in range(8)]
        ring_a = bank[0:4]
        ring_b = bank[4:6]
        pv_bank, oq_bank = bank[6], bank[7]
        dt_bank = bank[1]
        bc_bank = [bank[0], bank[2], bank[3], bank[4]]
        segsum_bank = [bank[5], bank[6], bank[7], bank[1]]

        names = """consts_ready x_in mask_in tables_in bias_in wk_in wv_in wq_in wo_in out_stored
            norm_stats norm_agg norm_eps norm_rstd xn_ready xnT_mm xnT_ready
            qx_hi_ready qx_lo_ready wq_hi_ready wq_lo_ready wo_hi_ready wo_lo_ready attn_hi_ready attn_lo_ready
            ctx_hi_ready ctx_lo_ready wk_hi_ready wk_lo_ready wv_hi_ready wv_lo_ready
            kproj_ready krope_mul krope_add k_hi_ready k_lo_ready
            qproj_ready qrope_mul qrope_add qT_mm qT_hi_ready qT_lo_ready
            vproj_ready v_copied vT_mm v_hi_ready v_lo_ready
            scores_ready scores_masked neg_max_ready probs_ready pT_mm pt_hi_ready pt_lo_ready pv_ready
            inv_sum_ready diag_ready bcast_mm bcast_ready attn_out_ready oproj_ready res_added
            small_in dequant_in dt_in gate_in0 gate_in1 hs_in0 hs_in1 wout_in0 wout_in1
            dt_mm dt_step dt_act neg_a a_dt_ready bc_mm bc_tap bc_conv bc_act_ready steps_even steps_odd segsum_mm decay_ready
            g_mm gm_ready digits_ready digits_off weights_ready wT_mm wT_ready
            hs_mm hs_tap hs_conv hs_act hsT_mm x_ready m_ready gate_mm gate_act y_mm y_sum y_gated square_ready
            xnT_hi_ready xnT_lo_ready gate_hi_ready gate_lo_ready first_gate_lo wout_hi_ready wout_lo_ready
            ygT_mm ygT_hi_ready ygT_lo_ready out_mm ms_sum ms_eps_ready scale_ready out_added
            ffn_mm ffn_bias""".split()
        s = {n: whole.enter_context(nc.semaphore(n)) for n in names}
        ctx_in = [whole.enter_context(nc.semaphore(f"ctx_in{b}")) for b in range(KB)]
        rope_k_in = [whole.enter_context(nc.semaphore(f"rope_k_in{b}")) for b in range(KB)]
        gate_in, hs_in, wout_in = ([s[f"{n}{i}"] for i in range(2)] for n in ("gate_in", "hs_in", "wout_in"))
        tap_chain = whole.enter_context(nc.semaphore("tap_chain"))
        block = whole.enter_context(nc.Block())

        N1 = 1

        @block.sync
        def _(sp):
            sp.dma_start(xres[:, :], x).then_inc(s["x_in"], 16)
            sp.dma_start(wk_raw[:, :, :], wk[0]).then_inc(s["wk_in"], 16)

            def load_context(b):
                sp.dma_start(ctx_raw[:, b, :, :], ctx_t[:, :, b * 512:(b + 1) * 512]).then_inc(ctx_in[b], 16)

            def load_rope_k(b):
                blk = slice(b * 512, (b + 1) * 512)
                sp.dma_start(cos_k[:, blk], rope_k_cos[:, blk]).then_inc(rope_k_in[b], 16)
                sp.dma_start(sin_k[:, blk], rope_k_sin[:, blk]).then_inc(rope_k_in[b], 16)

            load_context(0)
            sp.dma_start(wqo_raw[:, :, :], wq[0]).then_inc(s["wq_in"], 16)
            load_context(1)
            sp.dma_start(cos_q[:, :], rope_q_cos).then_inc(s["tables_in"], 16)
            sp.dma_start(sin_q[:, :], rope_q_sin).then_inc(s["tables_in"], 16)
            load_rope_k(0)
            sp.dma_start(wv_raw[:, :, :], wv[0]).then_inc(s["wv_in"], 16)
            load_context(2)
            load_rope_k(1)
            load_context(3)
            load_rope_k(2)
            load_rope_k(3)
            sp.dma_start(mask_sb[:, :], mask).then_inc(s["mask_in"], 16)
            sp.wait_ge(s["qproj_ready"], 1)
            sp.dma_start(wqo_raw[:, :, :], wq[1]).then_inc(s["wq_in"], 16)
            sp.wait_ge(s["kproj_ready"], KB)
            sp.dma_start(wk_raw[:, :, :], wk[1]).then_inc(s["wk_in"], 16)
            sp.wait_ge(s["vproj_ready"], KB)
            sp.dma_start(wv_raw[:, :, :], wv[1]).then_inc(s["wv_in"], 16)
            with sp.Fori(2, G) as g:
                sp.wait_ge(s["qproj_ready"], g)
                sp.dma_start(wqo_raw[:, :, :], wo[g - 2]).then_inc(s["wo_in"], 16)
                sp.wait_ge(s["kproj_ready"], KB * g)
                sp.dma_start(wk_raw[:, :, :], wk[g]).then_inc(s["wk_in"], 16)
                sp.wait_ge(s["vproj_ready"], KB * g)
                sp.dma_start(wv_raw[:, :, :], wv[g]).then_inc(s["wv_in"], 16)
                sp.wait_ge(s["oproj_ready"], g - 1)
                sp.dma_start(wqo_raw[:, :, :], wq[g]).then_inc(s["wq_in"], 16)
            sp.wait_ge(s["qproj_ready"], G)
            sp.dma_start(wqo_raw[:, :, :], wo[G - 2]).then_inc(s["wo_in"], 16)
            sp.wait_ge(s["oproj_ready"], G - 1)
            sp.dma_start(wqo_raw[:, :, :], wo[G - 1]).then_inc(s["wo_in"], 16)

            sp.wait_ge(s["vproj_ready"], KB * G)
            for i in range(BCC):
                ring, sem = (w_gate_sb, gate_in) if i < 2 else (w_out_sb, wout_in)
                sp.dma_start(ring[:, i % 2, :, :], w_bc[i]).then_inc(sem[i % 2], 16)
            sp.wait_ge(s["res_added"], G)
            sp.dma_start(w_dt_sb[:, :, :], w_dt).then_inc(s["dt_in"], 16)
            for dst, src in ((dtb_bc, dt_bias), (alog_bc, a_log), (d_bc, d_skip)):
                sp.dma_start(dst[:, :], src.partition_broadcast(P)).then_inc(s["small_in"], 16)
            sp.dma_start(cw[:, :, :], conv_w).then_inc(s["small_in"], 16)
            sp.dma_start(cb[:, :], conv_b).then_inc(s["small_in"], 16)
            sp.dma_start(nw[:, :], norm_w).then_inc(s["small_in"], 16)
            sp.dma_start(w_hs_sb[:, 0, :, :], w_hs[0]).then_inc(hs_in[0], 16)
            sp.dma_start(w_hs_sb[:, 1, :, :], w_hs[1]).then_inc(hs_in[1], 16)
            sp.dma_start(bias_bc[:, :], q_bias.partition_broadcast(P)).then_inc(s["bias_in"], 16)
            sp.dma_start(packed[:, :, :], q_packed).then_inc(s["dequant_in"], 16)
            sp.dma_start(scale_sb[:, :, :], q_scale).then_inc(s["dequant_in"], 16)
            sp.dma_start(zero_sb[:, :, :], q_zero).then_inc(s["dequant_in"], 16)
            for i in range(2):
                sp.wait_ge(s["bc_mm"], i + 1)
                sp.dma_start(w_gate_sb[:, i, :, :], w_gate[i]).then_inc(gate_in[i], 16)
            for i in range(2):
                sp.wait_ge(s["bc_mm"], i + 3)
                sp.dma_start(w_out_sb[:, i, :, :], w_out[i]).then_inc(wout_in[i], 16)

            def refill(n, i, hs, gate, out_w):
                c = 2 * n + i
                if hs:
                    sp.wait_ge(s["hs_mm"], c + 2)
                    sp.dma_start(w_hs_sb[:, 1 - i, :, :], w_hs[c + 3]).then_inc(hs_in[1 - i], 16)
                if gate:
                    sp.wait_ge(s["gate_mm"], c + 1)
                    sp.dma_start(w_gate_sb[:, i, :, :], w_gate[c + 2]).then_inc(gate_in[i], 16)
                if out_w:
                    sp.wait_ge(s["out_mm"], c)
                    sp.dma_start(w_out_sb[:, 1 - i, :, :], w_out[c + 1]).then_inc(wout_in[1 - i], 16)

            sp.wait_ge(s["hs_mm"], 1)
            sp.dma_start(w_hs_sb[:, 0, :, :], w_hs[2]).then_inc(hs_in[0], 16)
            refill(0, 0, True, True, False)
            refill(0, 1, True, True, True)
            with sp.Fori(1, CH // 2 - 2) as n:
                refill(n, 0, True, True, True)
                refill(n, 1, True, True, True)
            refill(CH // 2 - 2, 0, True, True, True)
            refill(CH // 2 - 2, 1, False, True, True)
            refill(CH // 2 - 1, 0, False, False, True)

            sp.wait_ge(s["ffn_bias"], 2)
            sp.dma_start(out, xres[:, :]).then_inc(s["out_stored"], 16)
            sp.wait_ge(s["out_stored"], 16)

        @block.tensor
        def _(pe):
            def pairs(dst, left_hi, left_lo, right_hi, right_lo, first, last):
                pe.matmul(dst, left_hi, right_hi, start=first, stop=False)
                pe.matmul(dst, left_hi, right_lo, start=False, stop=False)
                return pe.matmul(dst, left_lo, right_hi, start=False, stop=last)

            def transpose_norm(n):
                pe.wait_ge(s["xn_ready"], n)
                for c in range(KC):
                    last = pe.transpose(oq_bank[:, c * P:(c + 1) * P], xn[:, c * P:(c + 1) * P], ident[:, :])
                last.then_inc(s["xnT_mm"], 1)

            def first_head(g):
                return isinstance(g, int) and g == 0

            def project_k_block(g, b):
                if b == 0:
                    pe.wait_ge(s["wk_lo_ready"], g + 1)
                if first_head(g):
                    pe.wait_ge(s["ctx_lo_ready"], b + 1)
                else:
                    pe.wait_ge(s["scores_masked"], HG * KB * g - KB + b + 1)
                for c in range(KC):
                    last = pairs(ring_a[b][:, :], wk_hi[:, c, :], wk_lo[:, c, :],
                                 ctx_hi[:, c, b * 512:(b + 1) * 512], ctx_lo[:, c, b * 512:(b + 1) * 512],
                                 c == 0, c == KC - 1)
                last.then_inc(s["kproj_ready"], 1)

            def project_q(g):
                pe.wait_ge(s["wq_lo_ready"], g + 1)
                if first_head(g):
                    pe.wait_ge(s["qx_lo_ready"], 1)
                for c in range(KC):
                    last = pairs(oq_bank[:, :], qx_hi[:, c, :], qx_lo[:, c, :], wqo_hi[:, c, :], wqo_lo[:, c, :],
                                 c == 0, c == KC - 1)
                last.then_inc(s["qproj_ready"], 1)

            def transpose_q(g):
                pe.wait_ge(s["qrope_add"], g + 1)
                if not first_head(g):
                    pe.wait_ge(s["v_lo_ready"], KB * g - 1)
                for h in range(HG):
                    last = pe.transpose(ring_b[0][:, h * P:(h + 1) * P], rope_a[:, 0, h * P:(h + 1) * P], ident[:, :])
                last.then_inc(s["qT_mm"], 1)

            def project_qk_and_first_v(g):
                project_k_block(g, 0)
                project_q(g)
                project_k_block(g, 1)
                transpose_q(g)
                project_k_block(g, 2)
                project_k_block(g, 3)
                project_v_block(g, 0)

            def project_v_block(g, b):
                if b == 0:
                    pe.wait_ge(s["wv_lo_ready"], g + 1)
                pe.wait_ge(s["krope_mul"], KB * g + b + 1)
                for c in range(KC):
                    last = pairs(ring_a[b][:, :], wv_hi[:, c, :], wv_lo[:, c, :],
                                 ctx_hi[:, c, b * 512:(b + 1) * 512], ctx_lo[:, c, b * 512:(b + 1) * 512],
                                 c == 0, c == KC - 1)
                last.then_inc(s["vproj_ready"], 1)

            def transpose_v_block(g, b):
                pe.wait_ge(s["v_copied"], KB * g + b + 1)
                if b == 0:
                    if first_head(g):
                        pe.wait_ge(s["qT_lo_ready"], 1)
                    else:
                        pe.wait_ge(s["pt_lo_ready"], KT * g)
                if b >= 2:
                    pe.wait_ge(s["v_lo_ready"], KB * g + b - 1)
                for t in range(4):
                    last = pe.transpose(ring_b[b % 2][:, t * P:(t + 1) * P], rope_b[:, b % 2, t * P:(t + 1) * P],
                                        ident[:, :])
                last.then_inc(s["vT_mm"], 1)

            def scores(g):
                pe.wait_ge(s["qT_lo_ready"], g + 1)
                for h in range(HG):
                    for b in range(KB):
                        j = KB * h + b
                        if h == 0:
                            pe.wait_ge(s["k_lo_ready"], KB * g + b + 1)
                            pe.wait_ge(s["v_copied"], KB * g + b + 1)
                        else:
                            pe.wait_ge(s["scores_masked"], HG * KB * g + j - KB + 1)
                        pairs(ring_a[b][:, :], qT_hi[:, h, :], qT_lo[:, h, :], k_hi[:, b * 512:(b + 1) * 512],
                              k_lo[:, b * 512:(b + 1) * 512], True, True).then_inc(s["scores_ready"], 1)
                    if h == 0:
                        transpose_v_block(g, KB - 1)

            def transpose_probs(g, t):
                if t == 0:
                    pe.wait_ge(s["probs_ready"], HG * (g + 1))
                    pe.wait_ge(s["v_lo_ready"], KB * (g + 1))
                elif t >= 2:
                    pe.wait_ge(s["pt_lo_ready"], KT * g + t - 1)
                for h in range(HG):
                    last = pe.transpose(ring_b[(t + 1) % 2][:, h * P:(h + 1) * P], probs[:, h, t * P:(t + 1) * P],
                                        ident[:, :])
                last.then_inc(s["pT_mm"], 1)

            def attend(g, last_head):
                for t in range(KT + 2):
                    if t == 1 and not last_head:
                        pe.wait_ge(s["qT_lo_ready"], g + 2)
                    if t == 2 and not last_head:
                        project_v_block(g + 1, 1)
                    if t < KT:
                        transpose_probs(g, t)
                    if t == 4:
                        pe.wait_ge(s["diag_ready"], g + 1)
                        pe.matmul(oq_bank[:, :], ones[:, :], rope_a[:, 0, :], start=True, stop=True)\
                            .then_inc(s["bcast_mm"], 1)
                    if t == KT + 1 and not last_head:
                        project_v_block(g + 1, 2)
                    if t >= 2:
                        j = t - 2
                        pe.wait_ge(s["pt_lo_ready"], KT * g + j + 1)
                        last = pairs(pv_bank[:, :], v_hi[:, j, :], v_lo[:, j, :], pt_hi[j % 3], pt_lo[j % 3],
                                     j == 0, j == KT - 1)
                last.then_inc(s["pv_ready"], 1)

            def project_out(g):
                pe.wait_ge(s["wo_lo_ready"], g + 1)
                pe.wait_ge(s["attn_lo_ready"], g + 1)
                for h in range(HG):
                    last = pairs(oq_bank[:, :], attn_hi[:, h, :], attn_lo[:, h, :], wqo_hi[:, h, :], wqo_lo[:, h, :],
                                 h == 0, h == HG - 1)
                last.then_inc(s["oproj_ready"], 1)

            pe.wait_ge(s["consts_ready"], 4)
            transpose_norm(1)
            project_k_block(0, 0)
            project_q(0)
            project_k_block(0, 1)
            transpose_q(0)
            project_v_block(0, 0)
            project_k_block(0, 2)
            project_v_block(0, 1)
            project_k_block(0, 3)
            project_v_block(0, 2)
            project_v_block(0, 3)
            transpose_v_block(0, 0)
            transpose_v_block(0, 1)
            transpose_v_block(0, 2)
            with pe.Fori(0, G - 1) as g:
                scores(g)
                project_qk_and_first_v(g + 1)
                attend(g, False)
                transpose_v_block(g + 1, 0)
                project_v_block(g + 1, 3)
                transpose_v_block(g + 1, 1)
                project_out(g)
                transpose_v_block(g + 1, 2)
            scores(G - 1)
            attend(G - 1, True)
            project_out(G - 1)

            transpose_norm(2)
            pe.wait_ge(s["xnT_ready"], 1)
            pe.wait_ge(s["dt_in"], 16)
            for c in range(KC):
                last = pe.matmul(dt_bank[:, 0:MH], xnT[:, c, :], w_dt_sb[:, c, :], start=c == 0, stop=c == KC - 1)
            last.then_inc(s["dt_mm"], 1)

            def project_transposed(dst, w, done):
                for t in range(4):
                    for c in range(KC):
                        last = pe.matmul(dst[:, t * P:(t + 1) * P], w[:, c, t * P:(t + 1) * P], xnT[:, c, :],
                                         start=c == 0, stop=c == KC - 1)
                last.then_inc(done, 1)

            for i in range(BCC):
                ring, sem = (w_gate_sb, gate_in) if i < 2 else (w_out_sb, wout_in)
                pe.wait_ge(sem[i % 2], 16)
                project_transposed(bc_bank[i], ring[:, i % 2, :, :], s["bc_mm"])

            def segment_sums(n):
                for i in range(2):
                    if i == 0:
                        pe.wait_ge(s["steps_even"], n + 1)
                    if i == 1:
                        pe.wait_ge(s["dt_step"], 1)
                    at_least(pe, s["decay_ready"], 2 * n + i - 1)
                    for j in range(2):
                        if i == 1:
                            pe.wait_ge(s["steps_odd"], 2 * n + j + 1)
                        dst = segsum_bank[2 * i + j]
                        last = pe.matmul(dst[:, :], below[:, :],
                                         steps[:, i, 4 * j:4 * j + 4, :].rearrange("p h l -> p (h l)"),
                                         start=True, stop=True)
                    last.then_inc(s["segsum_mm"], 1)

            segment_sums(0)
            with pe.Fori(1, CH // 2) as n:
                segment_sums(n)

            def hs_step(n, i):
                pe.wait_ge(hs_in[i], 16 * n + 16)
                if not (isinstance(n, int) and n == 0):
                    pe.wait_ge(s["hs_conv"], 12 * (2 * n + i - 1))
                project_transposed(bank[i], w_hs_sb[:, i, :, :], s["hs_mm"])

            def out_step(n, i):
                pe.wait_ge(s["wout_lo_ready"], 2 * n + i + 1)
                pe.wait_ge(s["ygT_lo_ready"], 4 * (2 * n + i + 1))
                if i == 0:
                    at_least(pe, s["out_added"], n)
                for t in range(4):
                    last = pairs(bank[6][:, :], y_gT_hi[:, t, :], y_gT_lo[:, t, :], w_out_hi[:, i, t, :],
                                 w_out_lo[:, i, t, :], i == 0 and t == 0, i == 1 and t == 3)
                last.then_inc(s["out_mm"], 1)

            def chunk_step(n, i, first, last_chunk):
                c = 2 * n + i
                if not first and not last_chunk:
                    hs_step(n + i, 1 - i)
                pe.wait_ge(s["hs_act"], c + 1)
                at_least(pe, s["x_ready"], c)
                for t in range(4):
                    last = pe.transpose(bank[3][:, t * P:(t + 1) * P], hsT[:, i, t, :], ident[:, :])
                last.then_inc(s["hsT_mm"], 1)
                if first:
                    pe.wait_ge(s["first_gate_lo"], 2)
                else:
                    pe.wait_ge(s["gate_lo_ready"], c)
                at_least(pe, s["gate_act"], c)
                for k in range(KC):
                    last = pairs(bank[2][:, :], xnT_hi[:, k, :], xnT_lo[:, k, :], w_gate_hi[:, k, :],
                                 w_gate_lo[:, i, k, :], k == 0, k == KC - 1)
                last.then_inc(s["gate_mm"], 1)
                pe.wait_ge(s["x_ready"], c + 1)
                pe.wait_ge(s["m_ready"], c + 1)
                at_least(pe, s["y_sum"], c)
                for h in range(HC):
                    last = pe.matmul(bank[4][:, h * PH:(h + 1) * PH], m_t[:, i, h, :], x_dt[:, i, h, :],
                                     start=True, stop=True)
                last.then_inc(s["y_mm"], 1)
                if not first:
                    out_step(n + i - 1, 1 - i)
                pe.wait_ge(s["y_gated"], c + 1)
                if not (isinstance(n, int) and n == 0 and i == 0):
                    pe.wait_ge(s["ygT_lo_ready"], 4 * c)
                for t in range(4):
                    last = pe.transpose(bank[5][:, t * P:(t + 1) * P], y[:, i, t * P:(t + 1) * P], ident[:, :])
                last.then_inc(s["ygT_mm"], 1)

            pe.wait_ge(s["bc_tap"], 4)
            pe.wait_ge(s["bc_conv"], 4)
            hs_step(0, 0)
            pe.wait_ge(s["decay_ready"], CH)
            hs_step(0, 1)
            pe.wait_ge(s["bc_act_ready"], BCC)
            pe.wait_ge(s["decay_ready"], CH)
            for g in range(G):
                last = pe.matmul(bank[5 + g // 4][:, (g % 4) * P:(g % 4 + 1) * P], bc_act[:, g, :], bc_act[:, 8 + g, :],
                                 start=True, stop=True)
            last.then_inc(s["g_mm"], 1)

            pe.wait_ge(s["gm_ready"], 2)
            chunk_step(0, 0, True, False)
            chunk_step(0, 1, False, False)
            with pe.Fori(1, CH // 2 - 1) as n:
                chunk_step(n, 0, False, False)
                chunk_step(n, 1, False, False)
            chunk_step(CH // 2 - 1, 0, False, False)
            chunk_step(CH // 2 - 1, 1, False, True)
            out_step(CH // 2 - 1, 1)

            pe.wait_ge(s["weights_ready"], 1)
            for c in range(KC):
                for o in range(KC):
                    last = pe.transpose(bank[c][:, o * P:(o + 1) * P], weights[:, o, c * P:(c + 1) * P],
                                        ident[:, :])
                last.then_inc(s["wT_mm"], 1)
            transpose_norm(3)
            pe.wait_ge(s["xnT_ready"], 2)
            pe.wait_ge(s["wT_ready"], KC)
            for c in range(KC):
                last = pe.matmul(bank[4][:, :], xnT[:, c, :], wT[:, c, :], start=c == 0, stop=c == KC - 1)
            last.then_inc(s["ffn_mm"], 1)

        @block.scalar
        def _(act):
            act.wait_ge(s["xnT_mm"], 1)
            act.activation(qx_hi[:, :, :].rearrange("p c t -> p (c t)"), oq_bank[:, :], ACT.Copy)\
                .then_inc(s["qx_hi_ready"], 1)

            def wq_high(g):
                act.wait_ge(s["wq_in"], 16 * (g + 1))
                act.activation(wqo_hi[:, :, :], wqo_raw[:, :, :], ACT.Copy).then_inc(s["wq_hi_ready"], 1)

            def wo_high(g):
                act.wait_ge(s["wo_in"], 16 * (g + 1))
                act.activation(wqo_hi[:, :, :], wqo_raw[:, :, :], ACT.Copy).then_inc(s["wo_hi_ready"], 1)

            def attn_high(g):
                act.wait_ge(s["attn_out_ready"], g + 1)
                act.activation(attn_hi[:, :, :].rearrange("p h t -> p (h t)"), probs[:, 1, 0:512], ACT.Copy)\
                    .then_inc(s["attn_hi_ready"], 1)

            def q_high(g):
                act.wait_ge(s["qT_mm"], g + 1)
                act.activation(qT_hi[:, :, :].rearrange("p h t -> p (h t)"), ring_b[0][:, :], ACT.Copy)\
                    .then_inc(s["qT_hi_ready"], 1)

            def k_high(g, b):
                act.wait_ge(s["krope_add"], KB * g + b + 1)
                act.activation(k_hi[:, b * 512:(b + 1) * 512], rope_a[:, (b + 1) % 2, :], ACT.Copy)\
                    .then_inc(s["k_hi_ready"], 1)

            def q_and_k_high(g):
                k_high(g, 0)
                q_high(g)
                k_high(g, 1)
                wo_high(g - 1)
                k_high(g, 2)
                k_high(g, 3)

            def v_copy(g, b):
                act.wait_ge(s["vproj_ready"], KB * g + max(b, 2 * (b % 2)) + 1)
                act.wait_ge(s["krope_add"], KB * g + KB)
                if b >= 2:
                    act.wait_ge(s["vT_mm"], KB * g + b - 1)
                act.activation(rope_b[:, b % 2, :], ring_a[b][:, :], ACT.Copy).then_inc(s["v_copied"], 1)

            def v_high(g, b):
                act.wait_ge(s["vT_mm"], KB * g + b + 1)
                act.activation(v_hi[:, 4 * b:4 * b + 4, :].rearrange("p t d -> p (t d)"), ring_b[b % 2][:, :],
                               ACT.Copy).then_inc(s["v_hi_ready"], 1)

            def v_rest(g):
                for b in range(KB - 1):
                    v_high(g, b)
                    if b == 0 and not (isinstance(g, int) and g == 0):
                        attn_high(g - 1)
                    if b + 2 < KB:
                        v_copy(g, b + 2)

            def exps(g):
                for h in range(HG):
                    act.wait_ge(s["neg_max_ready"], HG * g + h + 1)
                    act.activation(probs[:, h, :], probs[:, h, :], ACT.Exp, bias=neg_max[:, h:h + 1],
                                   accum_out=row_sum[:, h:h + 1]).then_inc(s["probs_ready"], 1)

            def pt_high(g, last_head):
                for t in range(KT):
                    if t == 2:
                        act.wait_ge(s["k_lo_ready"], KB * (g + (1 if last_head else 2)))
                    act.wait_ge(s["pT_mm"], KT * g + t + 1)
                    act.activation(pt_hi[t % 3], ring_b[(t + 1) % 2][:, :], ACT.Copy).then_inc(s["pt_hi_ready"], 1)
                    if t == 5:
                        act.wait_ge(s["bcast_mm"], g + 1)
                        act.activation(probs[:, 2, 0:512], oq_bank[:, :], ACT.Copy).then_inc(s["bcast_ready"], 1)
                if not last_head:
                    v_copy(g + 1, 1)

            def ctx_high(b):
                act.wait_ge(ctx_in[b], 16)
                act.activation(ctx_hi[:, :, b * 512:(b + 1) * 512], ctx_raw[:, b, :, :], ACT.Copy)\
                    .then_inc(s["ctx_hi_ready"], 1)

            ctx_high(0)
            wq_high(0)
            ctx_high(1)
            ctx_high(2)
            k_high(0, 0)
            q_high(0)
            ctx_high(3)
            k_high(0, 1)
            k_high(0, 2)
            k_high(0, 3)
            v_copy(0, 0)
            v_copy(0, 1)
            v_rest(0)
            with act.Fori(0, G - 1) as g:
                v_high(g, KB - 1)
                wq_high(g + 1)
                exps(g)
                q_and_k_high(g + 1)
                v_copy(g + 1, 0)
                pt_high(g, False)
                v_rest(g + 1)
            v_high(G - 1, KB - 1)
            wo_high(G - 1)
            exps(G - 1)
            pt_high(G - 1, True)
            attn_high(G - 1)

            act.wait_ge(s["xnT_mm"], 2)
            act.activation(xnT[:, :, :].rearrange("p c t -> p (c t)"), oq_bank[:, :], ACT.Copy).then_inc(s["xnT_ready"], 1)
            act.wait_ge(s["xnT_ready"], 1)
            act.activation(xnT_hi[:, :, :], xnT[:, :, :], ACT.Copy).then_inc(s["xnT_hi_ready"], 1)
            act.wait_ge(s["small_in"], 96)
            act.activation(alog_bc[:, :], alog_bc[:, :], ACT.Exp).then_inc(s["neg_a"], 1)
            act.wait_ge(s["dt_step"], 2)
            act.activation(dt_t[:, 1, :], dt_t[:, 0, :], ACT.Exp).then_inc(s["dt_act"], 1)
            act.wait_ge(s["dt_act"], 1)
            act.activation(dt_t[:, 2, :], dt_t[:, 1, :], ACT.Ln, bias=1.0).then_inc(s["dt_act"], 1)
            for i in range(BCC):
                act.wait_ge(s["bc_mm"], i + 1)
                for t in range(4):
                    tile = 4 * i + t
                    act.activation(bc_acc[:, tile, :], bc_bank[i][:, t * P:(t + 1) * P], ACT.Identity,
                                   bias=cb[:, INTER // P + tile:INTER // P + tile + 1],
                                   scale=cw[:, INTER // P + tile, 3:4]).then_inc(s["bc_tap"], 1)

            def decays(n):
                for i in range(2):
                    act.wait_ge(s["segsum_mm"], 2 * n + i + 1)
                    for j in range(2):
                        last = act.activation(
                            decay[:, bass.ds(16 * n + 8 * i + 4 * j, 4), :].rearrange("p h l -> p (h l)"),
                            segsum_bank[2 * i + j][:, :], ACT.Exp)
                    last.then_inc(s["decay_ready"], 1)

            decays(0)
            with act.Fori(1, CH // 2) as n:
                decays(n)
            for i in range(BCC):
                act.wait_ge(s["bc_conv"], 4 * (i + 1))
                act.activation(bc_act[:, 4 * i:4 * i + 4, :].rearrange("p t l -> p (t l)"),
                               bc_acc[:, 4 * i:4 * i + 4, :].rearrange("p t l -> p (t l)"), ACT.Silu)\
                    .then_inc(s["bc_act_ready"], 1)

            def gate_high(n, i):
                act.wait_ge(gate_in[i], 16 * n + 32)
                act.activation(w_gate_hi[:, :, :], w_gate_sb[:, i, :, :], ACT.Copy).then_inc(s["gate_hi_ready"], 1)

            def out_high(n, i):
                act.wait_ge(wout_in[i], 16 * n + 32)
                if isinstance(n, int) and n == 0:
                    if i == 0:
                        act.wait_ge(s["g_mm"], 1)
                else:
                    act.wait_ge(s["out_mm"], 2 * n + i - 1)
                act.activation(w_out_hi[:, i, :, :], w_out_sb[:, i, :, :], ACT.Copy).then_inc(s["wout_hi_ready"], 1)

            def tap_step(n, i):
                c = 2 * n + i
                act.wait_ge(s["hs_mm"], c + 1)
                if not (isinstance(n, int) and n == 0):
                    act.wait_ge(s["hs_act"], c - 1)
                for t in range(4):
                    act.activation(conv[:, i, t, :], bank[i][:, t * P:(t + 1) * P], ACT.Identity,
                                   bias=cb[:, bass.ds(4 * c + t, 1)],
                                   scale=cw[:, bass.ds(4 * c + t, 1), 3:4].rearrange("p a b -> p (a b)"))\
                        .then_inc(s["hs_tap"], 1)

            def silu_step(n, i):
                c = 2 * n + i
                act.wait_ge(s["hs_conv"], 12 * (c + 1))
                if not (isinstance(n, int) and n == 0):
                    act.wait_ge(s["hsT_mm"], c - 1)
                act.activation(hsT[:, i, :, :].rearrange("p t l -> p (t l)"),
                               conv[:, i, :, :].rearrange("p t l -> p (t l)"), ACT.Silu).then_inc(s["hs_act"], 1)

            def chunk_act(n, i, last_chunk):
                c = 2 * n + i
                if not last_chunk:
                    tap_step(n + i, 1 - i)
                act.wait_ge(s["gate_mm"], c + 1)
                if not (isinstance(n, int) and n == 0):
                    act.wait_ge(s["y_gated"], c - 1)
                act.activation(gate[:, i, :], bank[2][:, :], ACT.Silu).then_inc(s["gate_act"], 1)
                if not last_chunk:
                    gate_high(n + i, 1 - i)
                    silu_step(n + i, 1 - i)
                out_high(n, i)
                act.wait_ge(s["y_gated"], c + 1)
                if i == 0:
                    at_least(act, s["ms_sum"], n)
                if not (isinstance(n, int) and n == 0 and i == 0):
                    act.wait_ge(s["square_ready"], c)
                act.activation(bank[7][:, :], y[:, i, :], ACT.Square, accum_out=square_sum[:, i:i + 1])\
                    .then_inc(s["square_ready"], 1)
                act.wait_ge(s["ygT_mm"], c + 1)
                at_least(act, s["out_mm"], c)
                for t in range(4):
                    act.activation(y_gT_hi[:, t, :], bank[5][:, t * P:(t + 1) * P], ACT.Identity,
                                   scale=nw[:, bass.ds(4 * c + t, 1)]).then_inc(s["ygT_hi_ready"], 1)

            tap_step(0, 0)
            act.wait_ge(s["bc_act_ready"], BCC)
            gate_high(0, 0)
            silu_step(0, 0)
            chunk_act(0, 0, False)
            chunk_act(0, 1, False)
            with act.Fori(1, CH // 2 - 1) as n:
                chunk_act(n, 0, False)
                chunk_act(n, 1, False)
            chunk_act(CH // 2 - 1, 0, False)
            chunk_act(CH // 2 - 1, 1, True)

            for c in range(KC):
                act.wait_ge(s["wT_mm"], c + 1)
                act.activation(wT[:, c, :], bank[c][:, :], ACT.Copy).then_inc(s["wT_ready"], 1)
            act.wait_ge(s["xnT_mm"], 3)
            act.activation(xnT[:, :, :].rearrange("p c t -> p (c t)"), oq_bank[:, :], ACT.Copy).then_inc(s["xnT_ready"], 1)

        @block.vector
        def _(dve):
            def layer_norm(n):
                dve.bn_stats(stats[:, :], xres[:, :]).then_inc(s["norm_stats"], 1)
                dve.wait_ge(s["norm_stats"], n)
                dve.bn_aggr(mean_var[:, :], stats[:, :]).then_inc(s["norm_agg"], 1)
                dve.wait_ge(s["norm_rstd"], n)
                dve.tensor_scalar(xn[:, :], xres[:, :], mean_var[:, 0:1], rstd[:, 0:1], ALU.subtract, ALU.mult)\
                    .then_inc(s["xn_ready"], 1)

            def k_rotate(g, b):
                blk, slot = slice(b * 512, (b + 1) * 512), (b + 1) % 2
                dve.wait_ge(s["kproj_ready"], KB * g + b + 1)
                if b == 0 and not (isinstance(g, int) and g == 0):
                    dve.wait_ge(s["k_lo_ready"], KB * g)
                    dve.wait_ge(s["vT_mm"], KB * g)
                if b == 1:
                    dve.wait_ge(s["qT_mm"], g + 1)
                if b >= 2:
                    dve.wait_ge(s["k_lo_ready"], KB * g + b - 1)
                dve.tensor_tensor(rope_a[:, slot, :], ring_a[b][:, :], cos_k[:, blk], ALU.mult)
                dve.tensor_tensor(rope_b[0:64, slot, :], ring_a[b][64:128, :], sin_k[64:128, blk], ALU.mult)
                dve.tensor_tensor(rope_b[64:128, slot, :], ring_a[b][0:64, :], sin_k[0:64, blk], ALU.mult)\
                    .then_inc(s["krope_mul"], 1)
                dve.wait_ge(s["krope_mul"], KB * g + b + 1)
                dve.tensor_tensor(rope_a[:, slot, :], rope_a[:, slot, :], rope_b[:, slot, :], ALU.add)\
                    .then_inc(s["krope_add"], 1)

            def q_rotate(g):
                dve.wait_ge(s["qproj_ready"], g + 1)
                q = oq_bank[:, :].rearrange("p (h two d) -> p h two d", h=HG, two=2)
                qb = rope_b[:, 0, :].rearrange("p (h two d) -> p h two d", h=HG, two=2)
                cos = cos_q[:, :].unsqueeze(1).broadcast_to([P, 2 * HG, DH // 2])
                sin = sin_q[:, :].unsqueeze(1).broadcast_to([P, HG, DH // 2])
                dve.tensor_tensor(rope_a[:, 0, :].rearrange("p (h d) -> p h d", d=DH // 2),
                                  oq_bank[:, :].rearrange("p (h d) -> p h d", d=DH // 2), cos, ALU.mult)
                dve.scalar_tensor_tensor(qb[:, :, 0, :], q[:, :, 1, :], -1.0, sin, ALU.mult, ALU.mult)
                dve.tensor_tensor(qb[:, :, 1, :], q[:, :, 0, :], sin, ALU.mult).then_inc(s["qrope_mul"], 1)
                dve.wait_ge(s["qrope_mul"], g + 1)
                dve.tensor_tensor(rope_a[:, 0, :], rope_a[:, 0, :], rope_b[:, 0, :], ALU.add).then_inc(s["qrope_add"], 1)

            def q_low(g):
                dve.wait_ge(s["qT_hi_ready"], g + 1)
                dve.tensor_tensor(qT_lo[:, :, :].rearrange("p h t -> p (h t)"), ring_b[0][:, :],
                                  qT_hi[:, :, :].rearrange("p h t -> p (h t)").bitcast(F32), ALU.subtract)\
                    .then_inc(s["qT_lo_ready"], 1)

            def q_and_k(g):
                k_rotate(g, 0)
                q_rotate(g)
                k_rotate(g, 1)
                q_low(g)
                k_rotate(g, 2)
                k_rotate(g, 3)

            def v_low(g, b):
                dve.wait_ge(s["v_hi_ready"], KB * g + b + 1)
                dve.tensor_tensor(v_lo[:, 4 * b:4 * b + 4, :].rearrange("p t d -> p (t d)"), ring_b[b % 2][:, :],
                                  v_hi[:, 4 * b:4 * b + 4, :].rearrange("p t d -> p (t d)").bitcast(F32),
                                  ALU.subtract).then_inc(s["v_lo_ready"], 1)

            def row_max(g, h):
                dve.wait_ge(s["scores_masked"], HG * KB * g + KB * (h + 1))
                dve.tensor_reduce(neg_max[:, h:h + 1], block_max[:, h, :], X_AXIS, ALU.max, negate=True)\
                    .then_inc(s["neg_max_ready"], 1)

            def mask_scores(g):
                for h in range(HG):
                    for b in range(KB):
                        dve.wait_ge(s["mask_in"], 16)
                        dve.wait_ge(s["scores_ready"], HG * KB * g + KB * h + b + 1)
                        keep_wait_apart(dve)
                        dve.tensor_tensor_reduce(
                            out=probs[:, h, b * 512:(b + 1) * 512], in0=ring_a[b][:, :],
                            in1=mask_sb[:, b * 512:(b + 1) * 512], scale=1.0, scalar=LOWEST, op0=ALU.add, op1=ALU.max,
                            accum_out=block_max[:, h, b:b + 1]).then_inc(s["scores_masked"], 1)
                        if b == 0 and h > 0:
                            row_max(g, h - 1)
                    if h == 0:
                        v_low(g, KB - 1)
                row_max(g, HG - 1)

            def inverse_sums(g, last_head):
                dve.wait_ge(s["probs_ready"], HG * (g + 1))
                dve.reciprocal(inv_sum[:, :], row_sum[:, :]).then_inc(s["inv_sum_ready"], 1)
                dve.wait_ge(s["inv_sum_ready"], g + 1)
                dve.wait_ge(s["k_lo_ready"], KB * (g + (1 if last_head else 2)))
                dve.tensor_tensor(rope_a[:, 0, :].rearrange("p (h t) -> p h t", h=HG),
                                  ident[:, :].unsqueeze(1).broadcast_to([P, HG, P]),
                                  inv_sum[:, :].unsqueeze(2).broadcast_to([P, HG, P]), ALU.mult)\
                    .then_inc(s["diag_ready"], 1)

            def pt_low(g, last_head):
                for t in range(KT):
                    dve.wait_ge(s["pt_hi_ready"], KT * g + t + 1)
                    dve.tensor_tensor(pt_lo[t % 3], ring_b[(t + 1) % 2][:, :], pt_hi[t % 3].bitcast(F32), ALU.subtract)\
                        .then_inc(s["pt_lo_ready"], 1)
                    if t == 1:
                        inverse_sums(g, last_head)

            def scale_out(g):
                dve.wait_ge(s["bcast_ready"], g + 1)
                dve.wait_ge(s["pv_ready"], g + 1)
                dve.tensor_tensor(probs[:, 1, 0:512], pv_bank[:, :], probs[:, 2, 0:512], ALU.mult)\
                    .then_inc(s["attn_out_ready"], 1)

            def add_out(g):
                dve.wait_ge(s["oproj_ready"], g + 1)
                dve.tensor_tensor(xres[:, :], xres[:, :], oq_bank[:, :], ALU.add).then_inc(s["res_added"], 1)
                dve.wait_ge(s["res_added"], g + 1)

            def attn_low(g):
                dve.wait_ge(s["attn_hi_ready"], g + 1)
                dve.tensor_tensor(attn_lo[:, :, :].rearrange("p h t -> p (h t)"), probs[:, 1, 0:512],
                                  attn_hi[:, :, :].rearrange("p h t -> p (h t)").bitcast(F32), ALU.subtract)\
                    .then_inc(s["attn_lo_ready"], 1)

            dve.wait_ge(s["x_in"], 16)
            layer_norm(1)
            dve.wait_ge(s["qx_hi_ready"], 1)
            dve.tensor_tensor(qx_lo[:, :, :].rearrange("p c t -> p (c t)"), oq_bank[:, :],
                              qx_hi[:, :, :].rearrange("p c t -> p (c t)").bitcast(F32), ALU.subtract)\
                .then_inc(s["qx_lo_ready"], 1)
            def ctx_low(b):
                dve.wait_ge(s["ctx_hi_ready"], b + 1)
                dve.tensor_tensor(ctx_lo[:, :, b * 512:(b + 1) * 512], ctx_raw[:, b, :, :],
                                  ctx_hi[:, :, b * 512:(b + 1) * 512].bitcast(F32), ALU.subtract)\
                    .then_inc(s["ctx_lo_ready"], 1)

            def first_k_rotate(b):
                dve.wait_ge(rope_k_in[b], 32)
                k_rotate(0, b)

            ctx_low(0)
            dve.wait_ge(s["wq_hi_ready"], 1)
            dve.tensor_tensor(wqo_lo[:, :, :], wqo_raw[:, :, :], wqo_hi[:, :, :].bitcast(F32), ALU.subtract)\
                .then_inc(s["wq_lo_ready"], 1)
            ctx_low(1)
            first_k_rotate(0)
            dve.wait_ge(s["tables_in"], 32)
            q_rotate(0)
            ctx_low(2)
            first_k_rotate(1)
            q_low(0)
            ctx_low(3)
            first_k_rotate(2)
            first_k_rotate(3)
            for b in range(KB - 1):
                v_low(0, b)
            with dve.Fori(0, G - 1) as g:
                mask_scores(g)
                q_and_k(g + 1)
                pt_low(g, False)
                scale_out(g)
                v_low(g + 1, 0)
                attn_low(g)
                v_low(g + 1, 1)
                add_out(g)
                v_low(g + 1, 2)
            mask_scores(G - 1)
            pt_low(G - 1, True)
            scale_out(G - 1)
            attn_low(G - 1)
            add_out(G - 1)

            layer_norm(2)
            dve.wait_ge(s["small_in"], 96)
            dve.wait_ge(s["dt_mm"], 1)
            dve.tensor_tensor(dt_x[:, :], dt_bank[:, 0:MH], dtb_bc[:, :], ALU.add).then_inc(s["dt_step"], 1)
            dve.wait_ge(s["dt_step"], 1)
            dve.scalar_tensor_tensor(dt_t[:, 0, :], dt_x[:, :], -1.0, dt_x[:, :], ALU.mult, ALU.min)\
                .then_inc(s["dt_step"], 1)
            dve.wait_ge(s["xnT_hi_ready"], 1)
            dve.tensor_tensor(xnT_lo[:, :, :], xnT[:, :, :], xnT_hi[:, :, :].bitcast(F32), ALU.subtract)\
                .then_inc(s["xnT_lo_ready"], 1)
            dve.wait_ge(s["dt_act"], 1)
            dve.tensor_scalar(dt[:, :], dt_t[:, 1, :], 1.0, -1.0, ALU.add, ALU.add).then_inc(s["dt_step"], 1)
            dve.wait_ge(s["dt_step"], 3)
            dve.tensor_scalar(dt_t[:, 3, :], dt[:, :], 0.0, None, ALU.is_equal).then_inc(s["dt_step"], 1)
            dve.wait_ge(s["dt_step"], 4)
            dve.tensor_tensor(dt[:, :], dt[:, :], dt_t[:, 3, :], ALU.add).then_inc(s["dt_step"], 1)
            dve.wait_ge(s["dt_step"], 5)
            dve.reciprocal(dt[:, :], dt[:, :]).then_inc(s["dt_step"], 1)
            dve.wait_ge(s["dt_step"], 6)
            dve.wait_ge(s["dt_act"], 2)
            dve.tensor_tensor(dt_t[:, 2, :], dt_t[:, 2, :], dt[:, :], ALU.mult).then_inc(s["dt_step"], 1)
            dve.wait_ge(s["dt_step"], 7)
            dve.tensor_tensor(dt_t[:, 2, :], dt_t[:, 2, :], dt_t[:, 3, :], ALU.add).then_inc(s["dt_step"], 1)
            dve.wait_ge(s["dt_step"], 8)
            dve.tensor_tensor(dt_t[:, 2, :], dt_t[:, 2, :], dt_t[:, 1, :], ALU.mult).then_inc(s["dt_step"], 1)
            dve.wait_ge(s["dt_step"], 9)
            dve.scalar_tensor_tensor(dt[:, :], dt_x[:, :], 0.0, dt_t[:, 2, :], ALU.max, ALU.add)\
                .then_inc(s["dt_step"], 1)
            dve.wait_ge(s["dt_step"], 10)
            dve.wait_ge(s["neg_a"], 1)
            dve.scalar_tensor_tensor(a_dt[:, :], dt[:, :], -1.0, alog_bc[:, :], ALU.mult, ALU.mult)\
                .then_inc(s["a_dt_ready"], 1)
            dve.wait_ge(s["a_dt_ready"], 1)

            def steps_chunk(n):
                if not (isinstance(n, int) and n == 0):
                    dve.wait_ge(s["segsum_mm"], 2 * n - 1)
                dve.tensor_tensor(steps[:, 0, :, :], upper[:, :].unsqueeze(1).broadcast_to([P, HC, P]),
                                  a_dt[:, bass.ds(2 * HC * n, HC)].unsqueeze(2).broadcast_to([P, HC, P]), ALU.mult)\
                    .then_inc(s["steps_even"], 1)

            def bc_taps(i, steps_of):
                dve.wait_ge(s["bc_tap"], 4 * (i + 1))
                for k in range(1, TAPS):
                    if k > 1:
                        dve.wait_ge(tap_chain, 4 * (2 * i + k - 1))
                    for t in range(4):
                        tile = 4 * i + t
                        dve.scalar_tensor_tensor(
                            bc_acc[:, tile, k:], bc_bank[i][:, t * P:t * P + P - k],
                            cw[:, INTER // P + tile, TAPS - 1 - k:TAPS - k], bc_acc[:, tile, k:], ALU.mult, ALU.add)\
                            .then_inc(tap_chain if k < TAPS - 1 else s["bc_conv"], 1)
                    if k - 1 < len(steps_of):
                        steps_chunk(steps_of[k - 1])

            steps_chunk(0)
            bc_taps(0, [1, 2])
            bc_taps(1, [3, 4])
            bc_taps(2, [5, 6])
            bc_taps(3, [7])

            def make_gm():
                dve.wait_ge(s["g_mm"], 1)
                for j in range(2):
                    dve.tensor_tensor(gm[:, 4 * j:4 * j + 4, :],
                                      bank[5 + j][:, :].rearrange("p (g l) -> p g l", g=4),
                                      upper[:, :].unsqueeze(1).broadcast_to([P, 4, P]), ALU.mult)\
                        .then_inc(s["gm_ready"], 1)

            def digits_of_weights():
                dve.wait_ge(s["dequant_in"], 48)
                dve.wait_ge(s["m_ready"], CH)
                dve.tensor_scalar(digits[:, :, :, 0], packed[:, :, :], 15, None, ALU.bitwise_and)\
                    .then_inc(s["digits_ready"], 1)
                dve.tensor_scalar(digits[:, :, :, 1], packed[:, :, :], 4, None, ALU.arith_shift_right)\
                    .then_inc(s["digits_ready"], 1)

            def subtract_zeros():
                dve.wait_ge(s["digits_ready"], 2)
                for o in range(KC):
                    dve.tensor_tensor(weights[:, o, :].rearrange("p (g k) -> p g k", g=QG),
                                      digits[:, o, :, :].rearrange("p (g k) two -> p g (k two)", g=QG),
                                      zero_sb[:, o, :].unsqueeze(2).broadcast_to([P, QG, DM // QG]), ALU.subtract)\
                        .then_inc(s["digits_off"], 1)

            def scale_weights():
                dve.wait_ge(s["digits_off"], KC)
                for o in range(KC):
                    last = dve.tensor_tensor(weights[:, o, :].rearrange("p (g k) -> p g k", g=QG),
                                             weights[:, o, :].rearrange("p (g k) -> p g k", g=QG),
                                             scale_sb[:, o, :].unsqueeze(2).broadcast_to([P, QG, DM // QG]), ALU.mult)
                last.then_inc(s["weights_ready"], 1)

            def gate_low(n, i):
                dve.wait_ge(s["gate_hi_ready"], 2 * n + i + 1)
                dve.tensor_tensor(w_gate_lo[:, i, :, :], w_gate_sb[:, i, :, :], w_gate_hi[:, :, :].bitcast(F32),
                                  ALU.subtract).then_inc(s["gate_lo_ready"], 1)

            def ygT_low(n, i):
                c = 2 * n + i
                dve.wait_ge(s["ygT_hi_ready"], 4 * (c + 1))
                for t in range(4):
                    dve.scalar_tensor_tensor(y_gT_lo[:, t, :], bank[5][:, t * P:(t + 1) * P],
                                             nw[:, bass.ds(4 * c + t, 1)], y_gT_hi[:, t, :].bitcast(F32),
                                             ALU.mult, ALU.subtract).then_inc(s["ygT_lo_ready"], 1)

            def conv_step(n, i):
                c = 2 * n + i
                dve.wait_ge(s["hs_tap"], 4 * (c + 1))
                for k in range(1, TAPS):
                    if k > 1:
                        dve.wait_ge(s["hs_conv"], 12 * c + 4 * (k - 1))
                    for t in range(4):
                        w = cw[:, bass.ds(4 * c + t, 1), TAPS - 1 - k:TAPS - k].rearrange("p a b -> p (a b)")
                        dve.scalar_tensor_tensor(conv[:, i, t, k:], bank[i][:, t * P:t * P + P - k], w,
                                                 conv[:, i, t, k:], ALU.mult, ALU.add).then_inc(s["hs_conv"], 1)

            def add_group(n):
                dve.wait_ge(s["out_mm"], 2 * (n + 1))
                dve.wait_ge(s["scale_ready"], n + 1)
                dve.scalar_tensor_tensor(xres[:, :], bank[6][:, :], group_scale[:, 0:1], xres[:, :], ALU.mult, ALU.add)\
                    .then_inc(s["out_added"], 1)
                dve.wait_ge(s["out_added"], n + 1)

            def chunk_dve(n, i, first_group, last_chunk):
                c = 2 * n + i
                dve.wait_ge(s["hsT_mm"], c + 1)
                if not first_group:
                    dve.wait_ge(s["y_mm"], c - 1)
                hs = bank[3][:, :].rearrange("p (h d) -> p h d", h=HC)
                dve.tensor_tensor(x_dt[:, i, :, :], hs, dt[:, bass.ds(HC * c, HC)].unsqueeze(2)
                                  .broadcast_to([P, HC, PH]), ALU.mult)
                dve.tensor_tensor(x_skip[:, i, :].rearrange("p (h d) -> p h d", h=HC), hs,
                                  d_bc[:, bass.ds(HC * c, HC)].unsqueeze(2).broadcast_to([P, HC, PH]), ALU.mult)\
                    .then_inc(s["x_ready"], 1)
                if last_chunk:
                    digits_of_weights()
                else:
                    conv_step(n + i, 1 - i)
                dve.wait_ge(s["y_mm"], c + 1)
                dve.wait_ge(s["x_ready"], c + 1)
                if not first_group:
                    dve.wait_ge(s["ygT_mm"], c - 1)
                    dve.wait_ge(s["square_ready"], c - 1)
                dve.tensor_tensor(y[:, i, :], bank[4][:, :], x_skip[:, i, :], ALU.add).then_inc(s["y_sum"], 1)
                dve.wait_ge(s["y_sum"], c + 1)
                dve.wait_ge(s["gate_act"], c + 1)
                dve.tensor_tensor(y[:, i, :], y[:, i, :], gate[:, i, :], ALU.mult).then_inc(s["y_gated"], 1)
                if last_chunk:
                    subtract_zeros()
                else:
                    gate_low(n + i, 1 - i)
                ygT_low(n, i)
                if i == 0 and not first_group:
                    add_group(n - 1)

            conv_step(0, 0)
            make_gm()
            dve.wait_ge(s["gate_hi_ready"], 1)
            dve.tensor_tensor(w_gate_lo[:, 0, 2:4, :], w_gate_sb[:, 0, 2:4, :], w_gate_hi[:, 2:4, :].bitcast(F32),
                              ALU.subtract).then_inc(s["first_gate_lo"], 1)
            chunk_dve(0, 0, True, False)
            chunk_dve(0, 1, True, False)
            with dve.Fori(1, CH // 2 - 1) as n:
                chunk_dve(n, 0, False, False)
                chunk_dve(n, 1, False, False)
            chunk_dve(CH // 2 - 1, 0, False, False)
            chunk_dve(CH // 2 - 1, 1, False, True)
            scale_weights()
            add_group(CH // 2 - 1)

            layer_norm(3)
            dve.wait_ge(s["xn_ready"], 3)
            dve.wait_ge(s["bias_in"], 16)
            dve.tensor_tensor(xres[:, :], xres[:, :], bias_bc[:, :], ALU.add).then_inc(s["ffn_bias"], 1)
            dve.wait_ge(s["ffn_bias"], 1)
            dve.wait_ge(s["ffn_mm"], 1)
            dve.tensor_tensor(xres[:, :], xres[:, :], bank[4][:, :], ALU.add).then_inc(s["ffn_bias"], 1)

        @block.gpsimd
        def _(pool):
            def norm_scale(n):
                pool.wait_ge(s["norm_agg"], n)
                pool.tensor_scalar(var_eps[:, :], mean_var[:, 1:2], EPS, None, ALU.add).then_inc(s["norm_eps"], 1)
                pool.wait_ge(s["norm_eps"], n)
                pool.tensor_tensor(rstd[:, :], var_eps[:, :], half_neg[:, :], ALU.pow).then_inc(s["norm_rstd"], 1)

            def split_weight(raw, hi, lo, arrived, hi_done, lo_done, g):
                pool.wait_ge(arrived, 16 * (g + 1))
                keep_wait_apart(pool)
                pool.tensor_copy(hi[:, :, :], raw[:, :, :]).then_inc(hi_done, 1)
                pool.wait_ge(hi_done, g + 1)
                pool.tensor_tensor(lo[:, :, :], raw[:, :, :], hi[:, :, :].bitcast(F32), ALU.subtract)\
                    .then_inc(lo_done, 1)

            def k_low(g):
                for b in range(KB):
                    blk = slice(b * 512, (b + 1) * 512)
                    pool.wait_ge(s["k_hi_ready"], KB * g + b + 1)
                    pool.tensor_tensor(k_lo[:, blk], rope_a[:, (b + 1) % 2, :], k_hi[:, blk].bitcast(F32), ALU.subtract)\
                        .then_inc(s["k_lo_ready"], 1)

            def split_wk(g):
                split_weight(wk_raw, wk_hi, wk_lo, s["wk_in"], s["wk_hi_ready"], s["wk_lo_ready"], g)

            def split_wv(g):
                split_weight(wv_raw, wv_hi, wv_lo, s["wv_in"], s["wv_hi_ready"], s["wv_lo_ready"], g)

            def wqo_low(hi_ready, done, g):
                pool.wait_ge(hi_ready, g + 1)
                pool.tensor_tensor(wqo_lo[:, :, :], wqo_raw[:, :, :], wqo_hi[:, :, :].bitcast(F32), ALU.subtract)\
                    .then_inc(done, 1)

            pool.memset(half_neg[:, :], -0.5).then_inc(s["consts_ready"], 1)
            pool.memset(ones[:, :], 1.0).then_inc(s["consts_ready"], 1)
            pool.wait_ge(s["consts_ready"], 2)
            pool.affine_select(out=ident[:, :], in_=ones[:, :], compare_op=ALU.is_equal, fill=0.0, base=0,
                               pattern=[[-1, P]], channel_multiplier=1).then_inc(s["consts_ready"], 1)
            pool.affine_select(out=upper[:, :], in_=ones[:, :], compare_op=ALU.is_ge, fill=0.0, base=0,
                               pattern=[[1, P]], channel_multiplier=-1).then_inc(s["consts_ready"], 1)
            pool.affine_select(out=below[:, :], in_=ones[:, :], compare_op=ALU.is_gt, fill=0.0, base=0,
                               pattern=[[-1, P]], channel_multiplier=1).then_inc(s["consts_ready"], 1)
            norm_scale(1)
            split_wk(0)
            split_wv(0)
            k_low(0)
            with pool.Fori(1, G) as g:
                split_wk(g)
                wqo_low(s["wq_hi_ready"], s["wq_lo_ready"], g)
                split_wv(g)
                k_low(g)
                wqo_low(s["wo_hi_ready"], s["wo_lo_ready"], g - 1)
            wqo_low(s["wo_hi_ready"], s["wo_lo_ready"], G - 1)

            norm_scale(2)

            def steps_odd_chunk(n):
                if not (isinstance(n, int) and n == 0):
                    pool.wait_ge(s["segsum_mm"], 2 * n)
                for j in range(2):
                    pool.tensor_tensor(
                        steps[:, 1, 4 * j:4 * j + 4, :], upper[:, :].unsqueeze(1).broadcast_to([P, 4, P]),
                        a_dt[:, bass.ds((2 * n + 1) * HC + 4 * j, 4)].unsqueeze(2).broadcast_to([P, 4, P]),
                        ALU.mult).then_inc(s["steps_odd"], 1)

            pool.wait_ge(s["a_dt_ready"], 1)
            steps_odd_chunk(0)
            with pool.Fori(1, CH // 2) as n:
                steps_odd_chunk(n)

            def out_low(n, i):
                pool.wait_ge(s["wout_hi_ready"], 2 * n + i + 1)
                pool.tensor_tensor(w_out_lo[:, i, :, :], w_out_sb[:, i, :, :], w_out_hi[:, i, :, :].bitcast(F32),
                                   ALU.subtract).then_inc(s["wout_lo_ready"], 1)

            def decay_products(n, i):
                c = 2 * n + i
                if isinstance(n, int) and n == 0:
                    pool.wait_ge(s["gm_ready"], 2)
                    pool.wait_ge(s["decay_ready"], CH)
                else:
                    pool.wait_ge(s["y_mm"], c - 1)
                pool.tensor_tensor(m_t[:, i, :, :], decay[:, bass.ds(HC * c, HC), :], gm[:, :, :], ALU.mult)\
                    .then_inc(s["m_ready"], 1)

            def group_norm(n):
                pool.wait_ge(s["square_ready"], 2 * (n + 1))
                pool.tensor_tensor(ms[:, :], square_sum[:, 0:1], square_sum[:, 1:2], ALU.add).then_inc(s["ms_sum"], 1)
                pool.wait_ge(s["ms_sum"], n + 1)
                keep_wait_apart(pool)
                pool.tensor_scalar(ms_eps[:, :], ms[:, :], NG / INTER, EPS, ALU.mult, ALU.add)\
                    .then_inc(s["ms_eps_ready"], 1)
                pool.wait_ge(s["ms_eps_ready"], n + 1)
                at_least(pool, s["out_added"], n)
                pool.tensor_tensor(group_scale[:, :], ms_eps[:, :], half_neg[:, :], ALU.pow).then_inc(s["scale_ready"], 1)

            pool.wait_ge(s["gate_hi_ready"], 1)
            pool.tensor_tensor(w_gate_lo[:, 0, 0:2, :], w_gate_sb[:, 0, 0:2, :], w_gate_hi[:, 0:2, :].bitcast(F32),
                               ALU.subtract).then_inc(s["first_gate_lo"], 1)
            decay_products(0, 0)
            decay_products(0, 1)

            with pool.Fori(1, CH // 2) as n:
                decay_products(n, 0)
                out_low(n - 1, 0)
                decay_products(n, 1)
                group_norm(n - 1)
                out_low(n - 1, 1)
            out_low(CH // 2 - 1, 0)
            out_low(CH // 2 - 1, 1)
            group_norm(CH // 2 - 1)
            norm_scale(3)


_F = np.float32


def _rope_tables():
    freq = _F(1.0) / _F(10000.0) ** (np.arange(0, DH, 2, dtype=_F) / _F(DH))
    angle = np.arange(SK, dtype=_F)[:, None] * freq[None, :].astype(_F)
    cos, sin = np.cos(angle.astype(np.float64)), np.sin(angle.astype(np.float64))
    k_cos = np.concatenate([cos.T, cos.T]).astype(_F)
    k_sin = np.concatenate([sin.T, -sin.T]).astype(_F)
    q_scale = 1.0 / np.sqrt(float(DH))
    return k_cos, k_sin, (cos[:P] * q_scale).astype(_F), (sin[:P] * q_scale).astype(_F)


def kernel(**inputs):
    import concourse.bacc as bacc
    from concourse.bass_utils import run_bass_kernel_spmd

    a = {name: np.asarray(v) for name, v in inputs.items()}

    def by_input(w, columns):
        return w.reshape(KC, P, -1, columns).transpose(2, 1, 0, 3)

    w_in = a["L0_attn_in_proj_w"].T
    gate_end, hs_end, bc_end = INTER, 2 * INTER, 2 * INTER + 2 * G * NS
    k_cos, k_sin, q_cos, q_sin = _rope_tables()
    laid = {
        "x": a["x"][0],
        "mask": a["mask_BxSxS2_ff0"][0],
        "ctx_t": a["ctx_4096"][0].T.reshape(KC, P, SK).transpose(1, 0, 2),
        "rope_k_cos": k_cos, "rope_k_sin": k_sin, "rope_q_cos": q_cos, "rope_q_sin": q_sin,
        "wk": by_input(a["L0_xattn_wk"], DH),
        "wv": by_input(a["L0_xattn_wv"], DH),
        "wq": by_input(a["L0_xattn_wq"], HG * DH),
        "wo": a["L0_xattn_wo"].reshape(G, HG, DH, DM).transpose(0, 2, 1, 3),
        "w_dt": by_input(w_in[:, bc_end:], MH)[0],
        "w_bc": by_input(w_in[:, hs_end:bc_end], 512),
        "w_hs": by_input(w_in[:, gate_end:hs_end], 512),
        "w_gate": by_input(w_in[:, :gate_end], 512),
        "w_out": a["L0_attn_out_proj_w"].T.reshape(CH, 4, P, DM).transpose(0, 2, 1, 3),
        "conv_w": a["L0_attn_conv_w"].reshape(XT_TILES, P, TAPS).transpose(1, 0, 2),
        "conv_b": a["L0_attn_conv_b"].reshape(XT_TILES, P).T,
        "dt_bias": a["L0_attn_dt_bias"],
        "a_log": a["L0_attn_A_log"],
        "d_skip": a["L0_attn_D"],
        "norm_w": a["L0_attn_norm_weight"].reshape(INTER // P, P).T,
        "q_packed": a["L0_ffn_weight_quantized"].reshape(KC, P, DM // 2).transpose(1, 0, 2),
        "q_scale": a["L0_ffn_weight_scales"].reshape(KC, P, QG).transpose(1, 0, 2),
        "q_zero": a["L0_ffn_weight_zero_points"].reshape(KC, P, QG).transpose(1, 0, 2),
        "q_bias": a["L0_ffn_bias"],
    }
    nc = bacc.Bacc("TRN2", target_bir_lowering=False, num_devices=1)
    arrays, args = {}, []
    for name, v in laid.items():
        arrays[f"in_{name}"] = v = np.ascontiguousarray(v)
        args.append(nc.dram_tensor(f"in_{name}", v.shape, mybir.dt.from_np(v.dtype), kind="ExternalInput").ap())
    args.append(nc.dram_tensor("out_x", (P, DM), F32, kind="ExternalOutput").ap())
    build(nc, *args)
    r = run_bass_kernel_spmd(nc, [arrays], core_ids=[0])
    return r.results[0]["out_x"].reshape(1, P, DM)
```

```python
from contextlib import ExitStack

import numpy as np

import concourse.bass as bass
from concourse import mybir

F32 = mybir.dt.float32
F32R = mybir.dt.float32r
I32 = mybir.dt.int32
ALU = mybir.AluOpType
ACT = mybir.ActivationFunctionType
X_AXIS = mybir.AxisListType.X

P = 128
DM = 512
KC = DM // P
SK = 2048
KB = SK // 512
KT = SK // P
G = 8
HG = 4
DH = 128
INTER = 8192
CH = INTER // 512
HC = 8
PH = 64
NS = 128
MH = 128
TAPS = 4
BCC = 4
XT_TILES = INTER // P + 4 * BCC
NG = 8
QG = 32
PAIRS = (slice(0, KC // 2), slice(KC // 2, KC))
HALVES = (slice(0, DM // 2), slice(DM // 2, DM))
EPS = 1e-5
LOWEST = -3.4028234663852886e38


def sum_steps(last_head):
    return (11, 12, 14, 15) if last_head else (1, 4, 7, 8)


def at_least(eng, sem, count):
    if not isinstance(count, int) or count > 0:
        eng.wait_ge(sem, count)


def keep_wait_apart(eng):
    eng.nop(nofuse=True)


def build(nc, x, mask, ctx_t, rope_k_cos, rope_k_sin, rope_q_cos, rope_q_sin, wk, wv, wq, wo, w_dt, w_bc,
          w_hs, w_gate, w_out, conv_w, conv_b, dt_bias, a_log, d_skip, norm_w, q_packed, q_scale, q_zero,
          q_bias, out):
    with ExitStack() as whole:
        def sb(name, shape, dt=F32, scope=whole):
            return scope.enter_context(nc.sbuf_tensor(name, shape, dt))

        xres = sb("xres", [P, DM])
        for_q = ExitStack()
        qx_lo = sb("qx_lo", [P, KC, P], F32R, for_q)
        qx_hi = sb("qx_hi", [P, KC, P], F32R, for_q)
        for_q.close()
        xn = sb("xn", [P, DM])
        bias_bc = sb("bias_bc", [P, DM])
        xnT = sb("xnT", [P, KC, P])
        ident = sb("ident", [P, P])
        ones = sb("ones", [P, P])
        upper = sb("upper", [P, P])
        below = sb("below", [P, P])
        ones_r = sb("ones_r", [P, P], F32R)
        stats = sb("stats", [P, 2, 6])
        mean_var = sb("mean_var", [P, 2])
        var_eps = sb("var_eps", [P, 1])
        rstd = sb("rstd", [P, 1])
        half_neg = sb("half_neg", [P, 1])

        attn = ExitStack()
        ctx_hi = sb("ctx_hi", [P, KC, SK], F32R, attn)
        ctx_lo = sb("ctx_lo", [P, KC, SK], F32R, attn)
        k_hi = sb("k_hi", [P, SK], F32R, attn)
        k_lo = sb("k_lo", [P, SK], F32R, attn)
        v_hi = sb("v_hi", [P, KT, DH], F32R, attn)
        v_lo = sb("v_lo", [P, KT, DH], F32R, attn)
        cos_k = sb("cos_k", [P, SK], F32, attn)
        sin_k = sb("sin_k", [P, SK], F32, attn)
        mask_sb = sb("mask_sb", [P, SK], F32, attn)
        pt_hi_01 = sb("pt_hi_01", [P, 2, 512], F32R, attn)
        pt_lo_01 = sb("pt_lo_01", [P, 2, 512], F32R, attn)
        third = ExitStack()
        sb("rope_a_first", [P, 512], F32, third)
        pt_hi_2 = sb("pt_hi_2", [P, 512], F32R, third)
        sb("rope_b_first", [P, 512], F32, third)
        pt_lo_2 = sb("pt_lo_2", [P, 512], F32R, third)
        third.close()
        diagonal = ExitStack()
        diag_hi = sb("diag_hi", [P, HG, P], F32R, diagonal)
        diagonal.close()
        rope_a = sb("rope_a", [P, 2, 512], F32, attn)
        rope_b = sb("rope_b", [P, 2, 512], F32, attn)
        pt_hi = [pt_hi_01[:, 0, :], pt_hi_01[:, 1, :], pt_hi_2[:, :]]
        pt_lo = [pt_lo_01[:, 0, :], pt_lo_01[:, 1, :], pt_lo_2[:, :]]
        wqo_hi = sb("wqo_hi", [P, KC, 512], F32R, attn)
        wk_hi = sb("wk_hi", [P, KC, DH], F32R, attn)
        wv_hi = sb("wv_hi", [P, KC, DH], F32R, attn)
        arriving = ExitStack()
        wk_raw = sb("wk_raw", [P, KC, DH], F32, arriving)
        wv_raw = sb("wv_raw", [P, KC, DH], F32, arriving)
        wqo_raw = sb("wqo_raw", [P, KC, 512], F32, arriving)
        arriving.close()
        wk_lo = sb("wk_lo", [P, KC, DH], F32R, attn)
        wv_lo = sb("wv_lo", [P, KC, DH], F32R, attn)
        wqo_lo = sb("wqo_lo", [P, KC, 512], F32R, attn)
        qT_hi = sb("qT_hi", [P, HG, P], F32R, attn)
        qT_lo = sb("qT_lo", [P, HG, P], F32R, attn)
        cos_q = sb("cos_q", [P, DH // 2], F32, attn)
        sin_q = sb("sin_q", [P, DH // 2], F32, attn)
        block_max = sb("block_max", [P, HG, KB], F32, attn)
        neg_max = sb("neg_max", [P, HG], F32, attn)
        row_sum = sb("row_sum", [P, HG], F32, attn)
        inv_sum = sb("inv_sum", [P, HG], F32, attn)
        inv_hi = sb("inv_hi", [P, HG], F32R, attn)
        inv_lo = sb("inv_lo", [P, HG], F32R, attn)
        stage = ExitStack()
        ctx_raw = sb("ctx_raw", [P, KB, KC, 512], F32, stage)
        stage.close()
        output = ExitStack()
        sb("probs_of_three", [P, HG - 1, SK], F32, output)
        attn_hi = sb("attn_hi", [P, HG, P], F32R, output)
        attn_lo = sb("attn_lo", [P, HG, P], F32R, output)
        output.close()
        turned = ExitStack()
        probs_r = sb("probs_r", [P, HG, SK], F32R, turned)
        diag_lo = probs_r[:, :, 0:P]
        turned.close()
        probs = sb("probs", [P, HG, SK], F32, attn)
        attn.close()

        mam = ExitStack()
        arriving = ExitStack()
        w_gate_sb = sb("w_gate_sb", [P, 2, KC, 512], F32, arriving)
        w_out_sb = sb("w_out_sb", [P, 2, KC, 512], F32, arriving)
        arriving.close()
        w_gate_lo = sb("w_gate_lo", [P, 2, KC, 512], F32R, mam)
        w_out_lo = sb("w_out_lo", [P, 2, KC, 512], F32R, mam)
        w_hs_sb = sb("w_hs_sb", [P, 2, KC, 512], F32, mam)
        w_dt_sb = sb("w_dt_sb", [P, KC, MH], F32, mam)
        cw = sb("cw", [P, XT_TILES, TAPS], F32, mam)
        cb = sb("cb", [P, XT_TILES], F32, mam)
        nw = sb("nw", [P, INTER // P], F32, mam)
        d_bc = sb("d_bc", [P, MH], F32, mam)
        dtb_bc = sb("dtb_bc", [P, MH], F32, mam)
        alog_bc = sb("alog_bc", [P, MH], F32, mam)
        scale_sb = sb("scale_sb", [P, KC, QG], F32, mam)
        zero_sb = sb("zero_sb", [P, KC, QG], I32, mam)
        packed = sb("packed", [P, KC, DM // 2], I32, mam)
        after_decay = ExitStack()
        digits = sb("digits", [P, KC, DM // 2, 2], I32, after_decay)
        weights = sb("weights", [P, KC, DM], F32, after_decay)
        wT = sb("wT", [P, KC, DM], F32, after_decay)
        after_decay.close()
        decay = sb("decay", [P, MH, P], F32, mam)
        pre = ExitStack()
        bc_acc = sb("bc_acc", [P, 4 * BCC, P], F32, pre)
        bc_act = sb("bc_act", [P, 4 * BCC, P], F32, pre)
        pre.close()
        w_gate_hi = sb("w_gate_hi", [P, KC, 512], F32R, mam)
        w_out_hi = sb("w_out_hi", [P, 2, KC, 512], F32R, mam)
        xnT_hi = sb("xnT_hi", [P, KC, P], F32R, mam)
        xnT_lo = sb("xnT_lo", [P, KC, P], F32R, mam)
        gm = sb("gm", [P, G, P], F32, mam)
        dt_x = sb("dt_x", [P, MH], F32, mam)
        dt_t = sb("dt_t", [P, 4, MH], F32, mam)
        dt = sb("dt", [P, MH], F32, mam)
        a_dt = sb("a_dt", [P, MH], F32, mam)
        x_dt = sb("x_dt", [P, 2, HC, PH], F32, mam)
        x_skip = sb("x_skip", [P, 2, 512], F32, mam)
        gate = sb("gate", [P, 2, 512], F32, mam)
        y = sb("y", [P, 2, 512], F32, mam)
        conv = sb("conv", [P, 2, 4, P], F32, mam)
        hsT = sb("hsT", [P, 2, 4, P], F32, mam)
        pre = ExitStack()
        steps_hi = sb("steps_hi", [P, HC, P], F32R, pre)
        steps_lo = sb("steps_lo", [P, HC, P], F32R, pre)
        steps = sb("steps", [P, HC, P], F32, pre)
        pre.close()
        m_t = sb("m_t", [P, 2, HC, P], F32, mam)
        y_gT_hi = sb("y_gT_hi", [P, 4, P], F32R, mam)
        y_gT_lo = sb("y_gT_lo", [P, 4, P], F32R, mam)
        below_r = sb("below_r", [P, P], F32R, mam)
        a_hi = sb("a_hi", [P, MH], F32R, mam)
        a_lo = sb("a_lo", [P, MH], F32R, mam)
        square_sum = sb("square_sum", [P, 2], F32, mam)
        ms = sb("ms", [P, 1], F32, mam)
        ms_eps = sb("ms_eps", [P, 1], F32, mam)
        group_scale = sb("group_scale", [P, 1], F32, mam)
        mam.close()

        bank = [whole.enter_context(nc.psum_tensor(f"bank{i}", [P, 512], F32)) for i in range(8)]
        ring_a = bank[0:4]
        ring_b = bank[4:6]
        pv_bank, oq_bank = bank[6], bank[7]
        dt_bank = bank[1]
        bc_bank = [bank[0], bank[2], bank[3], bank[4]]
        segsum_bank = [bank[5], bank[6], bank[7], bank[1]]

        def ygT_bank(t, last_chunk):
            return bank[3] if last_chunk and t >= 2 else bank[5]

        names = """consts_ready below_ready ones_r_ready below_r_ready x_in mask_in tables_in bias_in wk_in wv_in
            wq_in wo_in out_stored xres_half_added norm_stats norm_agg norm_eps norm_rstd xn_ready xnT_mm xnT_ready
            qx_hi_ready qx_lo_ready first_wq_hi first_wq_lo wq_hi_ready wq_lo_ready wo_hi_ready wo_lo_ready
            attn_hi_ready attn_lo_ready ctx_hi_ready ctx_lo_ready wk_hi_ready wk_lo_ready wv_hi_ready wv_lo_ready
            kproj_ready krope_mul krope_add k_hi_ready k_lo_ready qproj_ready qrope_mul qrope_add qT_mm qT_hi_ready
            qT_lo_ready vproj_ready v_copied vT_mm v_hi_ready v_lo_ready scores_ready scores_masked neg_max_ready
            probs_ready pT_mm pt_hi_ready pt_lo_ready pv_ready inv_sum_ready inv_hi_ready inv_lo_ready diag_ready
            bcast_mm bcast_ready attn_out_ready oproj_ready res_added small_in dequant_in dt_in gate_in0 gate_in1
            hs_in0 hs_in1 wout_in0 wout_in1 dt_mm dt_step dt_act neg_a a_dt_ready bc_mm bc_tap bc_tap_added bc_conv
            bc_act_ready steps_even steps_odd even_mm odd_mm a_hi_ready a_lo_ready decay_ready g_mm gm_ready
            digits_ready digits_off weights_ready wT_mm wT_ready hs_mm hs_tap hs_conv hs_act hsT_mm x_ready m_ready
            gate_mm gate_act y_mm y_sum y_gated square_ready xnT_hi_ready xnT_lo_ready gate_hi_ready gate_lo_ready
            first_gate_lo wout_hi_ready wout_lo_ready last_wout_lo ygT_mm ygT_hi_ready ygT_lo_ready out_mm ms_sum
            ms_eps_ready scale_ready out_added ffn_mm ffn_bias ffn_added o_half_mm out_half_mm last_exp
            last_sum_ready""".split()
        s = {n: whole.enter_context(nc.semaphore(n)) for n in names}
        first_ctx_in = [whole.enter_context(nc.semaphore(f"first_ctx_in{i}")) for i in range(2)]
        ctx_in = [whole.enter_context(nc.semaphore(f"ctx_in{b}")) for b in range(KB)]
        rope_k_in = [whole.enter_context(nc.semaphore(f"rope_k_in{b}")) for b in range(KB)]
        gate_in, hs_in, wout_in = ([s[f"{n}{i}"] for i in range(2)] for n in ("gate_in", "hs_in", "wout_in"))
        block = whole.enter_context(nc.Block())

        @block.sync
        def _(sp):
            sp.dma_start(xres[:, :], x).then_inc(s["x_in"], 16)
            sp.dma_start(wk_raw[:, :, :], wk[0]).then_inc(s["wk_in"], 16)

            def load_context(b):
                sp.dma_start(ctx_raw[:, b, :, :], ctx_t[:, :, b * 512:(b + 1) * 512]).then_inc(ctx_in[b], 16)

            def load_rope_k(b):
                blk = slice(b * 512, (b + 1) * 512)
                sp.dma_start(cos_k[:, blk], rope_k_cos[:, blk]).then_inc(rope_k_in[b], 16)
                sp.dma_start(sin_k[:, blk], rope_k_sin[:, blk]).then_inc(rope_k_in[b], 16)

            for i, two in enumerate(PAIRS):
                sp.dma_start(ctx_raw[:, 0, two, :], ctx_t[:, two, 0:512]).then_inc(first_ctx_in[i], 16)
            sp.dma_start(wqo_raw[:, :, :], wq[0]).then_inc(s["wq_in"], 16)
            load_context(1)
            sp.dma_start(cos_q[:, :], rope_q_cos).then_inc(s["tables_in"], 16)
            sp.dma_start(sin_q[:, :], rope_q_sin).then_inc(s["tables_in"], 16)
            load_rope_k(0)
            sp.dma_start(wv_raw[:, :, :], wv[0]).then_inc(s["wv_in"], 16)
            load_context(2)
            load_rope_k(1)
            load_context(3)
            load_rope_k(2)
            load_rope_k(3)
            sp.dma_start(mask_sb[:, :], mask).then_inc(s["mask_in"], 16)
            sp.wait_ge(s["qproj_ready"], 1)
            sp.dma_start(wqo_raw[:, :, :], wq[1]).then_inc(s["wq_in"], 16)
            sp.wait_ge(s["kproj_ready"], KB)
            sp.dma_start(wk_raw[:, :, :], wk[1]).then_inc(s["wk_in"], 16)
            sp.wait_ge(s["vproj_ready"], KB)
            sp.dma_start(wv_raw[:, :, :], wv[1]).then_inc(s["wv_in"], 16)
            with sp.Fori(2, G) as g:
                sp.wait_ge(s["qproj_ready"], g)
                sp.dma_start(wqo_raw[:, :, :], wo[g - 2]).then_inc(s["wo_in"], 16)
                sp.wait_ge(s["kproj_ready"], KB * g)
                sp.dma_start(wk_raw[:, :, :], wk[g]).then_inc(s["wk_in"], 16)
                sp.wait_ge(s["vproj_ready"], KB * g)
                sp.dma_start(wv_raw[:, :, :], wv[g]).then_inc(s["wv_in"], 16)
                sp.wait_ge(s["oproj_ready"], g - 1)
                sp.dma_start(wqo_raw[:, :, :], wq[g]).then_inc(s["wq_in"], 16)
            sp.wait_ge(s["qproj_ready"], G)
            sp.dma_start(wqo_raw[:, :, :], wo[G - 2]).then_inc(s["wo_in"], 16)
            sp.wait_ge(s["oproj_ready"], G - 1)
            sp.dma_start(wqo_raw[:, :, :], wo[G - 1]).then_inc(s["wo_in"], 16)

            sp.wait_ge(s["vproj_ready"], KB * G)
            for i in range(BCC):
                ring, sem = (w_gate_sb, gate_in) if i < 2 else (w_out_sb, wout_in)
                sp.dma_start(ring[:, i % 2, :, :], w_bc[i]).then_inc(sem[i % 2], 16)
            sp.wait_ge(s["xres_half_added"], 2)
            sp.dma_start(w_dt_sb[:, :, :], w_dt).then_inc(s["dt_in"], 16)
            for dst, src in ((dtb_bc, dt_bias), (alog_bc, a_log), (d_bc, d_skip)):
                sp.dma_start(dst[:, :], src.partition_broadcast(P)).then_inc(s["small_in"], 16)
            sp.dma_start(cw[:, :, :], conv_w).then_inc(s["small_in"], 16)
            sp.dma_start(cb[:, :], conv_b).then_inc(s["small_in"], 16)
            sp.dma_start(nw[:, :], norm_w).then_inc(s["small_in"], 16)
            sp.dma_start(w_hs_sb[:, 0, :, :], w_hs[0]).then_inc(hs_in[0], 16)
            sp.dma_start(w_hs_sb[:, 1, :, :], w_hs[1]).then_inc(hs_in[1], 16)
            sp.dma_start(bias_bc[:, :], q_bias.partition_broadcast(P)).then_inc(s["bias_in"], 16)
            sp.dma_start(packed[:, :, :], q_packed).then_inc(s["dequant_in"], 16)
            sp.dma_start(scale_sb[:, :, :], q_scale).then_inc(s["dequant_in"], 16)
            sp.dma_start(zero_sb[:, :, :], q_zero).then_inc(s["dequant_in"], 16)
            for i in range(2):
                sp.wait_ge(s["bc_mm"], i + 1)
                sp.dma_start(w_gate_sb[:, i, :, :], w_gate[i]).then_inc(gate_in[i], 16)
            for i in range(2):
                sp.wait_ge(s["bc_mm"], i + 3)
                sp.dma_start(w_out_sb[:, i, :, :], w_out[i]).then_inc(wout_in[i], 16)

            def refill(n, i, hs, gate, out_w):
                c = 2 * n + i
                if hs:
                    sp.wait_ge(s["hs_mm"], c + 2)
                    sp.dma_start(w_hs_sb[:, 1 - i, :, :], w_hs[c + 3]).then_inc(hs_in[1 - i], 16)
                if gate:
                    sp.wait_ge(s["gate_mm"], c + 1)
                    sp.dma_start(w_gate_sb[:, i, :, :], w_gate[c + 2]).then_inc(gate_in[i], 16)
                if out_w:
                    sp.wait_ge(s["out_mm"], c)
                    sp.dma_start(w_out_sb[:, 1 - i, :, :], w_out[c + 1]).then_inc(wout_in[1 - i], 16)

            sp.wait_ge(s["hs_mm"], 1)
            sp.dma_start(w_hs_sb[:, 0, :, :], w_hs[2]).then_inc(hs_in[0], 16)
            refill(0, 0, True, True, False)
            refill(0, 1, True, True, True)
            with sp.Fori(1, CH // 2 - 2) as n:
                refill(n, 0, True, True, True)
                refill(n, 1, True, True, True)
            refill(CH // 2 - 2, 0, True, True, True)
            refill(CH // 2 - 2, 1, False, True, True)
            refill(CH // 2 - 1, 0, False, False, True)

            for i, cols in enumerate(HALVES):
                sp.wait_ge(s["ffn_added"], i + 1)
                sp.dma_start(out[:, cols], xres[:, cols]).then_inc(s["out_stored"], 16)
            sp.wait_ge(s["out_stored"], 32)

        @block.tensor
        def _(pe):
            def pairs(dst, left_hi, left_lo, right_hi, right_lo, first, last):
                pe.matmul(dst, left_hi, right_hi, start=first, stop=False)
                pe.matmul(dst, left_hi, right_lo, start=False, stop=False)
                return pe.matmul(dst, left_lo, right_hi, start=False, stop=last)

            def transpose_norm(n):
                pe.wait_ge(s["xn_ready"], n)
                for c in range(KC):
                    last = pe.transpose(oq_bank[:, c * P:(c + 1) * P], xn[:, c * P:(c + 1) * P], ident[:, :])
                last.then_inc(s["xnT_mm"], 1)

            def first_head(g):
                return isinstance(g, int) and g == 0

            def project_k_block(g, b):
                if b == 0:
                    pe.wait_ge(s["wk_lo_ready"], g + 1)
                if not first_head(g):
                    pe.wait_ge(s["scores_masked"], HG * KB * g - KB + b + 1)
                for c in range(KC):
                    if first_head(g):
                        pe.wait_ge(s["ctx_lo_ready"], 2 * b + c // 2 + 1 if b < 2 else b + 3)
                    last = pairs(ring_a[b][:, :], wk_hi[:, c, :], wk_lo[:, c, :],
                                 ctx_hi[:, c, b * 512:(b + 1) * 512], ctx_lo[:, c, b * 512:(b + 1) * 512],
                                 c == 0, c == KC - 1)
                last.then_inc(s["kproj_ready"], 1)

            def project_q(g):
                if first_head(g):
                    pe.wait_ge(s["qx_lo_ready"], 1)
                for c in range(KC):
                    if first_head(g) and c == 0:
                        pe.wait_ge(s["first_wq_lo"], 1)
                    elif c == (2 if first_head(g) else 0):
                        pe.wait_ge(s["wq_lo_ready"], g + 1)
                    last = pairs(oq_bank[:, :], qx_hi[:, c, :], qx_lo[:, c, :], wqo_hi[:, c, :], wqo_lo[:, c, :],
                                 c == 0, c == KC - 1)
                last.then_inc(s["qproj_ready"], 1)

            def transpose_q(g):
                pe.wait_ge(s["qrope_add"], g + 1)
                if not first_head(g):
                    pe.wait_ge(s["v_lo_ready"], KB * g - 1)
                for h in range(HG):
                    last = pe.transpose(ring_b[0][:, h * P:(h + 1) * P], rope_a[:, 0, h * P:(h + 1) * P], ident[:, :])
                last.then_inc(s["qT_mm"], 1)

            def project_qk_and_first_v(g):
                project_k_block(g, 0)
                project_q(g)
                project_k_block(g, 1)
                transpose_q(g)
                project_k_block(g, 2)
                project_k_block(g, 3)
                project_v_block(g, 0)

            def project_v_block(g, b):
                if b == 0:
                    pe.wait_ge(s["wv_lo_ready"], g + 1)
                pe.wait_ge(s["krope_mul"], KB * g + b + 1)
                for c in range(KC):
                    last = pairs(ring_a[b][:, :], wv_hi[:, c, :], wv_lo[:, c, :],
                                 ctx_hi[:, c, b * 512:(b + 1) * 512], ctx_lo[:, c, b * 512:(b + 1) * 512],
                                 c == 0, c == KC - 1)
                last.then_inc(s["vproj_ready"], 1)

            def transpose_v_block(g, b):
                pe.wait_ge(s["v_copied"], KB * g + b + 1)
                if b == 0:
                    if first_head(g):
                        pe.wait_ge(s["qT_lo_ready"], 1)
                    else:
                        pe.wait_ge(s["pt_lo_ready"], KT * g)
                if b >= 2:
                    pe.wait_ge(s["v_lo_ready"], KB * g + b - 1)
                for t in range(4):
                    last = pe.transpose(ring_b[b % 2][:, t * P:(t + 1) * P], rope_b[:, b % 2, t * P:(t + 1) * P],
                                        ident[:, :])
                last.then_inc(s["vT_mm"], 1)

            def scores(g):
                pe.wait_ge(s["qT_lo_ready"], g + 1)
                for h in range(HG):
                    for b in range(KB):
                        j = KB * h + b
                        if h == 0:
                            pe.wait_ge(s["k_lo_ready"], KB * g + b + 1)
                            pe.wait_ge(s["v_copied"], KB * g + b + 1)
                        else:
                            pe.wait_ge(s["scores_masked"], HG * KB * g + j - KB + 1)
                        pairs(ring_a[b][:, :], qT_hi[:, h, :], qT_lo[:, h, :], k_hi[:, b * 512:(b + 1) * 512],
                              k_lo[:, b * 512:(b + 1) * 512], True, True).then_inc(s["scores_ready"], 1)
                    if h == 0:
                        transpose_v_block(g, KB - 1)

            def transpose_probs(g, t, last_head):
                if t == 0:
                    pe.wait_ge(s["probs_ready"], HG * (g + 1) - last_head)
                    pe.wait_ge(s["v_lo_ready"], KB * (g + 1))
                elif t >= 2:
                    pe.wait_ge(s["pt_lo_ready"], KT * g + t - 1)
                if last_head and t % 4 == 0:
                    pe.wait_ge(s["last_exp"], t // 4 + 1)
                for h in range(HG):
                    last = pe.transpose(ring_b[(t + 1) % 2][:, h * P:(h + 1) * P], probs[:, h, t * P:(t + 1) * P],
                                        ident[:, :])
                last.then_inc(s["pT_mm"], 1)

            def attend(g, last_head):
                for t in range(KT + 2):
                    if t == 1 and not last_head:
                        pe.wait_ge(s["qT_lo_ready"], g + 2)
                    if t == 2 and not last_head:
                        project_v_block(g + 1, 1)
                    if t < KT:
                        transpose_probs(g, t, last_head)
                    if t == sum_steps(last_head)[2]:
                        if first_head(g) or not isinstance(g, int):
                            pe.wait_ge(s["ones_r_ready"], 1)
                        pe.wait_ge(s["diag_ready"], g + 1)
                        pe.matmul(oq_bank[:, :].rearrange("p (h t) -> p h t", h=HG), ones_r[:, :], diag_hi[:, :, :],
                                  start=True, stop=False)
                        pe.matmul(oq_bank[:, :].rearrange("p (h t) -> p h t", h=HG), ones_r[:, :], diag_lo,
                                  start=False, stop=True).then_inc(s["bcast_mm"], 1)
                    if t == KT + 1 and not last_head:
                        project_v_block(g + 1, 2)
                    if t >= 2:
                        j = t - 2
                        pe.wait_ge(s["pt_lo_ready"], KT * g + j + 1)
                        last = pairs(pv_bank[:, :], v_hi[:, j, :], v_lo[:, j, :], pt_hi[j % 3], pt_lo[j % 3],
                                     j == 0, j == KT - 1)
                last.then_inc(s["pv_ready"], 1)

            def project_out(g):
                pe.wait_ge(s["wo_lo_ready"], g + 1)
                pe.wait_ge(s["attn_lo_ready"], g + 1)
                for h in range(HG):
                    last = pairs(oq_bank[:, :], attn_hi[:, h, :], attn_lo[:, h, :], wqo_hi[:, h, :], wqo_lo[:, h, :],
                                 h == 0, h == HG - 1)
                last.then_inc(s["oproj_ready"], 1)

            pe.wait_ge(s["consts_ready"], 4)
            transpose_norm(1)
            project_k_block(0, 0)
            project_q(0)
            project_k_block(0, 1)
            transpose_q(0)
            project_v_block(0, 0)
            project_k_block(0, 2)
            project_v_block(0, 1)
            project_k_block(0, 3)
            project_v_block(0, 2)
            project_v_block(0, 3)
            transpose_v_block(0, 0)
            transpose_v_block(0, 1)
            transpose_v_block(0, 2)
            with pe.Fori(0, G - 1) as g:
                scores(g)
                project_qk_and_first_v(g + 1)
                attend(g, False)
                transpose_v_block(g + 1, 0)
                project_v_block(g + 1, 3)
                transpose_v_block(g + 1, 1)
                project_out(g)
                transpose_v_block(g + 1, 2)
            scores(G - 1)
            attend(G - 1, True)
            pe.wait_ge(s["wo_lo_ready"], G)
            for dst, cols in zip((oq_bank, bank[0]), HALVES):
                for h in range(HG):
                    pe.wait_ge(s["attn_lo_ready"], G + h // 2)
                    last = pairs(dst[:, 0:DM // 2], attn_hi[:, h, :], attn_lo[:, h, :], wqo_hi[:, h, cols],
                                 wqo_lo[:, h, cols], h == 0, h == HG - 1)
                last.then_inc(s["o_half_mm"], 1)

            transpose_norm(2)
            pe.wait_ge(s["xnT_ready"], 1)
            pe.wait_ge(s["dt_in"], 16)
            for c in range(KC):
                last = pe.matmul(dt_bank[:, 0:MH], xnT[:, c, :], w_dt_sb[:, c, :], start=c == 0, stop=c == KC - 1)
            last.then_inc(s["dt_mm"], 1)

            def project_transposed(dst, w, done):
                for t in range(4):
                    for c in range(KC):
                        last = pe.matmul(dst[:, t * P:(t + 1) * P], w[:, c, t * P:(t + 1) * P], xnT[:, c, :],
                                         start=c == 0, stop=c == KC - 1)
                last.then_inc(done, 1)

            for i in range(BCC):
                ring, sem = (w_gate_sb, gate_in) if i < 2 else (w_out_sb, wout_in)
                pe.wait_ge(sem[i % 2], 16)
                project_transposed(bc_bank[i], ring[:, i % 2, :, :], s["bc_mm"])

            def segment_sums(n):
                for j in range(2):
                    at_least(pe, s["decay_ready"], 4 * n + j - 3)
                    pe.wait_ge(s["steps_even"], 2 * n + j + 1)
                    half = slice(4 * j, 4 * j + 4)
                    pe.matmul(segsum_bank[j][:, :], below_r[:, :],
                              steps_hi[:, half, :].rearrange("p h l -> p (h l)"), start=True, stop=False)
                    pe.matmul(segsum_bank[j][:, :], below_r[:, :],
                              steps_lo[:, half, :].rearrange("p h l -> p (h l)"), start=False, stop=True)\
                        .then_inc(s["even_mm"], 1)
                pe.wait_ge(s["dt_step"], 1)
                for j in range(2):
                    at_least(pe, s["decay_ready"], 4 * n + j - 1)
                    pe.wait_ge(s["steps_odd"], 2 * n + j + 1)
                    pe.matmul(segsum_bank[2 + j][:, :], below[:, :],
                              steps[:, 4 * j:4 * j + 4, :].rearrange("p h l -> p (h l)"),
                              start=True, stop=True).then_inc(s["odd_mm"], 1)

            pe.wait_ge(s["below_r_ready"], 1)
            segment_sums(0)
            with pe.Fori(1, CH // 2) as n:
                segment_sums(n)

            def hs_step(n, i):
                pe.wait_ge(hs_in[i], 16 * n + 16)
                if not (isinstance(n, int) and n == 0):
                    pe.wait_ge(s["hs_conv"], 12 * (2 * n + i - 1))
                project_transposed(bank[i], w_hs_sb[:, i, :, :], s["hs_mm"])

            def out_step(n, i):
                if isinstance(n, int) and n == CH // 2 - 1 and i == 1:
                    pe.wait_ge(s["last_wout_lo"], 2)
                else:
                    pe.wait_ge(s["wout_lo_ready"], 2 * n + i + 1)
                if not (isinstance(n, int) and n == CH // 2 - 1):
                    pe.wait_ge(s["ygT_lo_ready"], 4 * (2 * n + i + 1))
                if i == 0:
                    at_least(pe, s["out_added"], n)
                if isinstance(n, int) and n == CH // 2 - 1:
                    for dst, cols in zip((bank[6], bank[0]), HALVES):
                        for t in range(4):
                            pe.wait_ge(s["ygT_lo_ready"], 4 * (2 * n + i) + t + 1)
                            last = pairs(dst[:, 0:DM // 2], y_gT_hi[:, t, :], y_gT_lo[:, t, :], w_out_hi[:, i, t, cols],
                                         w_out_lo[:, i, t, cols], i == 0 and t == 0, i == 1 and t == 3)
                        if i == 1:
                            last.then_inc(s["out_half_mm"], 1)
                    if i == 0:
                        last.then_inc(s["out_mm"], 1)
                    return
                for t in range(4):
                    last = pairs(bank[6][:, :], y_gT_hi[:, t, :], y_gT_lo[:, t, :], w_out_hi[:, i, t, :],
                                 w_out_lo[:, i, t, :], i == 0 and t == 0, i == 1 and t == 3)
                last.then_inc(s["out_mm"], 1)

            def chunk_step(n, i, first, last_chunk):
                c = 2 * n + i
                if not last_chunk and not (isinstance(n, int) and n == 0):
                    hs_step(n + i, 1 - i)
                pe.wait_ge(s["hs_act"], c + 1)
                at_least(pe, s["x_ready"], c)
                for t in range(4):
                    last = pe.transpose(bank[3][:, t * P:(t + 1) * P], hsT[:, i, t, :], ident[:, :])
                last.then_inc(s["hsT_mm"], 1)
                if first:
                    pe.wait_ge(s["xnT_lo_ready"], 1)
                    pe.wait_ge(s["first_gate_lo"], 2)
                else:
                    pe.wait_ge(s["gate_lo_ready"], c)
                at_least(pe, s["gate_act"], c)
                for k in range(KC):
                    last = pairs(bank[2][:, :], xnT_hi[:, k, :], xnT_lo[:, k, :], w_gate_hi[:, k, :],
                                 w_gate_lo[:, i, k, :], k == 0, k == KC - 1)
                last.then_inc(s["gate_mm"], 1)
                pe.wait_ge(s["x_ready"], c + 1)
                pe.wait_ge(s["m_ready"], c + 1)
                at_least(pe, s["y_sum"], c)
                for h in range(HC):
                    last = pe.matmul(bank[4][:, h * PH:(h + 1) * PH], m_t[:, i, h, :], x_dt[:, i, h, :],
                                     start=True, stop=True)
                last.then_inc(s["y_mm"], 1)
                if not first:
                    out_step(n + i - 1, 1 - i)
                else:
                    hs_step(1, 0)
                pe.wait_ge(s["y_gated"], c + 1)
                if not (isinstance(n, int) and n == 0 and i == 0):
                    pe.wait_ge(s["ygT_lo_ready"], 4 * c)
                for t in range(4):
                    last = pe.transpose(ygT_bank(t, last_chunk)[:, t * P:(t + 1) * P], y[:, i, t * P:(t + 1) * P],
                                        ident[:, :])
                last.then_inc(s["ygT_mm"], 1)

            pe.wait_ge(s["bc_tap"], 4)
            pe.wait_ge(s["bc_conv"], 4)
            hs_step(0, 0)
            pe.wait_ge(s["decay_ready"], 2 * CH)
            hs_step(0, 1)
            pe.wait_ge(s["bc_act_ready"], BCC)
            pe.wait_ge(s["decay_ready"], 2 * CH)
            for g in range(G):
                last = pe.matmul(bank[5 + g // 4][:, (g % 4) * P:(g % 4 + 1) * P], bc_act[:, g, :], bc_act[:, 8 + g, :],
                                 start=True, stop=True)
            last.then_inc(s["g_mm"], 1)

            pe.wait_ge(s["gm_ready"], 2)
            chunk_step(0, 0, True, False)
            chunk_step(0, 1, False, False)
            with pe.Fori(1, CH // 2 - 1) as n:
                chunk_step(n, 0, False, False)
                chunk_step(n, 1, False, False)
            chunk_step(CH // 2 - 1, 0, False, False)
            chunk_step(CH // 2 - 1, 1, False, True)
            out_step(CH // 2 - 1, 1)

            def transpose_weights(c):
                for o in range(KC):
                    last = pe.transpose(bank[1 + c][:, o * P:(o + 1) * P], weights[:, o, c * P:(c + 1) * P],
                                        ident[:, :])
                last.then_inc(s["wT_mm"], 1)

            pe.wait_ge(s["weights_ready"], 1)
            transpose_weights(0)
            transpose_weights(1)
            transpose_norm(3)
            transpose_weights(2)
            transpose_weights(3)
            pe.wait_ge(s["xnT_ready"], 2)
            for dst, cols in zip((bank[5], bank[0]), HALVES):
                for c in range(KC):
                    pe.wait_ge(s["wT_ready"], c + 1)
                    last = pe.matmul(dst[:, 0:DM // 2], xnT[:, c, :], wT[:, c, cols], start=c == 0, stop=c == KC - 1)
                last.then_inc(s["ffn_mm"], 1)

        @block.scalar
        def _(act):
            def wq_high(g):
                act.wait_ge(s["wq_in"], 16 * (g + 1))
                act.activation(wqo_hi[:, :, :], wqo_raw[:, :, :], ACT.Copy).then_inc(s["wq_hi_ready"], 1)

            def wo_high(g):
                act.wait_ge(s["wo_in"], 16 * (g + 1))
                act.activation(wqo_hi[:, :, :], wqo_raw[:, :, :], ACT.Copy).then_inc(s["wo_hi_ready"], 1)

            def attn_high(g):
                act.wait_ge(s["attn_out_ready"], g + 1)
                act.activation(attn_hi[:, :, :].rearrange("p h t -> p (h t)"), probs[:, 1, 0:512], ACT.Copy)\
                    .then_inc(s["attn_hi_ready"], 1)

            def q_high(g):
                act.wait_ge(s["qT_mm"], g + 1)
                act.activation(qT_hi[:, :, :].rearrange("p h t -> p (h t)"), ring_b[0][:, :], ACT.Copy)\
                    .then_inc(s["qT_hi_ready"], 1)

            def k_high(g, b):
                act.wait_ge(s["krope_add"], KB * g + b + 1)
                act.activation(k_hi[:, b * 512:(b + 1) * 512], rope_a[:, (b + 1) % 2, :], ACT.Copy)\
                    .then_inc(s["k_hi_ready"], 1)

            def q_and_k_high(g):
                k_high(g, 0)
                q_high(g)
                k_high(g, 1)
                wo_high(g - 1)
                k_high(g, 2)
                k_high(g, 3)

            def v_copy(g, b):
                act.wait_ge(s["vproj_ready"], KB * g + max(b, 2 * (b % 2)) + 1)
                act.wait_ge(s["krope_add"], KB * g + KB)
                if b >= 2:
                    act.wait_ge(s["vT_mm"], KB * g + b - 1)
                act.activation(rope_b[:, b % 2, :], ring_a[b][:, :], ACT.Copy).then_inc(s["v_copied"], 1)

            def v_high(g, b):
                act.wait_ge(s["vT_mm"], KB * g + b + 1)
                act.activation(v_hi[:, 4 * b:4 * b + 4, :].rearrange("p t d -> p (t d)"), ring_b[b % 2][:, :],
                               ACT.Copy).then_inc(s["v_hi_ready"], 1)

            def v_rest(g):
                for b in range(KB - 1):
                    v_high(g, b)
                    if b == 0 and not (isinstance(g, int) and g == 0):
                        attn_high(g - 1)
                    if b + 2 < KB:
                        v_copy(g, b + 2)

            def last_exp_block(b):
                h, blk = HG - 1, slice(b * 512, (b + 1) * 512)
                act.activation(probs[:, h, blk], probs[:, h, blk], ACT.Exp, bias=neg_max[:, h:h + 1],
                               accum_out=block_max[:, h, b:b + 1]).then_inc(s["last_exp"], 1)

            def exps(g, last_head):
                for h in range(HG):
                    act.wait_ge(s["neg_max_ready"], HG * g + h + 1)
                    if last_head and h == HG - 1:
                        last_exp_block(0)
                        continue
                    act.activation(probs[:, h, :], probs[:, h, :], ACT.Exp, bias=neg_max[:, h:h + 1],
                                   accum_out=row_sum[:, h:h + 1]).then_inc(s["probs_ready"], 1)

            def pt_high(g, last_head):
                for t in range(KT):
                    if t == 2:
                        act.wait_ge(s["k_lo_ready"], KB * (g + (1 if last_head else 2)))
                    if last_head and t % 4 == 2 and t // 4 < KB - 1:
                        last_exp_block(t // 4 + 1)
                    act.wait_ge(s["pT_mm"], KT * g + t + 1)
                    act.activation(pt_hi[t % 3], ring_b[(t + 1) % 2][:, :], ACT.Copy).then_inc(s["pt_hi_ready"], 1)
                    if t == sum_steps(last_head)[3]:
                        act.wait_ge(s["bcast_mm"], g + 1)
                        act.activation(probs[:, 2, 0:512], oq_bank[:, :], ACT.Copy).then_inc(s["bcast_ready"], 1)
                if not last_head:
                    v_copy(g + 1, 1)

            def ctx_high(b, pieces=slice(0, KC)):
                act.activation(ctx_hi[:, pieces, b * 512:(b + 1) * 512], ctx_raw[:, b, pieces, :], ACT.Copy)\
                    .then_inc(s["ctx_hi_ready"], 1)

            act.wait_ge(first_ctx_in[0], 16)
            ctx_high(0, PAIRS[0])
            act.wait_ge(s["xnT_mm"], 1)
            act.activation(qx_hi[:, :, :].rearrange("p c t -> p (c t)"), oq_bank[:, :], ACT.Copy)\
                .then_inc(s["qx_hi_ready"], 1)
            act.wait_ge(first_ctx_in[1], 16)
            ctx_high(0, PAIRS[1])
            act.wait_ge(s["wq_in"], 16)
            for two, done in zip(PAIRS, (s["first_wq_hi"], s["wq_hi_ready"])):
                act.activation(wqo_hi[:, two, :], wqo_raw[:, two, :], ACT.Copy).then_inc(done, 1)
            act.wait_ge(ctx_in[1], 16)
            ctx_high(1, PAIRS[0])
            ctx_high(1, PAIRS[1])
            act.wait_ge(ctx_in[2], 16)
            ctx_high(2)
            k_high(0, 0)
            q_high(0)
            act.wait_ge(ctx_in[3], 16)
            ctx_high(3)
            k_high(0, 1)
            k_high(0, 2)
            k_high(0, 3)
            v_copy(0, 0)
            v_copy(0, 1)
            v_rest(0)
            with act.Fori(0, G - 1) as g:
                v_high(g, KB - 1)
                wq_high(g + 1)
                exps(g, False)
                q_and_k_high(g + 1)
                v_copy(g + 1, 0)
                pt_high(g, False)
                v_rest(g + 1)
            v_high(G - 1, KB - 1)
            wo_high(G - 1)
            exps(G - 1, True)
            pt_high(G - 1, True)
            for i in range(2):
                act.wait_ge(s["attn_out_ready"], G + i)
                act.activation(attn_hi[:, 2 * i:2 * i + 2, :].rearrange("p h t -> p (h t)"),
                               probs[:, 1, 256 * i:256 * (i + 1)], ACT.Copy).then_inc(s["attn_hi_ready"], 1)

            act.wait_ge(s["xnT_mm"], 2)
            act.activation(xnT[:, :, :].rearrange("p c t -> p (c t)"), oq_bank[:, :], ACT.Copy)\
                .then_inc(s["xnT_ready"], 1)
            act.wait_ge(s["xnT_ready"], 1)
            act.activation(xnT_hi[:, :, :], xnT[:, :, :], ACT.Copy).then_inc(s["xnT_hi_ready"], 1)
            act.wait_ge(s["small_in"], 96)
            act.activation(alog_bc[:, :], alog_bc[:, :], ACT.Exp).then_inc(s["neg_a"], 1)
            act.wait_ge(s["dt_step"], 2)
            act.activation(dt_t[:, 1, :], dt_t[:, 0, :], ACT.Exp).then_inc(s["dt_act"], 1)
            act.wait_ge(s["dt_act"], 1)
            act.activation(dt_t[:, 2, :], dt_t[:, 1, :], ACT.Ln, bias=1.0).then_inc(s["dt_act"], 1)
            for i in range(BCC):
                act.wait_ge(s["bc_mm"], i + 1)
                for t in range(4):
                    tile = 4 * i + t
                    act.activation(bc_acc[:, tile, :], bc_bank[i][:, t * P:(t + 1) * P], ACT.Identity,
                                   bias=cb[:, INTER // P + tile:INTER // P + tile + 1],
                                   scale=cw[:, INTER // P + tile, 3:4]).then_inc(s["bc_tap"], 1)

            def decays(n):
                for i in range(2):
                    for j in range(2):
                        act.wait_ge(s["odd_mm" if i else "even_mm"], 2 * n + j + 1)
                        act.activation(
                            decay[:, bass.ds(16 * n + 8 * i + 4 * j, 4), :].rearrange("p h l -> p (h l)"),
                            segsum_bank[2 * i + j][:, :], ACT.Exp).then_inc(s["decay_ready"], 1)

            decays(0)
            with act.Fori(1, CH // 2) as n:
                decays(n)
            for i in range(BCC):
                act.wait_ge(s["bc_conv"], 4 * (i + 1))
                act.activation(bc_act[:, 4 * i:4 * i + 4, :].rearrange("p t l -> p (t l)"),
                               bc_acc[:, 4 * i:4 * i + 4, :].rearrange("p t l -> p (t l)"), ACT.Silu)\
                    .then_inc(s["bc_act_ready"], 1)

            def gate_high(n, i):
                act.wait_ge(gate_in[i], 16 * n + 32)
                act.activation(w_gate_hi[:, :, :], w_gate_sb[:, i, :, :], ACT.Copy).then_inc(s["gate_hi_ready"], 1)

            def out_high(n, i):
                act.wait_ge(wout_in[i], 16 * n + 32)
                if isinstance(n, int) and n == 0:
                    if i == 0:
                        act.wait_ge(s["g_mm"], 1)
                else:
                    act.wait_ge(s["out_mm"], 2 * n + i - 1)
                act.activation(w_out_hi[:, i, :, :], w_out_sb[:, i, :, :], ACT.Copy).then_inc(s["wout_hi_ready"], 1)

            def tap_step(n, i):
                c = 2 * n + i
                act.wait_ge(s["hs_mm"], c + 1)
                if not (isinstance(n, int) and n == 0):
                    act.wait_ge(s["hs_act"], c - 1)
                for t in range(4):
                    act.activation(conv[:, i, t, :], bank[i][:, t * P:(t + 1) * P], ACT.Identity,
                                   bias=cb[:, bass.ds(4 * c + t, 1)],
                                   scale=cw[:, bass.ds(4 * c + t, 1), 3:4].rearrange("p a b -> p (a b)"))\
                        .then_inc(s["hs_tap"], 1)

            def silu_step(n, i):
                c = 2 * n + i
                act.wait_ge(s["hs_conv"], 12 * (c + 1))
                if not (isinstance(n, int) and n == 0):
                    act.wait_ge(s["hsT_mm"], c - 1)
                act.activation(hsT[:, i, :, :].rearrange("p t l -> p (t l)"),
                               conv[:, i, :, :].rearrange("p t l -> p (t l)"), ACT.Silu).then_inc(s["hs_act"], 1)

            def chunk_act(n, i, last_chunk):
                c = 2 * n + i
                if not last_chunk:
                    tap_step(n + i, 1 - i)
                act.wait_ge(s["gate_mm"], c + 1)
                if not (isinstance(n, int) and n == 0):
                    act.wait_ge(s["y_gated"], c - 1)
                act.activation(gate[:, i, :], bank[2][:, :], ACT.Silu).then_inc(s["gate_act"], 1)
                if not last_chunk:
                    gate_high(n + i, 1 - i)
                    silu_step(n + i, 1 - i)
                out_high(n, i)
                act.wait_ge(s["y_gated"], c + 1)
                if i == 0:
                    at_least(act, s["ms_sum"], n)
                if not (isinstance(n, int) and n == 0 and i == 0):
                    act.wait_ge(s["square_ready"], c)
                act.activation(bank[7][:, :], y[:, i, :], ACT.Square, accum_out=square_sum[:, i:i + 1])\
                    .then_inc(s["square_ready"], 1)
                act.wait_ge(s["ygT_mm"], c + 1)
                at_least(act, s["out_mm"], c)
                for t in range(4):
                    act.activation(y_gT_hi[:, t, :], ygT_bank(t, last_chunk)[:, t * P:(t + 1) * P], ACT.Identity,
                                   scale=nw[:, bass.ds(4 * c + t, 1)]).then_inc(s["ygT_hi_ready"], 1)

            tap_step(0, 0)
            act.wait_ge(s["bc_act_ready"], BCC)
            gate_high(0, 0)
            silu_step(0, 0)
            chunk_act(0, 0, False)
            chunk_act(0, 1, False)
            with act.Fori(1, CH // 2 - 1) as n:
                chunk_act(n, 0, False)
                chunk_act(n, 1, False)
            chunk_act(CH // 2 - 1, 0, False)
            chunk_act(CH // 2 - 1, 1, True)

            for c in range(KC):
                if c == 2:
                    act.wait_ge(s["xnT_mm"], 3)
                    act.activation(xnT[:, :, :].rearrange("p c t -> p (c t)"), oq_bank[:, :], ACT.Copy)\
                        .then_inc(s["xnT_ready"], 1)
                act.wait_ge(s["wT_mm"], c + 1)
                act.activation(wT[:, c, :], bank[1 + c][:, :], ACT.Copy).then_inc(s["wT_ready"], 1)

        @block.vector
        def _(dve):
            def half_stats(n, half):
                if n > 1:
                    dve.wait_ge(s["xres_half_added"], 2 * (n - 2) + half + 1)
                dve.bn_stats(stats[:, half, :], xres[:, HALVES[half]]).then_inc(s["norm_stats"], 1)

            def layer_norm(n):
                dve.wait_ge(s["norm_stats"], 2 * n)
                dve.bn_aggr(mean_var[:, :], stats[:, :, :].rearrange("p a b -> p (a b)")).then_inc(s["norm_agg"], 1)
                dve.wait_ge(s["norm_rstd"], n)
                dve.tensor_scalar(xn[:, :], xres[:, :], mean_var[:, 0:1], rstd[:, 0:1], ALU.subtract, ALU.mult)\
                    .then_inc(s["xn_ready"], 1)

            def k_rotate(g, b):
                blk, slot = slice(b * 512, (b + 1) * 512), (b + 1) % 2
                dve.wait_ge(s["kproj_ready"], KB * g + b + 1)
                if b == 0 and not (isinstance(g, int) and g == 0):
                    dve.wait_ge(s["k_lo_ready"], KB * g)
                    dve.wait_ge(s["vT_mm"], KB * g)
                if b == 1:
                    dve.wait_ge(s["qT_mm"], g + 1)
                if b >= 2:
                    dve.wait_ge(s["k_lo_ready"], KB * g + b - 1)
                dve.tensor_tensor(rope_a[:, slot, :], ring_a[b][:, :], cos_k[:, blk], ALU.mult)
                dve.tensor_tensor(rope_b[0:64, slot, :], ring_a[b][64:128, :], sin_k[64:128, blk], ALU.mult)
                dve.tensor_tensor(rope_b[64:128, slot, :], ring_a[b][0:64, :], sin_k[0:64, blk], ALU.mult)\
                    .then_inc(s["krope_mul"], 1)
                dve.wait_ge(s["krope_mul"], KB * g + b + 1)
                dve.tensor_tensor(rope_a[:, slot, :], rope_a[:, slot, :], rope_b[:, slot, :], ALU.add)\
                    .then_inc(s["krope_add"], 1)

            def q_rotate(g):
                dve.wait_ge(s["qproj_ready"], g + 1)
                q = oq_bank[:, :].rearrange("p (h two d) -> p h two d", h=HG, two=2)
                qb = rope_b[:, 0, :].rearrange("p (h two d) -> p h two d", h=HG, two=2)
                cos = cos_q[:, :].unsqueeze(1).broadcast_to([P, 2 * HG, DH // 2])
                sin = sin_q[:, :].unsqueeze(1).broadcast_to([P, HG, DH // 2])
                dve.tensor_tensor(rope_a[:, 0, :].rearrange("p (h d) -> p h d", d=DH // 2),
                                  oq_bank[:, :].rearrange("p (h d) -> p h d", d=DH // 2), cos, ALU.mult)
                dve.scalar_tensor_tensor(qb[:, :, 0, :], q[:, :, 1, :], -1.0, sin, ALU.mult, ALU.mult)
                dve.tensor_tensor(qb[:, :, 1, :], q[:, :, 0, :], sin, ALU.mult).then_inc(s["qrope_mul"], 1)
                dve.wait_ge(s["qrope_mul"], g + 1)
                dve.tensor_tensor(rope_a[:, 0, :], rope_a[:, 0, :], rope_b[:, 0, :], ALU.add)\
                    .then_inc(s["qrope_add"], 1)

            def q_low(g):
                dve.wait_ge(s["qT_hi_ready"], g + 1)
                dve.tensor_tensor(qT_lo[:, :, :].rearrange("p h t -> p (h t)"), ring_b[0][:, :],
                                  qT_hi[:, :, :].rearrange("p h t -> p (h t)").bitcast(F32), ALU.subtract)\
                    .then_inc(s["qT_lo_ready"], 1)

            def q_and_k(g):
                k_rotate(g, 0)
                q_rotate(g)
                k_rotate(g, 1)
                q_low(g)
                k_rotate(g, 2)
                k_rotate(g, 3)

            def v_low(g, b):
                dve.wait_ge(s["v_hi_ready"], KB * g + b + 1)
                dve.tensor_tensor(v_lo[:, 4 * b:4 * b + 4, :].rearrange("p t d -> p (t d)"), ring_b[b % 2][:, :],
                                  v_hi[:, 4 * b:4 * b + 4, :].rearrange("p t d -> p (t d)").bitcast(F32),
                                  ALU.subtract).then_inc(s["v_lo_ready"], 1)

            def row_max(g, h):
                dve.wait_ge(s["scores_masked"], HG * KB * g + KB * (h + 1))
                dve.tensor_reduce(neg_max[:, h:h + 1], block_max[:, h, :], X_AXIS, ALU.max, negate=True)\
                    .then_inc(s["neg_max_ready"], 1)

            def mask_scores(g):
                for h in range(HG):
                    for b in range(KB):
                        dve.wait_ge(s["mask_in"], 16)
                        dve.wait_ge(s["scores_ready"], HG * KB * g + KB * h + b + 1)
                        keep_wait_apart(dve)
                        dve.tensor_tensor_reduce(
                            out=probs[:, h, b * 512:(b + 1) * 512], in0=ring_a[b][:, :],
                            in1=mask_sb[:, b * 512:(b + 1) * 512], scale=1.0, scalar=LOWEST, op0=ALU.add, op1=ALU.max,
                            accum_out=block_max[:, h, b:b + 1]).then_inc(s["scores_masked"], 1)
                        if b == 0 and h > 0:
                            row_max(g, h - 1)
                    if h == 0:
                        v_low(g, KB - 1)
                row_max(g, HG - 1)

            def inverse_sums(g, last_head):
                dve.wait_ge(s["probs_ready"], HG * (g + 1) - last_head)
                if last_head:
                    dve.wait_ge(s["last_exp"], KB)
                    dve.tensor_reduce(row_sum[:, HG - 1:HG], block_max[:, HG - 1, :], X_AXIS, ALU.add)\
                        .then_inc(s["last_sum_ready"], 1)
                    dve.wait_ge(s["last_sum_ready"], 1)
                dve.reciprocal(inv_sum[:, :], row_sum[:, :]).then_inc(s["inv_sum_ready"], 1)
                dve.wait_ge(s["inv_sum_ready"], g + 1)
                dve.tensor_scalar(inv_hi[:, :], inv_sum[:, :], 1.0, None, ALU.mult).then_inc(s["inv_hi_ready"], 1)
                dve.wait_ge(s["inv_hi_ready"], g + 1)
                dve.tensor_tensor(inv_lo[:, :], inv_sum[:, :], inv_hi[:, :].bitcast(F32), ALU.subtract)\
                    .then_inc(s["inv_lo_ready"], 1)
                dve.wait_ge(s["k_lo_ready"], KB * (g + (1 if last_head else 2)))
                dve.tensor_tensor(diag_hi[:, :, :], ident[:, :].unsqueeze(1).broadcast_to([P, HG, P]),
                                  inv_hi[:, :].bitcast(F32).unsqueeze(2).broadcast_to([P, HG, P]), ALU.mult)

            def inverse_sums_low(g):
                dve.wait_ge(s["inv_lo_ready"], g + 1)
                dve.wait_ge(s["pT_mm"], KT * g + 1)
                dve.tensor_tensor(diag_lo, ident[:, :].unsqueeze(1).broadcast_to([P, HG, P]),
                                  inv_lo[:, :].bitcast(F32).unsqueeze(2).broadcast_to([P, HG, P]), ALU.mult)\
                    .then_inc(s["diag_ready"], 1)

            def pt_low(g, last_head):
                for t in range(KT):
                    dve.wait_ge(s["pt_hi_ready"], KT * g + t + 1)
                    dve.tensor_tensor(pt_lo[t % 3], ring_b[(t + 1) % 2][:, :], pt_hi[t % 3].bitcast(F32), ALU.subtract)\
                        .then_inc(s["pt_lo_ready"], 1)
                    if t == sum_steps(last_head)[0]:
                        inverse_sums(g, last_head)
                    if t == sum_steps(last_head)[1]:
                        inverse_sums_low(g)

            def scale_out(g):
                dve.wait_ge(s["bcast_ready"], g + 1)
                dve.wait_ge(s["pv_ready"], g + 1)
                dve.tensor_tensor(probs[:, 1, 0:512], pv_bank[:, :], probs[:, 2, 0:512], ALU.mult)\
                    .then_inc(s["attn_out_ready"], 1)

            def add_out(g):
                dve.wait_ge(s["oproj_ready"], g + 1)
                dve.tensor_tensor(xres[:, :], xres[:, :], oq_bank[:, :], ALU.add).then_inc(s["res_added"], 1)
                dve.wait_ge(s["res_added"], g + 1)

            def attn_low(g):
                dve.wait_ge(s["attn_hi_ready"], g + 1)
                dve.tensor_tensor(attn_lo[:, :, :].rearrange("p h t -> p (h t)"), probs[:, 1, 0:512],
                                  attn_hi[:, :, :].rearrange("p h t -> p (h t)").bitcast(F32), ALU.subtract)\
                    .then_inc(s["attn_lo_ready"], 1)

            dve.wait_ge(s["x_in"], 16)
            half_stats(1, 0)
            half_stats(1, 1)
            layer_norm(1)
            def ctx_low(b, i, pieces=slice(0, KC)):
                dve.wait_ge(s["ctx_hi_ready"], i)
                dve.tensor_tensor(ctx_lo[:, pieces, b * 512:(b + 1) * 512], ctx_raw[:, b, pieces, :],
                                  ctx_hi[:, pieces, b * 512:(b + 1) * 512].bitcast(F32), ALU.subtract)\
                    .then_inc(s["ctx_lo_ready"], 1)

            def first_k_rotate(b):
                dve.wait_ge(rope_k_in[b], 32)
                k_rotate(0, b)

            ctx_low(0, 1, PAIRS[0])
            dve.wait_ge(s["qx_hi_ready"], 1)
            dve.tensor_tensor(qx_lo[:, :, :].rearrange("p c t -> p (c t)"), oq_bank[:, :],
                              qx_hi[:, :, :].rearrange("p c t -> p (c t)").bitcast(F32), ALU.subtract)\
                .then_inc(s["qx_lo_ready"], 1)
            ctx_low(0, 2, PAIRS[1])
            for two, high, low in zip(PAIRS, ("first_wq_hi", "wq_hi_ready"), ("first_wq_lo", "wq_lo_ready")):
                dve.wait_ge(s[high], 1)
                dve.tensor_tensor(wqo_lo[:, two, :], wqo_raw[:, two, :], wqo_hi[:, two, :].bitcast(F32), ALU.subtract)\
                    .then_inc(s[low], 1)
            ctx_low(1, 3, PAIRS[0])
            ctx_low(1, 4, PAIRS[1])
            first_k_rotate(0)
            dve.wait_ge(s["tables_in"], 32)
            q_rotate(0)
            ctx_low(2, 5)
            first_k_rotate(1)
            q_low(0)
            ctx_low(3, 6)
            first_k_rotate(2)
            first_k_rotate(3)
            for b in range(KB - 1):
                v_low(0, b)
            with dve.Fori(0, G - 1) as g:
                mask_scores(g)
                q_and_k(g + 1)
                pt_low(g, False)
                scale_out(g)
                v_low(g + 1, 0)
                attn_low(g)
                v_low(g + 1, 1)
                add_out(g)
                v_low(g + 1, 2)
            mask_scores(G - 1)
            pt_low(G - 1, True)
            dve.wait_ge(s["bcast_ready"], G)
            dve.wait_ge(s["pv_ready"], G)
            for i in range(2):
                two = slice(256 * i, 256 * (i + 1))
                dve.tensor_tensor(probs[:, 1, two], pv_bank[:, two], probs[:, 2, two], ALU.mult)\
                    .then_inc(s["attn_out_ready"], 1)
            for i in range(2):
                two = slice(2 * i, 2 * i + 2)
                dve.wait_ge(s["attn_hi_ready"], G + i)
                dve.tensor_tensor(attn_lo[:, two, :].rearrange("p h t -> p (h t)"), probs[:, 1, 256 * i:256 * (i + 1)],
                                  attn_hi[:, two, :].rearrange("p h t -> p (h t)").bitcast(F32), ALU.subtract)\
                    .then_inc(s["attn_lo_ready"], 1)
            for half, src in enumerate((oq_bank, bank[0])):
                cols = HALVES[half]
                dve.wait_ge(s["o_half_mm"], half + 1)
                dve.tensor_tensor(xres[:, cols], xres[:, cols], src[:, 0:DM // 2], ALU.add)\
                    .then_inc(s["xres_half_added"], 1)
                half_stats(2, half)

            layer_norm(2)
            dve.wait_ge(s["small_in"], 96)
            dve.wait_ge(s["dt_mm"], 1)
            dve.tensor_tensor(dt_x[:, :], dt_bank[:, 0:MH], dtb_bc[:, :], ALU.add).then_inc(s["dt_step"], 1)
            dve.wait_ge(s["dt_step"], 1)
            dve.scalar_tensor_tensor(dt_t[:, 0, :], dt_x[:, :], -1.0, dt_x[:, :], ALU.mult, ALU.min)\
                .then_inc(s["dt_step"], 1)
            dve.wait_ge(s["xnT_hi_ready"], 1)
            dve.tensor_tensor(xnT_lo[:, :, :], xnT[:, :, :], xnT_hi[:, :, :].bitcast(F32), ALU.subtract)\
                .then_inc(s["xnT_lo_ready"], 1)
            dve.wait_ge(s["dt_act"], 1)
            dve.tensor_scalar(dt[:, :], dt_t[:, 1, :], 1.0, -1.0, ALU.add, ALU.add).then_inc(s["dt_step"], 1)
            dve.wait_ge(s["dt_step"], 3)
            dve.tensor_scalar(dt_t[:, 3, :], dt[:, :], 0.0, None, ALU.is_equal).then_inc(s["dt_step"], 1)
            dve.wait_ge(s["dt_step"], 4)
            dve.tensor_tensor(dt[:, :], dt[:, :], dt_t[:, 3, :], ALU.add).then_inc(s["dt_step"], 1)
            dve.wait_ge(s["dt_step"], 5)
            dve.reciprocal(dt[:, :], dt[:, :]).then_inc(s["dt_step"], 1)
            dve.wait_ge(s["dt_step"], 6)
            dve.wait_ge(s["dt_act"], 2)
            dve.tensor_tensor(dt_t[:, 2, :], dt_t[:, 2, :], dt[:, :], ALU.mult).then_inc(s["dt_step"], 1)
            dve.wait_ge(s["dt_step"], 7)
            dve.tensor_tensor(dt_t[:, 2, :], dt_t[:, 2, :], dt_t[:, 3, :], ALU.add).then_inc(s["dt_step"], 1)
            dve.wait_ge(s["dt_step"], 8)
            dve.tensor_tensor(dt_t[:, 2, :], dt_t[:, 2, :], dt_t[:, 1, :], ALU.mult).then_inc(s["dt_step"], 1)
            dve.wait_ge(s["dt_step"], 9)
            dve.scalar_tensor_tensor(dt[:, :], dt_x[:, :], 0.0, dt_t[:, 2, :], ALU.max, ALU.add)\
                .then_inc(s["dt_step"], 1)
            dve.wait_ge(s["dt_step"], 10)
            dve.wait_ge(s["neg_a"], 1)
            dve.scalar_tensor_tensor(a_dt[:, :], dt[:, :], -1.0, alog_bc[:, :], ALU.mult, ALU.mult)\
                .then_inc(s["a_dt_ready"], 1)
            dve.wait_ge(s["a_dt_ready"], 1)

            dve.tensor_copy(a_hi[:, :], a_dt[:, :]).then_inc(s["a_hi_ready"], 1)
            dve.wait_ge(s["a_hi_ready"], 1)
            dve.tensor_tensor(a_lo[:, :], a_dt[:, :], a_hi[:, :].bitcast(F32), ALU.subtract)\
                .then_inc(s["a_lo_ready"], 1)
            dve.wait_ge(s["a_lo_ready"], 1)

            def steps_half(n, j):
                half, heads = slice(4 * j, 4 * j + 4), slice(2 * HC * n + 4 * j, 2 * HC * n + 4 * j + 4)
                if n > 0:
                    dve.wait_ge(s["even_mm"], 2 * (n - 1) + j + 1)
                for part, a_part in ((steps_hi, a_hi), (steps_lo, a_lo)):
                    last = dve.tensor_tensor(part[:, half, :], upper[:, :].unsqueeze(1).broadcast_to([P, 4, P]),
                                             a_part[:, heads].bitcast(F32).unsqueeze(2).broadcast_to([P, 4, P]),
                                             ALU.mult)
                last.then_inc(s["steps_even"], 1)

            def bc_taps(i, steps_between=()):
                dve.wait_ge(s["bc_tap"], 4 * (i + 1))
                for k in range(1, TAPS):
                    if k > 1:
                        dve.wait_ge(s["bc_tap_added"], 4 * (2 * i + k - 1))
                    for t in range(4):
                        tile = 4 * i + t
                        dve.scalar_tensor_tensor(
                            bc_acc[:, tile, k:], bc_bank[i][:, t * P:t * P + P - k],
                            cw[:, INTER // P + tile, TAPS - 1 - k:TAPS - k], bc_acc[:, tile, k:], ALU.mult, ALU.add)\
                            .then_inc(s["bc_tap_added" if k < TAPS - 1 else "bc_conv"], 1)
                    for n, j in steps_between if k == 1 else ():
                        steps_half(n, j)

            steps_half(0, 0)
            steps_half(0, 1)
            bc_taps(0)
            bc_taps(1)
            steps_half(1, 0)
            steps_half(1, 1)
            bc_taps(2, [(n, j) for n in range(2, CH // 2) for j in range(2)])
            bc_taps(3)

            def make_gm():
                dve.wait_ge(s["g_mm"], 1)
                for j in range(2):
                    dve.tensor_tensor(gm[:, 4 * j:4 * j + 4, :],
                                      bank[5 + j][:, :].rearrange("p (g l) -> p g l", g=4),
                                      upper[:, :].unsqueeze(1).broadcast_to([P, 4, P]), ALU.mult)\
                        .then_inc(s["gm_ready"], 1)

            def digits_of_weights():
                dve.wait_ge(s["dequant_in"], 48)
                dve.wait_ge(s["m_ready"], CH // 2)
                dve.tensor_scalar(digits[:, :, :, 0], packed[:, :, :], 15, None, ALU.bitwise_and)\
                    .then_inc(s["digits_ready"], 1)
                dve.tensor_scalar(digits[:, :, :, 1], packed[:, :, :], 4, None, ALU.arith_shift_right)\
                    .then_inc(s["digits_ready"], 1)

            def subtract_zeros(rows):
                dve.wait_ge(s["digits_ready"], 2)
                for o in rows:
                    dve.tensor_tensor(weights[:, o, :].rearrange("p (g k) -> p g k", g=QG),
                                      digits[:, o, :, :].rearrange("p (g k) two -> p g (k two)", g=QG),
                                      zero_sb[:, o, :].unsqueeze(2).broadcast_to([P, QG, DM // QG]), ALU.subtract)\
                        .then_inc(s["digits_off"], 1)

            def scale_weights():
                dve.wait_ge(s["digits_off"], KC)
                for o in range(KC):
                    last = dve.tensor_tensor(weights[:, o, :].rearrange("p (g k) -> p g k", g=QG),
                                             weights[:, o, :].rearrange("p (g k) -> p g k", g=QG),
                                             scale_sb[:, o, :].unsqueeze(2).broadcast_to([P, QG, DM // QG]), ALU.mult)
                last.then_inc(s["weights_ready"], 1)

            def gate_low(n, i):
                dve.wait_ge(s["gate_hi_ready"], 2 * n + i + 1)
                dve.tensor_tensor(w_gate_lo[:, i, :, :], w_gate_sb[:, i, :, :], w_gate_hi[:, :, :].bitcast(F32),
                                  ALU.subtract).then_inc(s["gate_lo_ready"], 1)

            def ygT_low(n, i, last_chunk=False):
                c = 2 * n + i
                for t in range(4):
                    if last_chunk or t == 0:
                        dve.wait_ge(s["ygT_hi_ready"], 4 * c + (2 * (t // 2 + 1) if last_chunk else 4))
                    dve.scalar_tensor_tensor(y_gT_lo[:, t, :], ygT_bank(t, last_chunk)[:, t * P:(t + 1) * P],
                                             nw[:, bass.ds(4 * c + t, 1)], y_gT_hi[:, t, :].bitcast(F32),
                                             ALU.mult, ALU.subtract).then_inc(s["ygT_lo_ready"], 1)

            def conv_step(n, i):
                c = 2 * n + i
                dve.wait_ge(s["hs_tap"], 4 * (c + 1))
                for k in range(1, TAPS):
                    if k > 1:
                        dve.wait_ge(s["hs_conv"], 12 * c + 4 * (k - 1))
                    for t in range(4):
                        w = cw[:, bass.ds(4 * c + t, 1), TAPS - 1 - k:TAPS - k].rearrange("p a b -> p (a b)")
                        dve.scalar_tensor_tensor(conv[:, i, t, k:], bank[i][:, t * P:t * P + P - k], w,
                                                 conv[:, i, t, k:], ALU.mult, ALU.add).then_inc(s["hs_conv"], 1)

            def add_group(n):
                dve.wait_ge(s["out_mm"], 2 * (n + 1))
                dve.wait_ge(s["scale_ready"], n + 1)
                dve.scalar_tensor_tensor(xres[:, :], bank[6][:, :], group_scale[:, 0:1], xres[:, :], ALU.mult, ALU.add)\
                    .then_inc(s["out_added"], 1)
                dve.wait_ge(s["out_added"], n + 1)

            def chunk_dve(n, i, first_group, last_chunk):
                c = 2 * n + i
                last_but_one = isinstance(n, int) and n == CH // 2 - 1 and i == 0
                dve.wait_ge(s["hsT_mm"], c + 1)
                if not first_group:
                    dve.wait_ge(s["y_mm"], c - 1)
                hs = bank[3][:, :].rearrange("p (h d) -> p h d", h=HC)
                dve.tensor_tensor(x_dt[:, i, :, :], hs, dt[:, bass.ds(HC * c, HC)].unsqueeze(2)
                                  .broadcast_to([P, HC, PH]), ALU.mult)
                dve.tensor_tensor(x_skip[:, i, :].rearrange("p (h d) -> p h d", h=HC), hs,
                                  d_bc[:, bass.ds(HC * c, HC)].unsqueeze(2).broadcast_to([P, HC, PH]), ALU.mult)\
                    .then_inc(s["x_ready"], 1)
                if last_chunk:
                    ygT_low(n, 0)
                    add_group(n - 1)
                    subtract_zeros((0, 1))
                else:
                    conv_step(n + i, 1 - i)
                dve.wait_ge(s["y_mm"], c + 1)
                dve.wait_ge(s["x_ready"], c + 1)
                if not first_group:
                    dve.wait_ge(s["ygT_mm"], c - 1)
                    dve.wait_ge(s["square_ready"], c - 1)
                dve.tensor_tensor(y[:, i, :], bank[4][:, :], x_skip[:, i, :], ALU.add).then_inc(s["y_sum"], 1)
                dve.wait_ge(s["y_sum"], c + 1)
                dve.wait_ge(s["gate_act"], c + 1)
                dve.tensor_tensor(y[:, i, :], y[:, i, :], gate[:, i, :], ALU.mult).then_inc(s["y_gated"], 1)
                if last_chunk:
                    dve.wait_ge(s["wout_hi_ready"], CH)
                    dve.tensor_tensor(w_out_lo[:, 1, PAIRS[1], :], w_out_sb[:, 1, PAIRS[1], :],
                                      w_out_hi[:, 1, PAIRS[1], :].bitcast(F32), ALU.subtract)\
                        .then_inc(s["last_wout_lo"], 1)
                    subtract_zeros((2, 3))
                else:
                    gate_low(n + i, 1 - i)
                if last_but_one:
                    return
                ygT_low(n, i, last_chunk)
                if i == 0 and not first_group:
                    add_group(n - 1)

            conv_step(0, 0)
            make_gm()
            dve.wait_ge(s["gate_hi_ready"], 1)
            dve.tensor_tensor(w_gate_lo[:, 0, PAIRS[1], :], w_gate_sb[:, 0, PAIRS[1], :],
                              w_gate_hi[:, PAIRS[1], :].bitcast(F32), ALU.subtract).then_inc(s["first_gate_lo"], 1)
            chunk_dve(0, 0, True, False)
            chunk_dve(0, 1, True, False)
            with dve.Fori(1, CH // 2 - 1) as n:
                chunk_dve(n, 0, False, False)
                chunk_dve(n, 1, False, False)
            digits_of_weights()
            chunk_dve(CH // 2 - 1, 0, False, False)
            chunk_dve(CH // 2 - 1, 1, False, True)
            scale_weights()
            dve.wait_ge(s["scale_ready"], CH // 2)
            for half, src in enumerate((bank[6], bank[0])):
                cols = HALVES[half]
                dve.wait_ge(s["out_half_mm"], half + 1)
                dve.scalar_tensor_tensor(xres[:, cols], src[:, 0:DM // 2], group_scale[:, 0:1], xres[:, cols],
                                         ALU.mult, ALU.add).then_inc(s["xres_half_added"], 1)
                half_stats(3, half)

            layer_norm(3)
            dve.wait_ge(s["xn_ready"], 3)
            dve.wait_ge(s["bias_in"], 16)
            dve.tensor_tensor(xres[:, :], xres[:, :], bias_bc[:, :], ALU.add).then_inc(s["ffn_bias"], 1)
            dve.wait_ge(s["ffn_bias"], 1)
            for half, src in enumerate((bank[5], bank[0])):
                cols = HALVES[half]
                dve.wait_ge(s["ffn_mm"], half + 1)
                dve.tensor_tensor(xres[:, cols], xres[:, cols], src[:, 0:DM // 2], ALU.add)\
                    .then_inc(s["ffn_added"], 1)

        @block.gpsimd
        def _(pool):
            def norm_scale(n):
                pool.wait_ge(s["norm_agg"], n)
                pool.tensor_scalar(var_eps[:, :], mean_var[:, 1:2], EPS, None, ALU.add).then_inc(s["norm_eps"], 1)
                pool.wait_ge(s["norm_eps"], n)
                pool.tensor_tensor(rstd[:, :], var_eps[:, :], half_neg[:, :], ALU.pow).then_inc(s["norm_rstd"], 1)

            def split_weight(raw, hi, lo, arrived, hi_done, lo_done, g):
                pool.wait_ge(arrived, 16 * (g + 1))
                keep_wait_apart(pool)
                pool.tensor_copy(hi[:, :, :], raw[:, :, :]).then_inc(hi_done, 1)
                pool.wait_ge(hi_done, g + 1)
                pool.tensor_tensor(lo[:, :, :], raw[:, :, :], hi[:, :, :].bitcast(F32), ALU.subtract)\
                    .then_inc(lo_done, 1)

            def k_low(g):
                for b in range(KB):
                    blk = slice(b * 512, (b + 1) * 512)
                    pool.wait_ge(s["k_hi_ready"], KB * g + b + 1)
                    pool.tensor_tensor(k_lo[:, blk], rope_a[:, (b + 1) % 2, :], k_hi[:, blk].bitcast(F32),
                                       ALU.subtract)\
                        .then_inc(s["k_lo_ready"], 1)

            def split_wk(g):
                split_weight(wk_raw, wk_hi, wk_lo, s["wk_in"], s["wk_hi_ready"], s["wk_lo_ready"], g)

            def split_wv(g):
                split_weight(wv_raw, wv_hi, wv_lo, s["wv_in"], s["wv_hi_ready"], s["wv_lo_ready"], g)

            def wqo_low(hi_ready, done, g):
                pool.wait_ge(hi_ready, g + 1)
                pool.tensor_tensor(wqo_lo[:, :, :], wqo_raw[:, :, :], wqo_hi[:, :, :].bitcast(F32), ALU.subtract)\
                    .then_inc(done, 1)

            pool.memset(half_neg[:, :], -0.5).then_inc(s["consts_ready"], 1)
            pool.memset(ones[:, :], 1.0).then_inc(s["consts_ready"], 1)
            pool.wait_ge(s["consts_ready"], 2)
            pool.tensor_copy(ones_r[:, :], ones[:, :]).then_inc(s["ones_r_ready"], 1)
            pool.affine_select(out=ident[:, :], in_=ones[:, :], compare_op=ALU.is_equal, fill=0.0, base=0,
                               pattern=[[-1, P]], channel_multiplier=1).then_inc(s["consts_ready"], 1)
            pool.affine_select(out=upper[:, :], in_=ones[:, :], compare_op=ALU.is_ge, fill=0.0, base=0,
                               pattern=[[1, P]], channel_multiplier=-1).then_inc(s["consts_ready"], 1)
            pool.affine_select(out=below[:, :], in_=ones[:, :], compare_op=ALU.is_gt, fill=0.0, base=0,
                               pattern=[[-1, P]], channel_multiplier=1).then_inc(s["below_ready"], 1)
            norm_scale(1)
            split_wk(0)
            split_wv(0)
            k_low(0)
            with pool.Fori(1, G) as g:
                split_wk(g)
                wqo_low(s["wq_hi_ready"], s["wq_lo_ready"], g)
                split_wv(g)
                k_low(g)
                wqo_low(s["wo_hi_ready"], s["wo_lo_ready"], g - 1)
            wqo_low(s["wo_hi_ready"], s["wo_lo_ready"], G - 1)

            pool.wait_ge(s["below_ready"], 1)
            norm_scale(2)
            pool.tensor_copy(below_r[:, :], below[:, :]).then_inc(s["below_r_ready"], 1)

            def steps_odd_chunk(n):
                for j in range(2):
                    if not (isinstance(n, int) and n == 0):
                        pool.wait_ge(s["odd_mm"], 2 * n + j - 1)
                    pool.tensor_tensor(
                        steps[:, 4 * j:4 * j + 4, :], upper[:, :].unsqueeze(1).broadcast_to([P, 4, P]),
                        a_dt[:, bass.ds((2 * n + 1) * HC + 4 * j, 4)].unsqueeze(2).broadcast_to([P, 4, P]),
                        ALU.mult).then_inc(s["steps_odd"], 1)

            pool.wait_ge(s["a_dt_ready"], 1)
            steps_odd_chunk(0)
            with pool.Fori(1, CH // 2) as n:
                steps_odd_chunk(n)

            def out_low(n, i):
                pool.wait_ge(s["wout_hi_ready"], 2 * n + i + 1)
                pool.tensor_tensor(w_out_lo[:, i, :, :], w_out_sb[:, i, :, :], w_out_hi[:, i, :, :].bitcast(F32),
                                   ALU.subtract).then_inc(s["wout_lo_ready"], 1)

            def decay_products(n, i):
                c = 2 * n + i
                if isinstance(n, int) and n == 0:
                    pool.wait_ge(s["gm_ready"], 2)
                    pool.wait_ge(s["decay_ready"], 2 * CH)
                else:
                    pool.wait_ge(s["y_mm"], c - 1)
                pool.tensor_tensor(m_t[:, i, :, :], decay[:, bass.ds(HC * c, HC), :], gm[:, :, :], ALU.mult)\
                    .then_inc(s["m_ready"], 1)

            def group_norm(n):
                pool.wait_ge(s["square_ready"], 2 * (n + 1))
                pool.tensor_tensor(ms[:, :], square_sum[:, 0:1], square_sum[:, 1:2], ALU.add).then_inc(s["ms_sum"], 1)
                pool.wait_ge(s["ms_sum"], n + 1)
                keep_wait_apart(pool)
                pool.tensor_scalar(ms_eps[:, :], ms[:, :], NG / INTER, EPS, ALU.mult, ALU.add)\
                    .then_inc(s["ms_eps_ready"], 1)
                pool.wait_ge(s["ms_eps_ready"], n + 1)
                at_least(pool, s["out_added"], n)
                pool.tensor_tensor(group_scale[:, :], ms_eps[:, :], half_neg[:, :], ALU.pow)\
                    .then_inc(s["scale_ready"], 1)

            pool.wait_ge(s["gate_hi_ready"], 1)
            pool.tensor_tensor(w_gate_lo[:, 0, PAIRS[0], :], w_gate_sb[:, 0, PAIRS[0], :],
                               w_gate_hi[:, PAIRS[0], :].bitcast(F32), ALU.subtract).then_inc(s["first_gate_lo"], 1)
            decay_products(0, 0)
            decay_products(0, 1)

            with pool.Fori(1, CH // 2) as n:
                decay_products(n, 0)
                out_low(n - 1, 0)
                decay_products(n, 1)
                group_norm(n - 1)
                out_low(n - 1, 1)
            out_low(CH // 2 - 1, 0)
            pool.wait_ge(s["wout_hi_ready"], CH)
            pool.tensor_tensor(w_out_lo[:, 1, PAIRS[0], :], w_out_sb[:, 1, PAIRS[0], :],
                               w_out_hi[:, 1, PAIRS[0], :].bitcast(F32), ALU.subtract).then_inc(s["last_wout_lo"], 1)
            group_norm(CH // 2 - 1)
            norm_scale(3)


_F = np.float32


def _rope_tables():
    freq = _F(1.0) / _F(10000.0) ** (np.arange(0, DH, 2, dtype=_F) / _F(DH))
    angle = np.arange(SK, dtype=_F)[:, None] * freq[None, :].astype(_F)
    cos, sin = np.cos(angle.astype(np.float64)), np.sin(angle.astype(np.float64))
    k_cos = np.concatenate([cos.T, cos.T]).astype(_F)
    k_sin = np.concatenate([sin.T, -sin.T]).astype(_F)
    q_scale = 1.0 / np.sqrt(float(DH))
    return k_cos, k_sin, (cos[:P] * q_scale).astype(_F), (sin[:P] * q_scale).astype(_F)


def kernel(**inputs):
    import concourse.bacc as bacc
    from concourse.bass_utils import run_bass_kernel_spmd

    a = {name: np.asarray(v) for name, v in inputs.items()}

    def by_input(w, columns):
        return w.reshape(KC, P, -1, columns).transpose(2, 1, 0, 3)

    w_in = a["L0_attn_in_proj_w"].T
    gate_end, hs_end, bc_end = INTER, 2 * INTER, 2 * INTER + 2 * G * NS
    k_cos, k_sin, q_cos, q_sin = _rope_tables()
    laid = {
        "x": a["x"][0],
        "mask": a["mask_BxSxS2_ff0"][0],
        "ctx_t": a["ctx_4096"][0].T.reshape(KC, P, SK).transpose(1, 0, 2),
        "rope_k_cos": k_cos, "rope_k_sin": k_sin, "rope_q_cos": q_cos, "rope_q_sin": q_sin,
        "wk": by_input(a["L0_xattn_wk"], DH),
        "wv": by_input(a["L0_xattn_wv"], DH),
        "wq": by_input(a["L0_xattn_wq"], HG * DH),
        "wo": a["L0_xattn_wo"].reshape(G, HG, DH, DM).transpose(0, 2, 1, 3),
        "w_dt": by_input(w_in[:, bc_end:], MH)[0],
        "w_bc": by_input(w_in[:, hs_end:bc_end], 512),
        "w_hs": by_input(w_in[:, gate_end:hs_end], 512),
        "w_gate": by_input(w_in[:, :gate_end], 512),
        "w_out": a["L0_attn_out_proj_w"].T.reshape(CH, 4, P, DM).transpose(0, 2, 1, 3),
        "conv_w": a["L0_attn_conv_w"].reshape(XT_TILES, P, TAPS).transpose(1, 0, 2),
        "conv_b": a["L0_attn_conv_b"].reshape(XT_TILES, P).T,
        "dt_bias": a["L0_attn_dt_bias"],
        "a_log": a["L0_attn_A_log"],
        "d_skip": a["L0_attn_D"],
        "norm_w": a["L0_attn_norm_weight"].reshape(INTER // P, P).T,
        "q_packed": a["L0_ffn_weight_quantized"].reshape(KC, P, DM // 2).transpose(1, 0, 2),
        "q_scale": a["L0_ffn_weight_scales"].reshape(KC, P, QG).transpose(1, 0, 2),
        "q_zero": a["L0_ffn_weight_zero_points"].reshape(KC, P, QG).transpose(1, 0, 2),
        "q_bias": a["L0_ffn_bias"],
    }
    nc = bacc.Bacc("TRN2", target_bir_lowering=False, num_devices=1)
    arrays, args = {}, []
    for name, v in laid.items():
        arrays[f"in_{name}"] = v = np.ascontiguousarray(v)
        args.append(nc.dram_tensor(f"in_{name}", v.shape, mybir.dt.from_np(v.dtype), kind="ExternalInput").ap())
    args.append(nc.dram_tensor("out_x", (P, DM), F32, kind="ExternalOutput").ap())
    build(nc, *args)
    r = run_bass_kernel_spmd(nc, [arrays], core_ids=[0])
    return r.results[0]["out_x"].reshape(1, P, DM)
```
